# Optimizing a Trainium2 kernel written in Bass

```python
import numpy as np
import jax
import jax.numpy as jnp

def _softmax(x, axis=-1):
    return jax.nn.softmax(x, axis=axis)

def _gelu(x):
    return jax.nn.gelu(x, approximate=True)

def _silu(x):
    return jax.nn.silu(x)

def _sigmoid(x):
    return jax.nn.sigmoid(x)

def _layernorm(x, axis=-1, eps=1e-05):
    m = jnp.mean(x, axis=axis, keepdims=True)
    v = jnp.var(x, axis=axis, keepdims=True)
    return (x - m) / jnp.sqrt(v + eps)

def _scatter_add(tgt, idx, src, axis=0):
    return tgt.at[idx].add(src)

def _segment_sum(src, seg, n):
    return jax.ops.segment_sum(src, seg, n)
kernel_name = 'mk_flamingo_gated_d2_seqx_r8_7cd373'

def setup_inputs(seed: int=0):
    np.random.seed(seed)
    _w = jnp.asarray

    def _rec_inputs():
        import jax
        import jax.numpy as jnp
        _rk = jax.random.key(seed)
        x = 7.22e-05 + 1 * jax.random.normal(jax.random.fold_in(_rk, 1), (4, 256, 256), jnp.float32)
        _lenS = 256 - jax.random.randint(jax.random.fold_in(_rk, 7), (4,), 0, max(1, 256 // 4) + 1, jnp.int32)
        _lenS2 = 256 - jax.random.randint(jax.random.fold_in(_rk, 8), (4,), 0, max(1, 256 // 4) + 1, jnp.int32)
        _ctx_512P = jax.random.normal(jax.random.fold_in(_rk, 11), (4, 16, 64), jnp.float32)
        _ctx_512c = jax.random.dirichlet(jax.random.fold_in(_rk, 511), 0.3 * jnp.ones((16,), jnp.float32), (4, 256))
        _ctx_512t = jnp.einsum('bsk,bkd->bsd', _ctx_512c, _ctx_512P)
        _ctx_512t = _ctx_512t * jax.lax.rsqrt(jnp.mean(jnp.square(_ctx_512t)) + 1e-12) * 0.953939
        ctx_512 = -0.000514642 + 1.00011 * (_ctx_512t + 0.3 * jax.random.normal(jax.random.fold_in(_rk, 611), (4, 256, 64), jnp.float32))
        _g = jax.random.normal(jax.random.fold_in(_rk, 9001), (2, 2), jnp.float32)
        _g = jnp.sign(_g) * jnp.maximum(jnp.abs(_g), 1.0) + (_g == 0) * 1.0
        g_xattn = _g[0]
        g_ffn = _g[1]
        return (x, ctx_512, g_xattn, g_ffn)
    x, ctx_512, g_xattn, g_ffn = _rec_inputs()

    def _L0_xattn_setup():
        import jax, jax.numpy as jnp
        import numpy as np
        N_HEADS = 16
        N_KV_HEADS = 4
        ROPE_THETA = 10000.0
        EPS = 1e-05

        def _rms_norm(x, w):
            var = jnp.mean(x * x, axis=-1, keepdims=True)
            return x * jax.lax.rsqrt(var + EPS) * w

        def _rope_sin_cos(T, head_dim, dtype):
            inv_freq = 1.0 / ROPE_THETA ** (jnp.arange(0, head_dim, 2, dtype=jnp.float32) / head_dim)
            t = jnp.arange(T, dtype=jnp.float32)
            freqs = jnp.outer(t, inv_freq)
            emb = jnp.concatenate([freqs, freqs], -1)
            return (jnp.sin(emb).astype(dtype)[None, None], jnp.cos(emb).astype(dtype)[None, None])

        def _rotate_half(x):
            h = x.shape[-1] // 2
            x1, x2 = (x[..., :h], x[..., h:])
            return jnp.concatenate([-x2, x1], axis=-1)
        key = jax.random.key(seed)
        ks = jax.random.split(key, 6)
        B, T, C = (2, 256, 256)
        Ckv = C // N_HEADS * N_KV_HEADS
        return {'q': jax.random.normal(ks[0], (B, T, C), jnp.float32), 'k': jax.random.normal(ks[1], (B, T, Ckv), jnp.float32), 'v': jax.random.normal(ks[2], (B, T, Ckv), jnp.float32), 'q_norm_w': jnp.ones((C,), jnp.float32), 'k_norm_w': jnp.ones((Ckv,), jnp.float32), 'w_out': jax.random.normal(ks[3], (C, C), jnp.float32) * C ** (-0.5)}
    _L0_xattn_all = _L0_xattn_setup()
    _L0_xattn_in = {k: v for k, v in _L0_xattn_all.items() if k in ('q_norm_w', 'k_norm_w', 'w_out')}
    del _L0_xattn_all

    def _L0_ffn_setup():
        import jax, jax.numpy as jnp
        import numpy as np
        EPS = 1e-05

        def _act_quant(x):
            scale = 127.0 / jnp.clip(jnp.max(jnp.abs(x), axis=-1, keepdims=True), EPS, None)
            return jnp.clip(jnp.round(x * scale), -128.0, 127.0) / scale

        def _weight_quant(w):
            scale = 1.0 / jnp.clip(jnp.mean(jnp.abs(w)), EPS, None)
            return jnp.clip(jnp.round(w * scale), -1.0, 1.0) / scale

        def _ste(x, q):
            return x + jax.lax.stop_gradient(q - x)

        def _bitlinear(x, w, b):
            xq = _ste(x, _act_quant(x))
            wq = _ste(w, _weight_quant(w))
            return jnp.einsum('bsd,hd->bsh', xq, wq) + b
        key = jax.random.key(seed)
        k1, k2, k3 = jax.random.split(key, 3)
        dim, hidden = (256, 1024)
        x = jax.random.normal(k1, (4, 256, dim), dtype=jnp.float32)
        w1 = jax.random.normal(k2, (hidden, dim), dtype=jnp.float32) * 0.02
        b1 = jnp.zeros((hidden,), dtype=jnp.float32)
        w2 = jax.random.normal(k3, (dim, hidden), dtype=jnp.float32) * 0.02
        b2 = jnp.zeros((dim,), dtype=jnp.float32)
        return {'x': x, 'w1': w1, 'b1': b1, 'w2': w2, 'b2': b2}
    _L0_ffn_all = _L0_ffn_setup()
    _L0_ffn_in = {k: v for k, v in _L0_ffn_all.items() if k in ('w1', 'b1', 'w2', 'b2')}
    del _L0_ffn_all

    def _L1_xattn_setup():
        import jax, jax.numpy as jnp
        import numpy as np
        B, S, L = (2, 128, 128)
        DIM_Q, H, K, D_C, D_CQ, R = (256, 16, 128, 64, 192, 64)

        def _rope_tables(length, dim):
            inv = 1.0 / 10000.0 ** (jnp.arange(0, dim, 2, dtype=jnp.float32) / dim)
            f = jnp.arange(length, dtype=jnp.float32)[:, None] * inv[None, :]
            sin = jnp.repeat(jnp.sin(f), 2, axis=-1)
            cos = jnp.repeat(jnp.cos(f), 2, axis=-1)
            return (sin, cos)

        def _rotate_half(x):
            half = x.shape[-1] // 2
            return jnp.concatenate([-x[..., half:], x[..., :half]], axis=-1)

        def _apply_rope(x, sin, cos):
            return x * cos + _rotate_half(x) * sin
        key = jax.random.key(seed)
        ks = jax.random.split(key, 8)
        return {'hidden_q': jax.random.normal(ks[0], (B, S, DIM_Q), jnp.float32), 'kv_c': jax.random.normal(ks[1], (B, L, D_C), jnp.float32), 'Wq': jax.random.normal(ks[2], (H * K, DIM_Q), jnp.float32) / np.sqrt(DIM_Q).astype(np.float32), 'w_kc_q': jax.random.normal(ks[3], (H, K, D_CQ), jnp.float32) / np.sqrt(K).astype(np.float32), 'w_kc_kv': jax.random.normal(ks[4], (H, K, D_C), jnp.float32) / np.sqrt(K).astype(np.float32), 'W_qr': jax.random.normal(ks[5], (H, D_CQ, R), jnp.float32) / np.float32(np.sqrt(D_CQ) * np.sqrt(R)), 'W_kr': jax.random.normal(ks[6], (H, D_C, R), jnp.float32) / np.sqrt(D_C).astype(np.float32), 'Wo': jax.random.normal(ks[7], (DIM_Q, H * K), jnp.float32) / np.sqrt(H * K).astype(np.float32)}
    _L1_xattn_all = _L1_xattn_setup()
    _L1_xattn_in = {k: v for k, v in _L1_xattn_all.items() if k in ('Wq', 'w_kc_q', 'w_kc_kv', 'W_qr', 'W_kr', 'Wo')}
    del _L1_xattn_all

    def _L1_ffn_setup():
        import jax, jax.numpy as jnp
        import numpy as np
        from jax import lax
        B, S, H = (1, 256, 256)
        E, I, TOP_K = (64, 64, 8)
        SHARED_I = 64
        key = jax.random.key(seed)
        ks = jax.random.split(key, 8)
        sc = 0.02
        return {'hidden_states': jax.random.normal(ks[0], (B, S, H), jnp.float32), 'router_w': jax.random.normal(ks[1], (E, H), jnp.float32) * sc, 'gate_up_proj': jax.random.normal(ks[2], (E, 2 * I, H), jnp.float32) * sc, 'down_proj': jax.random.normal(ks[3], (E, H, I), jnp.float32) * sc, 'shared_gate_w': jax.random.normal(ks[4], (SHARED_I, H), jnp.float32) * sc, 'shared_up_w': jax.random.normal(ks[5], (SHARED_I, H), jnp.float32) * sc, 'shared_down_w': jax.random.normal(ks[6], (H, SHARED_I), jnp.float32) * sc, 'shared_expert_gate_w': jax.random.normal(ks[7], (1, H), jnp.float32) * sc}
    _L1_ffn_all = _L1_ffn_setup()
    _L1_ffn_in = {k: v for k, v in _L1_ffn_all.items() if k in ('router_w', 'gate_up_proj', 'down_proj', 'shared_gate_w', 'shared_up_w', 'shared_down_w', 'shared_expert_gate_w')}
    del _L1_ffn_all
    return {'x': x, 'ctx_512': ctx_512, 'g_xattn': g_xattn, 'g_ffn': g_ffn, 'L0_xattn_q_norm_w': _L0_xattn_in['q_norm_w'], 'L0_xattn_k_norm_w': _L0_xattn_in['k_norm_w'], 'L0_xattn_w_out': _L0_xattn_in['w_out'], 'L0_ffn_w1': _L0_ffn_in['w1'], 'L0_ffn_b1': _L0_ffn_in['b1'], 'L0_ffn_w2': _L0_ffn_in['w2'], 'L0_ffn_b2': _L0_ffn_in['b2'], 'L1_xattn_Wq': _L1_xattn_in['Wq'], 'L1_xattn_w_kc_q': _L1_xattn_in['w_kc_q'], 'L1_xattn_w_kc_kv': _L1_xattn_in['w_kc_kv'], 'L1_xattn_W_qr': _L1_xattn_in['W_qr'], 'L1_xattn_W_kr': _L1_xattn_in['W_kr'], 'L1_xattn_Wo': _L1_xattn_in['Wo'], 'L1_ffn_router_w': _L1_ffn_in['router_w'], 'L1_ffn_gate_up_proj': _L1_ffn_in['gate_up_proj'], 'L1_ffn_down_proj': _L1_ffn_in['down_proj'], 'L1_ffn_shared_gate_w': _L1_ffn_in['shared_gate_w'], 'L1_ffn_shared_up_w': _L1_ffn_in['shared_up_w'], 'L1_ffn_shared_down_w': _L1_ffn_in['shared_down_w'], 'L1_ffn_shared_expert_gate_w': _L1_ffn_in['shared_expert_gate_w']}

def reference(x, ctx_512, g_xattn, g_ffn, L0_xattn_q_norm_w, L0_xattn_k_norm_w, L0_xattn_w_out, L0_ffn_w1, L0_ffn_b1, L0_ffn_w2, L0_ffn_b2, L1_xattn_Wq, L1_xattn_w_kc_q, L1_xattn_w_kc_kv, L1_xattn_W_qr, L1_xattn_W_kr, L1_xattn_Wo, L1_ffn_router_w, L1_ffn_gate_up_proj, L1_ffn_down_proj, L1_ffn_shared_gate_w, L1_ffn_shared_up_w, L1_ffn_shared_down_w, L1_ffn_shared_expert_gate_w):
    import jax
    import jax.numpy as jnp

    def _L0_xattn_ref(q, k, v, q_norm_w, k_norm_w, w_out):
        import jax, jax.numpy as jnp
        import numpy as np
        N_HEADS = 16
        N_KV_HEADS = 4
        ROPE_THETA = 10000.0
        EPS = 1e-05

        def _rms_norm(x, w):
            var = jnp.mean(x * x, axis=-1, keepdims=True)
            return x * jax.lax.rsqrt(var + EPS) * w

        def _rope_sin_cos(T, head_dim, dtype):
            inv_freq = 1.0 / ROPE_THETA ** (jnp.arange(0, head_dim, 2, dtype=jnp.float32) / head_dim)
            t = jnp.arange(T, dtype=jnp.float32)
            freqs = jnp.outer(t, inv_freq)
            emb = jnp.concatenate([freqs, freqs], -1)
            return (jnp.sin(emb).astype(dtype)[None, None], jnp.cos(emb).astype(dtype)[None, None])

        def _rotate_half(x):
            h = x.shape[-1] // 2
            x1, x2 = (x[..., :h], x[..., h:])
            return jnp.concatenate([-x2, x1], axis=-1)
        B, T, C = q.shape
        hd = C // N_HEADS
        g = N_HEADS // N_KV_HEADS
        q = _rms_norm(q, q_norm_w)
        k = _rms_norm(k, k_norm_w)
        q = q.reshape(B, T, N_HEADS, hd).transpose(0, 2, 1, 3)
        k = k.reshape(B, T, N_KV_HEADS, hd).transpose(0, 2, 1, 3)
        v = v.reshape(B, T, N_KV_HEADS, hd).transpose(0, 2, 1, 3)
        sin, cos = _rope_sin_cos(T, hd, q.dtype)
        q = q * cos + _rotate_half(q) * sin
        k = k * cos + _rotate_half(k) * sin
        qg = q.reshape(B, N_KV_HEADS, g, T, hd)
        scale = 1.0 / jnp.sqrt(jnp.asarray(hd, q.dtype))
        scores = jnp.einsum('bgnqd,bgkd->bgnqk', qg, k) * scale
        causal = jnp.tril(jnp.ones((T, T), bool))
        scores = jnp.where(causal, scores, jnp.asarray(-1e+30, scores.dtype))
        attn = jax.nn.softmax(scores, axis=-1)
        out = jnp.einsum('bgnqk,bgkd->bgnqd', attn, v)
        out = out.reshape(B, N_HEADS, T, hd).transpose(0, 2, 1, 3).reshape(B, T, C)
        return out @ w_out.T

    def _L0_ffn_ref(x, w1, b1, w2, b2):
        import jax, jax.numpy as jnp
        import numpy as np
        EPS = 1e-05

        def _act_quant(x):
            scale = 127.0 / jnp.clip(jnp.max(jnp.abs(x), axis=-1, keepdims=True), EPS, None)
            return jnp.clip(jnp.round(x * scale), -128.0, 127.0) / scale

        def _weight_quant(w):
            scale = 1.0 / jnp.clip(jnp.mean(jnp.abs(w)), EPS, None)
            return jnp.clip(jnp.round(w * scale), -1.0, 1.0) / scale

        def _ste(x, q):
            return x + jax.lax.stop_gradient(q - x)

        def _bitlinear(x, w, b):
            xq = _ste(x, _act_quant(x))
            wq = _ste(w, _weight_quant(w))
            return jnp.einsum('bsd,hd->bsh', xq, wq) + b
        h = jax.nn.gelu(_bitlinear(x, w1, b1), approximate=False)
        return _bitlinear(h, w2, b2)

    def _L1_xattn_ref(hidden_q, kv_c, Wq, w_kc_q, w_kc_kv, W_qr, W_kr, Wo):
        import jax, jax.numpy as jnp
        import numpy as np
        B, S, L = (2, 128, 128)
        DIM_Q, H, K, D_C, D_CQ, R = (256, 16, 128, 64, 192, 64)

        def _rope_tables(length, dim):
            inv = 1.0 / 10000.0 ** (jnp.arange(0, dim, 2, dtype=jnp.float32) / dim)
            f = jnp.arange(length, dtype=jnp.float32)[:, None] * inv[None, :]
            sin = jnp.repeat(jnp.sin(f), 2, axis=-1)
            cos = jnp.repeat(jnp.cos(f), 2, axis=-1)
            return (sin, cos)

        def _rotate_half(x):
            half = x.shape[-1] // 2
            return jnp.concatenate([-x[..., half:], x[..., :half]], axis=-1)

        def _apply_rope(x, sin, cos):
            return x * cos + _rotate_half(x) * sin
        Bv, Sv, _ = hidden_q.shape
        _, Lv, _ = kv_c.shape
        q_hk = (hidden_q @ Wq.T).reshape(Bv, Sv, H, K)
        q_big = jnp.einsum('bshk,hkq->bshq', q_hk, w_kc_q)
        sin_q, cos_q = _rope_tables(Sv, D_CQ)
        q_big = _apply_rope(q_big, sin_q[None, :, None, :], cos_q[None, :, None, :])
        sin_k, cos_k = _rope_tables(Lv, D_C)
        kv_r = _apply_rope(kv_c, sin_k[None], cos_k[None])
        q_r = jnp.einsum('bshq,hqr->bhsr', q_big, W_qr)
        k_r = jnp.einsum('bld,hdr->bhlr', kv_r, W_kr)
        scores = jnp.einsum('bhsr,bhlr->bhsl', q_r, k_r)
        attn = jax.nn.softmax(scores, axis=-1)
        ctx_c = jnp.einsum('bhsl,bld->bhsd', attn, kv_r)
        ctx_lat = jnp.einsum('bhsd,hkd->bhsk', ctx_c, w_kc_kv)
        ctx = ctx_lat.transpose(0, 2, 1, 3).reshape(Bv, Sv, H * K)
        return ctx @ Wo.T

    def _L1_ffn_ref(hidden_states, router_w, gate_up_proj, down_proj, shared_gate_w, shared_up_w, shared_down_w, shared_expert_gate_w):
        import jax, jax.numpy as jnp
        import numpy as np
        from jax import lax
        B, S, H = (1, 256, 256)
        E, I, TOP_K = (64, 64, 8)
        SHARED_I = 64
        b, s, h_dim = hidden_states.shape
        h = hidden_states.reshape(-1, h_dim)
        T = h.shape[0]
        shared = jnp.dot(jax.nn.silu(jnp.dot(h, shared_gate_w.T)) * jnp.dot(h, shared_up_w.T), shared_down_w.T)
        shared = jax.nn.sigmoid(jnp.dot(h, shared_expert_gate_w.T)) * shared
        logits = jnp.dot(h, router_w.T)
        probs = jax.nn.softmax(logits.astype(jnp.float32), axis=-1)
        top_vals, top_idx = lax.top_k(probs, TOP_K)
        top_vals = top_vals / jnp.sum(top_vals, axis=-1, keepdims=True)
        top_vals = top_vals.astype(h.dtype)
        comb = jnp.zeros((T, E), h.dtype).at[jnp.arange(T)[:, None], top_idx].add(top_vals)

        def body(acc, xs):
            wgu, wd, w_e = xs
            g, u = jnp.split(jnp.dot(h, wgu.T), 2, axis=-1)
            eo = jnp.dot(jax.nn.silu(g) * u, wd.T)
            return (acc + eo * w_e[:, None], None)
        expert_out, _ = lax.scan(body, jnp.zeros_like(h), (gate_up_proj, down_proj, comb.T))
        return (expert_out + shared).reshape(b, s, h_dim)
    x = x + jnp.tanh(g_xattn[0]) * _L0_xattn_ref(_layernorm(x, axis=-1), ctx_512, ctx_512, L0_xattn_q_norm_w, L0_xattn_k_norm_w, L0_xattn_w_out)
    x = x + jnp.tanh(g_ffn[0]) * _L0_ffn_ref(_layernorm(x, axis=-1), L0_ffn_w1, L0_ffn_b1, L0_ffn_w2, L0_ffn_b2)
    x = x + jnp.tanh(g_xattn[1]) * _L1_xattn_ref(_layernorm(x, axis=-1), ctx_512, L1_xattn_Wq, L1_xattn_w_kc_q, L1_xattn_w_kc_kv, L1_xattn_W_qr, L1_xattn_W_kr, L1_xattn_Wo)
    x = x + jnp.tanh(g_ffn[1]) * _L1_ffn_ref(_layernorm(x, axis=-1), L1_ffn_router_w, L1_ffn_gate_up_proj, L1_ffn_down_proj, L1_ffn_shared_gate_w, L1_ffn_shared_up_w, L1_ffn_shared_down_w, L1_ffn_shared_expert_gate_w)
    return x

_drawn_inputs = setup_inputs


def setup_inputs(seed=0):
    import zlib

    import numpy as np

    out = dict(_drawn_inputs(seed))
    spreads = {'g_ffn': (-1.0, 0.6),
     'L0_xattn_q_norm_w': (1.0, 0.2),
     'L0_xattn_k_norm_w': (1.0, 0.537),
     'L0_ffn_b1': (0.0, 0.506),
     'L0_ffn_b2': (0.0, 0.1)}
    factors = {'L1_ffn_router_w': 8.0,
     'L1_ffn_gate_up_proj': 8.0,
     'L1_ffn_down_proj': 8.0,
     'L1_ffn_shared_gate_w': 8.0,
     'L1_ffn_shared_up_w': 8.0,
     'L1_ffn_shared_down_w': 8.0,
     'L1_ffn_shared_expert_gate_w': 8.0}
    for name, (base, spread) in spreads.items():
        noise = np.random.default_rng([zlib.crc32(name.encode()), seed]).standard_normal(out[name].shape)
        drawn = base * np.exp(spread * noise) if base else spread * noise
        out[name] = jnp.asarray(drawn.astype(out[name].dtype))
    for name, factor in factors.items():
        out[name] = (out[name] * factor).astype(out[name].dtype)
    return out
```

```python
from contextlib import ExitStack

import numpy as np

import concourse.bass as bass
from concourse import mybir

ALU = mybir.AluOpType
ACT = mybir.ActivationFunctionType
AX = mybir.AxisListType
F32 = mybir.dt.float32
F32R = mybir.dt.float32r
BF16 = mybir.dt.bfloat16

P = 128
SEQS, T, D = 4, 256, 256
TILES = SEQS * T // P
TOK = SEQS * T
DC = 64
KD = D // P
EPS = 1e-5
NEG = -1e30
ROUND = 12582912.0
TINY = 1e-5

QH, HD = 16, 16
GROUPS = 4
CHUNKS = QH * HD // P
HPC = QH // CHUNKS
PAIRS = QH // 2
DIAG = P + HD
HID = 1024
HK = HID // P
LH, LK, LQ, LR = 16, 128, 192, 64
HP = LH // 2
FCH = 2 * LQ // P
E, EI, TOPK = 64, 64, 8
EP = E // 2
EW = KD * 2 * P + D
TB = 2
BLK = TOK // TB

PARAMS = (("g", 4), ("qw", D), ("kw", DC), ("b1", HID), ("b2", D))
CONSTS = (("ident", P), ("causal", P), ("headmask", HPC), ("expertsel", E),
          ("cos0", 2 * HD), ("sin0", 2 * HD), ("cosk", 2 * DC), ("sink", 2 * DC),
          ("cosq", FCH * T), ("sinq", FCH * T))


def offsets(table):
    at, out = 0, {}
    for name, w in table:
        out[name] = (at, w)
        at += w
    return out, at


def shape_constants():
    f32 = np.float32
    tabs, width = offsets(CONSTS)
    c = np.zeros((P, width), f32)

    def put(name, a):
        at, w = tabs[name]
        c[:, at:at + w] = np.asarray(a, f32).reshape(P, w)

    p = np.arange(P)
    put("ident", np.eye(P))
    put("causal", np.where(p[None, :] <= p[:, None], 0.0, NEG))
    put("headmask", (p[:, None] // HD == np.arange(HPC)[None, :]))
    put("expertsel", (p[:, None] % E == np.arange(E)[None, :]))
    t = np.arange(T, dtype=f32)

    def angles(dim):
        inv = (f32(1.0) / f32(10000.0) ** (np.arange(0, dim, 2, dtype=f32) / f32(dim))).astype(f32)
        return (t[:, None] * inv[None, :]).astype(f32)

    def by_tile(a):
        return a.reshape(2, P, -1).transpose(1, 0, 2)

    def signed(s):
        h = s.shape[-1] // 2
        return np.concatenate([-s[:, :h], s[:, h:]], -1)

    a0 = np.concatenate([angles(HD)] * 2, -1)
    put("cos0", by_tile(np.cos(a0)))
    put("sin0", by_tile(signed(np.sin(a0))))
    ak = np.repeat(angles(DC), 2, -1)
    put("cosk", by_tile(np.cos(ak)))
    put("sink", by_tile(signed(np.sin(ak))))
    aq = np.repeat(angles(LQ), 2, -1)
    cos, sin = np.cos(aq), np.sin(aq)
    cross = np.concatenate([sin[:, LQ // 2:], -sin[:, :LQ // 2]], -1)
    for name, a in (("cosq", cos), ("sinq", cross)):
        two = np.concatenate([a, a], -1).T
        put(name, two.reshape(FCH, P, T).transpose(1, 0, 2))
    return c


class OwnSteps:

    def __init__(self, eng, sem, per_round):
        self.eng, self.sem, self.per_round = eng, sem, per_round
        self.base, self.n = 0, 0

    def round(self, r):
        assert self.n in (0, self.per_round), self.n
        self.base, self.n = r * self.per_round, 0

    def __call__(self, ins):
        self.n += 1
        ins.then_inc(self.sem, 1)
        self.eng.wait_ge(self.sem, self.base + self.n)

    def done(self):
        assert self.n == self.per_round, (self.n, self.per_round)


def flamingo_program(nc, x, ctx, consts, params, woutT, w1T, w2T, wq, wkcq, wqr, wkr, wkckv, woT,
                     routerT, wsg, experts, out):
    tabs, CW = offsets(CONSTS)
    pars, PW = offsets(PARAMS)
    with ExitStack() as stack:
        room = [stack]

        def sb(name, shape, dt=F32):
            return room[0].enter_context(nc.sbuf_tensor(name, shape, dt))

        def sem(name):
            return stack.enter_context(nc.semaphore(name))

        pair_bank = [stack.enter_context(nc.psum_tensor(f"pair_bank{i}", [P, 2, 512], F32)) for i in range(4)]
        bank = [pair_bank[i // 2][:, i % 2, :] for i in range(8)]

        x_sb = sb("x_sb", [P, TILES, D])
        ctx_sb = sb("ctx_sb", [P, TILES, DC])
        c_sb = sb("c_sb", [P, CW])
        par = sb("par", [P, PW])
        eps_col = sb("eps_col", [P, 1])
        tg = sb("tg", [P, 4])
        stats = sb("stats", [P, TILES, 6])
        mv = sb("mv", [P, TILES, 2])
        var_eps = sb("var_eps", [P, TILES])
        rstd = sb("rstd", [P, TILES])
        xn = sb("xn", [P, TILES, D])
        ident_bf = sb("ident_bf", [P, P], BF16)
        mask = sb("mask", [P, 3 * P], BF16)

        def const(name):
            at, w = tabs[name]
            return c_sb[:, at:at + w]

        def param(name):
            at, w = pars[name]
            return par[:, at:at + w]

        ident = const("ident")

        kvr = sb("kvr", [P, TILES, 3 * DC])
        kvtmp = sb("kvtmp", [P, TILES, DC])
        kvT = sb("kvT", [P, TOK])
        wq_sb = sb("wq_sb", [P, 2, D])
        wkcq_sb = sb("wkcq_sb", [P, 2, LQ])
        wqr_sb = sb("wqr_sb", [P, 2, FCH, P])
        wkr_sb = sb("wkr_sb", [P, 2, LR])
        wkckv_sb = sb("wkckv_sb", [P, 2, DC])
        woT_sb = sb("woT_sb", [P, 2, D])
        krT = [sb(f"krT{j}", [P, TOK]) for j in range(2)]
        w_mean = sb("w_mean", [P, 2])

        room[0] = ExitStack()
        kq = sb("kq", [P, TILES, DC])
        kn = sb("kn", [P, TILES, DC])
        kr = sb("kr", [P, TILES, DC])
        ktmp = sb("ktmp", [P, TILES, DC])
        rk = sb("rk", [P, 2 * TILES])
        rkr = sb("rkr", [P, 2 * TILES])
        ck0 = sb("ck0", [P, 2, GROUPS, HD])
        sk0 = sb("sk0", [P, 2, GROUPS, HD])
        cq0 = sb("cq0", [P, 2, QH, HD])
        sq0 = sb("sq0", [P, 2, QH, HD])
        qrot = sb("qrot", [P, 2, QH, HD])
        qtmp = sb("qtmp", [P, 2, QH, HD])
        krep = sb("krep", [P, 2, GROUPS, QH // GROUPS, HD])
        qT = [sb(f"qT{c}", [P, T]) for c in range(CHUNKS)]
        kT = [sb(f"kT{c}", [P, T]) for c in range(CHUNKS)]
        kpad = [sb(f"kpad{c}", [P, HPC, T]) for c in range(CHUNKS)]
        vpad = [[sb(f"vpad{c}{kt}", [P, HPC * DIAG]) for kt in range(2)] for c in range(CHUNKS)]
        probs = [sb(f"probs{s}", [P, 2, 3 * P]) for s in range(2)]
        probsT = [[sb(f"probsT{s}{j}", [P, 3 * P]) for j in range(2)] for s in range(2)]
        negmax = [sb(f"negmax{s}", [P, 4]) for s in range(2)]
        psums = [sb(f"psums{s}", [P, 4]) for s in range(2)]
        pinv = [sb(f"pinv{s}", [P, 4]) for s in range(2)]
        oT = [sb(f"oT{c}", [P, T]) for c in range(CHUNKS)]
        wout_sb = sb("wout_sb", [P, KD, D])

        w1_raw = sb("w1_raw", [P, KD * HID])
        w2_raw = sb("w2_raw", [P, HK * D])
        w1q = sb("w1q", [P, KD, HID], BF16)
        w2q = sb("w2q", [P, HK, D], BF16)
        w_abs = sb("w_abs", [P, 2])
        ones = sb("ones", [P, P])
        round_col = sb("round_col", [P, 1])
        w_scale = sb("w_scale", [P, 2])
        amax = sb("amax", [P, TILES])
        ascale = sb("ascale", [P, TILES])
        adeq = sb("adeq", [P, TILES])
        aq = sb("aq", [P, TILES, D], BF16)
        aT = sb("aT", [P, KD, TOK], BF16)
        pre = [sb(f"pre{k}", [P, HID]) for k in range(2)]
        hid_all = sb("hid_all", [P, 2 * HID])
        hid = [hid_all[:, k * HID:(k + 1) * HID] for k in range(2)]
        hrnd = [sb(f"hrnd{k}", [P, HID]) for k in range(2)]
        hq = [sb(f"hq{k}", [P, HID], BF16) for k in range(2)]
        hqT = [sb(f"hqT{k}", [P, HK, P], BF16) for k in range(2)]
        hmax = [sb(f"hmax{k}", [P, 1]) for k in range(2)]
        hinv = [sb(f"hinv{k}", [P, 1]) for k in range(2)]
        hscale = [sb(f"hscale{k}", [P, 1]) for k in range(2)]
        hdeq = [sb(f"hdeq{k}", [P, 1]) for k in range(2)]
        yb = [sb(f"yb{k}", [P, D]) for k in range(2)]

        room[0].close()
        room[0] = stack
        hT = sb("hT", [P, KD, TOK])
        router_sb = sb("router_sb", [P, KD, E])
        wsg_sb = sb("wsg_sb", [P, KD, P])
        zeros_bf = sb("zeros_bf", [P, BLK], BF16)
        e_raw = [sb(f"e_raw{k}", [P, EW]) for k in range(2)]
        room[0] = ExitStack()
        gq = sb("gq", [P, KD, 2 * LQ])
        turned = [sb(f"turned{k}", [P, 2, BLK]) for k in range(2)]
        qrT = sb("qrT", [P, TOK])
        lprobs = [sb(f"lprobs{k}", [P, 2, T]) for k in range(3)]
        lprobsT = [sb(f"lprobsT{k}", [P, 2, T]) for k in range(2)]
        lneg = [sb(f"lneg{k}", [P, 2]) for k in range(3)]
        lsum = [sb(f"lsum{k}", [P, 2]) for k in range(3)]
        linv = [sb(f"linv{k}", [P, 2]) for k in range(3)]
        ctxT = sb("ctxT", [P, HP * TOK])
        mout = sb("mout", [P, HP * D])

        room[0].close()
        room[0] = stack
        hT_hi = sb("hT_hi", [P, KD, TOK], F32R)
        hT_lo = sb("hT_lo", [P, KD, TOK], F32R)
        logits = sb("logits", [P, TILES, E])
        rmax = sb("rmax", [P, TILES])
        rexp = sb("rexp", [P, TILES, E])
        top8 = sb("top8", [P, TILES, TOPK])
        chosen = sb("chosen", [P, TILES, E])
        tsum = sb("tsum", [P, TILES])
        tinv = sb("tinv", [P, TILES])
        comb = sb("comb", [P, TILES, E])
        comb2 = sb("comb2", [P, TILES, 2 * E])
        combT = sb("combT", [P, TOK], F32R)
        sel = [sb(f"sel{k}", [P, P], F32R) for k in range(2)]
        e_hi = [sb(f"e_hi{k}", [P, EW], F32R) for k in range(2)]
        e_lo = [sb(f"e_lo{k}", [P, EW], F32R) for k in range(2)]
        silu = [sb(f"silu{k}", [P, BLK]) for k in range(2)]
        sgate = [sb(f"sgate{k}", [P, BLK]) for k in range(2)]
        act_u = sb("act_u", [P, BLK])
        act_w = [sb(f"act_w{k}", [P, BLK]) for k in range(2)]
        act_hi = [sb(f"act_hi{k}", [P, BLK], F32R) for k in range(2)]
        act_lo = [sb(f"act_lo{k}", [P, BLK], F32R) for k in range(2)]

        router_in = sem("router_in")
        e_in = [sem(f"e_in{k}") for k in range(2)]
        d_var, d_root, dve_d, xd_ready = sem("d_var"), sem("d_root"), sem("dve_d"), sem("xd_ready")
        hTd_ready, hTd_sb, hT_split = sem("hTd_ready"), sem("hTd_sb"), sem("hT_split")
        logits_ready, logits_sb, rexp_done, comb_ready = sem("logits_ready"), sem("logits_sb"), sem("rexp_done"), sem("comb_ready")
        combT_ready, combT_sb, dve_r, zeros_ready = sem("combT_ready"), sem("combT_sb"), sem("dve_r"), sem("zeros_ready")
        e_hi_ready, e_lo_ready, sel_ready = sem("e_hi_ready"), sem("e_lo_ready"), sem("sel_ready")
        gate_ready, up_ready, weight_ready = sem("gate_ready"), sem("up_ready"), sem("weight_ready")
        silu_done, sgate_done, up_used, act_ready = sem("silu_done"), sem("sgate_done"), sem("up_used"), sem("act_ready")
        act_hi_ready, act_lo_ready, down_done = sem("act_hi_ready"), sem("act_lo_ready"), sem("down_done")
        acc_sb, y_turned, x4_done = sem("acc_sb"), sem("y_turned"), sem("x4_done")
        wq_in, wkcq_in, wqr_in = sem("wq_in"), sem("wkcq_in"), sem("wqr_in")
        wkr_in, wkckv_in, woT_in = sem("wkr_in"), sem("wkckv_in"), sem("woT_in")
        kv_own, kvr_ready, kvT_ready, kvT_sb = sem("kv_own"), sem("kvr_ready"), sem("kvT_ready"), sem("kvT_sb")
        c_var, c_root, dve_c, xn_ready = sem("c_var"), sem("c_root"), sem("dve_c"), sem("xn_ready")
        hT_ready, hT_sb = sem("hT_ready"), sem("hT_sb")
        gq_ready, gq_sb = sem("gq_ready"), sem("gq_sb")
        mout_ready, mout_sb = sem("mout_ready"), sem("mout_sb")
        kr_done, krT_sb = sem("kr_done"), sem("krT_sb")
        lq_ready, lq_turned = sem("lq_ready"), sem("lq_turned")
        qr_step, qrT_sb = sem("qr_step"), sem("qrT_sb")
        ls_ready, lneg_ready, lexp_done, lprobs_ready = sem("ls_ready"), sem("lneg_ready"), sem("lexp_done"), sem("lprobs_ready")
        lpT_ready, lpT_sb, lpv_done, ctxT_sb = sem("lpT_ready"), sem("lpT_sb"), sem("lpv_done"), sem("ctxT_sb")
        dve_l, lpv_half = sem("dve_l"), sem("lpv_half")
        x3_ready, x3_done = sem("x3_ready"), sem("x3_done")
        b_stats, c_stats = sem("b_stats"), sem("c_stats")
        w1_in, w2_in = sem("w1_in"), sem("w2_in")
        w_abs_ready = sem("w_abs_ready")
        w_sum_ready = sem("w_sum_ready")
        w_scale_ready = sem("w_scale_ready")
        pool_w = sem("pool_w")
        wq_ready = sem("wq_ready")
        b_var, b_root = sem("b_var"), sem("b_root")
        dve_b = sem("dve_b")
        aq_ready = sem("aq_ready")
        aT_ready = sem("aT_ready")
        aT_sb = sem("aT_sb")
        h1_ready, pre_ready, gelu_done, hscale_ready = sem("h1_ready"), sem("pre_ready"), sem("gelu_done"), sem("hscale_ready")
        hrnd_ready, hq_ready, hqT_ready, hqT_sb = sem("hrnd_ready"), sem("hq_ready"), sem("hqT_ready"), sem("hqT_sb")
        y_ready, x2_done = sem("y_ready"), sem("x2_done")
        dve_h, yb_ready = sem("dve_h"), sem("yb_ready")
        x_in, c_in, par_in, ctx_in = sem("x_in"), sem("c_in"), sem("par_in"), sem("ctx_in")
        wout_in = sem("wout_in")
        stored = sem("stored")
        consts_made = sem("consts_made")
        dve_setup = sem("dve_setup")
        pool_setup = sem("pool_setup")
        gains = sem("gains")
        a_var = sem("a_var")
        a_root = sem("a_root")
        kr_ready = sem("kr_ready")
        qrot_ready = sem("qrot_ready")
        krep_ready = sem("krep_ready")
        qkT_ready = sem("qkT_ready")
        qkT_sb = sem("qkT_sb")
        kpad_ready = sem("kpad_ready")
        vpad_ready = sem("vpad_ready")
        scores_ready = sem("scores_ready")
        negmax_ready = sem("negmax_ready")
        exp_done = sem("exp_done")
        probs_ready = sem("probs_ready")
        pT_ready = sem("pT_ready")
        pT_sb_dve = sem("pT_sb_dve")
        pT_sb_act = sem("pT_sb_act")
        pv_done = sem("pv_done")
        oT_ready = sem("oT_ready")
        wout_done = sem("wout_done")
        x1_done = sem("x1_done")
        dve_a = sem("dve_a")
        dve_q = sem("dve_q")
        dve_soft = sem("dve_soft")

        block = stack.enter_context(nc.Block())

        @block.sync
        def _(sp):
            sp.dma_start(x_sb[:], x.rearrange("(i p) d -> p i d", p=P)).then_inc(x_in, 16)
            sp.dma_start(ctx_sb[:], ctx.rearrange("(i p) d -> p i d", p=P)).then_inc(ctx_in, 16)
            sp.dma_start(par[:], params).then_inc(par_in, 16)
            sp.dma_start(c_sb[:], consts).then_inc(c_in, 16)
            sp.dma_start(w1_raw[:], w1T.rearrange("p k n -> p (k n)")).then_inc(w1_in, 16)
            sp.dma_start(w2_raw[:], w2T.rearrange("p k n -> p (k n)")).then_inc(w2_in, 16)
            sp.dma_start(wout_sb[:], woutT).then_inc(wout_in, 16)
            def latent_weights(hp, first):
                def load(dst, src, arrived, used, count):
                    if not first:
                        sp.wait_ge(used, hp * count)
                    a = src[bass.ds(hp, 1)].rearrange("o p a b -> p (o a) b")
                    sp.dma_start(dst[:], a).then_inc(arrived, 16)

                load(wq_sb, wq, wq_in, gq_ready, 1)
                load(wkcq_sb, wkcq, wkcq_in, gq_ready, 1)
                load(wkckv_sb, wkckv, wkckv_in, mout_ready, 1)
                load(woT_sb, woT, woT_in, mout_ready, 1)
                if not first:
                    sp.wait_ge(kr_done, TB * hp)
                sp.dma_start(wkr_sb[0:DC], wkr[bass.ds(hp, 1)].rearrange("o p a b -> p (o a) b")).then_inc(wkr_in, 16)
                if not first:
                    sp.wait_ge(qr_step, 6 * hp)
                sp.dma_start(wqr_sb[:].rearrange("p n c r -> p (n c r)"),
                             wqr[bass.ds(hp, 1)].rearrange("o p n c r -> p (o n c r)")).then_inc(wqr_in, 16)

            latent_weights(0, True)
            with sp.Fori(1, HP) as hp:
                latent_weights(hp, False)
            sp.wait_ge(x2_done, TILES)
            sp.dma_start(router_sb[:], routerT).then_inc(router_in, 16)
            sp.dma_start(wsg_sb[:], wsg).then_inc(router_in, 16)
            for n in range(2):
                sp.dma_start(e_raw[n][:], experts[n]).then_inc(e_in[n], 16)
            with sp.Fori(0, EP // 2 - 1) as i:
                for k in range(2):
                    n = 2 * i + 2 + k
                    sp.wait_ge(e_lo_ready, n - 1)
                    sp.dma_start(e_raw[k][:], experts[bass.ds(n, 1)].rearrange("o p w -> p (o w)")).then_inc(e_in[k], 16)
            sp.wait_ge(e_lo_ready, EP - 1)
            sp.dma_start(e_raw[0][:], experts[EP]).then_inc(e_in[0], 16)
            for b in range(SEQS):
                sp.wait_ge(x4_done, b + 1)
                rows = out[b * T:(b + 1) * T, :].rearrange("(i p) d -> p i d", p=P)
                sp.dma_start(rows, x_sb[:, 2 * b:2 * b + 2, :]).then_inc(stored, 16)
            sp.wait_ge(stored, 16 * SEQS)
        def attention_a_pool(g):
            vflat = [[vpad[c][kt][:].rearrange("p (h e) -> p h e", e=DIAG) for kt in range(2)]
                     for c in range(CHUNKS)]
            for c in range(CHUNKS):
                for kt in range(2):
                    nc.gpsimd.memset(vpad[c][kt][:], 0.0).then_inc(pool_setup, 1)
            nc.gpsimd.memset(round_col[:], ROUND).then_inc(pool_setup, 1)
            g.wait_ge(pool_setup, 2 * CHUNKS + 1)
            g.wait_ge(c_in, 16)

            def repeat_keys(b):
                g.wait_ge(kr_ready, 1)
                if isinstance(b, int) and b == 0:
                    pass
                else:
                    g.wait_ge(qkT_ready, CHUNKS * b)
                for i in range(2):
                    src = kr[:, bass.ds(2 * b + i, 1), :].rearrange("p o (g d) -> p (o g) d", d=HD)
                    last = nc.gpsimd.tensor_copy(
                        krep[:, i], src.unsqueeze(2).broadcast_to([P, GROUPS, QH // GROUPS, HD]))
                last.then_inc(krep_ready, 1)

            def pads(b, c, first):
                g.wait_ge(qkT_sb, CHUNKS * b + c + 1)
                if not first:
                    g.wait_ge(scores_ready, PAIRS * (b - 1) + 4 * (c + 1))
                nc.gpsimd.tensor_tensor(
                    kpad[c][:], kT[c][:].unsqueeze(1).broadcast_to([P, HPC, T]),
                    const("headmask").unsqueeze(2).broadcast_to([P, HPC, T]), ALU.mult).then_inc(kpad_ready, 1)
                if first:
                    g.wait_ge(ctx_in, 16)
                else:
                    g.wait_ge(pv_done, PAIRS * (b - 1) + 4 * (c + 1))
                for kt in range(2):
                    src = ctx_sb[:, bass.ds(2 * b + kt, 1), 2 * c * HD:2 * (c + 1) * HD]
                    src = src.rearrange("p o (g d) -> p (o g) d", d=HD).unsqueeze(2).broadcast_to([P, 2, 4, HD])
                    dst = vflat[c][kt].rearrange("p (g n) e -> p g n e", g=2)[:, :, :, 0:HD]
                    last = nc.gpsimd.tensor_copy(dst, src)
                last.then_inc(vpad_ready, 1)

            def ternary_weights():
                g.wait_ge(w_scale_ready, 1)
                own = OwnSteps(g, pool_w, 4)
                for n, (w, q) in enumerate(((w1_raw, w1q), (w2_raw, w2q))):
                    own(nc.gpsimd.tensor_scalar(w[:], w[:], w_scale[:, n:n + 1], ROUND, ALU.mult, ALU.add))
                    own(nc.gpsimd.tensor_scalar(w[:], w[:], ROUND + 1, ROUND - 1, ALU.min, ALU.max))
                    nc.gpsimd.tensor_scalar(q[:].rearrange("p k n -> p (k n)"), w[:], -ROUND, 1.0,
                                            ALU.add, ALU.mult).then_inc(wq_ready, 1)

            repeat_keys(0)
            for c in range(CHUNKS):
                pads(0, c, True)
            ternary_weights()
            latent_kv_pool(g)
            with g.Fori(0, SEQS - 1) as b:
                repeat_keys(b + 1)
                for c in range(CHUNKS):
                    pads(b + 1, c, False)

        def latent_kv_pool(g):
            own = OwnSteps(g, kv_own, 4)
            own(nc.gpsimd.memset(kvr[:], 0.0))
            nc.gpsimd.memset(wkr_sb[DC:P], 0.0).then_inc(kvr_ready, 1)
            g.wait_ge(kvr_ready, 1)
            nc.gpsimd.memset(kvT[DC:P], 0.0).then_inc(kvr_ready, 1)
            g.wait_ge(kvr_ready, 2)
            nc.gpsimd.memset(krT[0][LR:P], 0.0).then_inc(kvr_ready, 1)
            g.wait_ge(kvr_ready, 3)
            nc.gpsimd.memset(krT[1][0:LR], 0.0).then_inc(kvr_ready, 1)
            g.wait_ge(kvr_ready, 4)
            half = DC // 2
            cos = const("cosk").rearrange("p (i d) -> p i d", d=DC).unsqueeze(1).broadcast_to([P, SEQS, 2, DC])
            sin = const("sink").rearrange("p (i d) -> p i d", d=DC)
            c4 = ctx_sb[:].rearrange("p (b i) d -> p b i d", i=2)
            t4 = kvtmp[:].rearrange("p (b i) d -> p b i d", i=2)
            for lo, other in ((0, half), (half, 0)):
                own(nc.gpsimd.tensor_tensor(t4[:, :, :, lo:lo + half], c4[:, :, :, other:other + half],
                                            sin[:, :, lo:lo + half].unsqueeze(1).broadcast_to([P, SEQS, 2, half]), ALU.mult))
            mid = kvr[:].rearrange("p (b i) e -> p b i e", i=2)[:, :, :, DC:2 * DC]
            own(nc.gpsimd.tensor_tensor(mid, c4, cos, ALU.mult))
            nc.gpsimd.tensor_tensor(mid, mid, t4, ALU.add).then_inc(kvr_ready, 1)

        def experts_pool(g):
            def low_weights(n, k):
                g.wait_ge(e_hi_ready, n + 1)
                nc.gpsimd.tensor_tensor(e_lo[k][:], e_raw[k][:], e_hi[k][:].bitcast(F32), ALU.subtract).then_inc(e_lo_ready, 1)

            def low_act(t, k):
                if not (isinstance(t, int) and t < 2):
                    g.wait_ge(down_done, t - 1)
                g.wait_ge(act_hi_ready, t + 1)
                nc.gpsimd.tensor_tensor(act_lo[k][:], act_w[k][:], act_hi[k][:].bitcast(F32), ALU.subtract).then_inc(act_lo_ready, 1)

            g.wait_ge(x2_done, TILES)
            nc.gpsimd.memset(zeros_bf[:], 0.0).then_inc(zeros_ready, 1)
            low_weights(0, 0)
            low_act(0, 0)
            low_weights(1, 1)
            low_act(1, 1)
            with g.Fori(0, EP // 2 - 1) as i:
                for k in range(2):
                    n = 2 * i + 1 + k
                    low_act(2 * n, 0)
                    low_weights(n + 1, k)
                    low_act(2 * n + 1, 1)
            low_act(2 * EP - 2, 0)
            low_weights(EP, 0)
            low_act(2 * EP - 1, 1)
            low_act(2 * EP, 0)
            low_act(2 * EP + 1, 1)

        def mlp_pool(g):
            def quantise(t, k):
                g.wait_ge(hrnd_ready, t + 1)
                if not (isinstance(t, int) and t < 2):
                    g.wait_ge(hqT_ready, t - 1)
                nc.gpsimd.tensor_tensor(hq[k][:], hrnd[k][:], round_col[:].broadcast_to([P, HID]),
                                        ALU.subtract).then_inc(hq_ready, 1)

            quantise(0, 0)
            quantise(1, 1)
            with g.Fori(1, SEQS) as b:
                for k in range(2):
                    quantise(2 * b + k, k)

        @block.gpsimd
        def _(g):
            attention_a_pool(g)
            mlp_pool(g)
            experts_pool(g)

        def attention_a_act(act):
            def evacuate_qk(b, c, first):
                act.wait_ge(qkT_ready, CHUNKS * b + c + 1)
                if not first:
                    act.wait_ge(scores_ready, PAIRS * (b - 1) + 4 * (c + 1))
                    act.wait_ge(kpad_ready, CHUNKS * (b - 1) + c + 1)
                nc.scalar.copy(qT[c][:], bank[6][:, 0:T])
                nc.scalar.copy(kT[c][:], bank[6][:, T:2 * T]).then_inc(qkT_sb, 1)

            def exps(b, s, early):
                act.wait_ge(negmax_ready, PAIRS * b + s + 1)
                if not early:
                    act.wait_ge(pT_ready, 2 * (PAIRS * b + s - 1))
                for j in range(2):
                    for k, lo, hi in ((j, P, 3 * P), (2 + j, 0, P)):
                        last = nc.scalar.activation(probs[s % 2][:, j, lo:hi], pair_bank[s % 2][:, j, lo:hi], ACT.Exp,
                                                    bias=negmax[s % 2][:, k:k + 1], accum_out=psums[s % 2][:, k:k + 1])
                last.then_inc(exp_done, 1)

            def evacuate_pT(b, s, early):
                act.wait_ge(pT_ready, 2 * (PAIRS * b + s) + 2)
                if not early:
                    act.wait_ge(pv_done, PAIRS * b + s - 1)
                nc.scalar.copy(probsT[s % 2][1][:], bank[5][:, 0:3 * P]).then_inc(pT_sb_act, 1)

            def evacuate_oT(b, c, first):
                act.wait_ge(pv_done, PAIRS * b + 4 * (c + 1))
                if not first:
                    act.wait_ge(wout_done, b)
                nc.scalar.copy(oT[c][:], bank[6 + c][:, 0:T]).then_inc(oT_ready, 1)

            def sequence(b, first, last):
                for s in range(PAIRS):
                    if s == 6:
                        evacuate_oT(b, 0, first)
                    exps(b, s, first and s < 2)
                    if s >= 2:
                        evacuate_pT(b, s - 2, first and s - 2 < 2)
                    if s == 6 and not last:
                        evacuate_qk(b + 1, 0, False)
                for s in (PAIRS - 2, PAIRS - 1):
                    evacuate_pT(b, s, False)
                if not last:
                    evacuate_qk(b + 1, 1, False)
                evacuate_oT(b, 1, first)

            act.wait_ge(par_in, 16)
            nc.scalar.activation(tg[:], param("g"), ACT.Tanh).then_inc(gains, 1)
            act.wait_ge(a_var, 1)
            nc.scalar.activation(rk[:], rkr[:], ACT.Sqrt).then_inc(a_root, 1)
            for n, (w, arrived) in enumerate(((w1_raw, w1_in), (w2_raw, w2_in))):
                act.wait_ge(arrived, 16)
                if n:
                    act.wait_ge(w_abs_ready, n)
                nc.scalar.activation(hid_all[:], w[:], ACT.Abs, accum_out=w_abs[:, n:n + 1]).then_inc(w_abs_ready, 1)
            evacuate_qk(0, 0, True)
            evacuate_qk(0, 1, True)
            sequence(0, True, False)
            with act.Fori(1, SEQS - 1) as b:
                sequence(b, False, False)
            sequence(SEQS - 1, False, True)

        def mlp_act(act):
            act.wait_ge(b_var, 1)
            nc.scalar.activation(rstd[:], var_eps[:], ACT.Sqrt).then_inc(b_root, 1)
            for n in range(2):
                act.wait_ge(aT_ready, n + 1)
                src = bank[6 + n].bitcast(BF16).rearrange("p (k t) -> p k t", k=KD)
                nc.scalar.copy(aT[:, :, n * BLK:(n + 1) * BLK], src).then_inc(aT_sb, 1)

            def gelu(t, k):
                act.wait_ge(pre_ready, t + 1)
                nc.scalar.activation(hid[k], pre[k][:], ACT.Gelu).then_inc(gelu_done, 1)

            def scale_and_round(t, k):
                act.wait_ge(hscale_ready, t + 1)
                if not (isinstance(t, int) and t < 2):
                    act.wait_ge(hq_ready, t - 1)
                nc.scalar.activation(hrnd[k][:], hid[k], ACT.Copy, bias=ROUND,
                                     scale=hscale[k][:, 0:1]).then_inc(hrnd_ready, 1)

            def evacuate(t, k):
                act.wait_ge(hqT_ready, t + 1)
                if not (isinstance(t, int) and t < 2):
                    act.wait_ge(y_ready, t - 1)
                nc.scalar.copy(hqT[k][:], bank[4].bitcast(BF16).rearrange("p (c t) -> p c t", c=HK)).then_inc(hqT_sb, 1)

            gelu(0, 0)
            scale_and_round(0, 0)
            gelu(1, 1)
            evacuate(0, 0)
            with act.Fori(1, SEQS) as b:
                for k in range(2):
                    t = 2 * b + k
                    scale_and_round(t - 1, 1 - k)
                    gelu(t, k)
                    evacuate(t - 1, 1 - k)
            scale_and_round(TILES - 1, 1)
            evacuate(TILES - 1, 1)

        def experts_act(act):
            def high_weights(n, k, first):
                if not first:
                    act.wait_ge(down_done, 2 * n - 2)
                nc.scalar.copy(e_hi[k][:], e_raw[k][:]).then_inc(e_hi_ready, 1)

            def select(n, k):
                src = const("expertsel")[:, bass.ds(2 * (n - 1), 2)].unsqueeze(2).broadcast_to([P, 2, EI])
                nc.scalar.copy(sel[k][:].rearrange("p (e i) -> p e i", e=2), src).then_inc(sel_ready, 1)

            def gate(t, k):
                act.wait_ge(gate_ready, t + 1)
                if not (isinstance(t, int) and t < 2):
                    act.wait_ge(up_used, t - 1)
                nc.scalar.activation(silu[k][:], bank[(4, 7)[k]], ACT.Silu).then_inc(silu_done, 1)

            act.wait_ge(d_var, 1)
            nc.scalar.activation(rstd[:], var_eps[:], ACT.Sqrt).then_inc(d_root, 1)
            for n in range(KD * TB):
                act.wait_ge(hTd_ready, n + 1)
                nc.scalar.copy(hT[:, n // 2, (n % 2) * BLK:(n % 2 + 1) * BLK], bank[4 + n]).then_inc(hTd_sb, 1)
            for n in range(2):
                act.wait_ge(e_in[n], 16)
                high_weights(n, n, True)
            select(1, 1)
            act.wait_ge(logits_sb, 1)
            nc.scalar.activation(rexp[:], logits[:], ACT.Exp).then_inc(rexp_done, 1)
            for t in range(2):
                act.wait_ge(weight_ready, t + 1)
                nc.scalar.activation(sgate[t][:], bank[6], ACT.Sigmoid).then_inc(sgate_done, 1)
            for t in range(2):
                gate(t, t)
            for n in range(TB):
                act.wait_ge(combT_ready, n + 1)
                nc.scalar.copy(combT[:, n * BLK:(n + 1) * BLK], bank[n]).then_inc(combT_sb, 1)
            with act.Fori(0, EP // 2 - 1) as i:
                for k in range(2):
                    n = 2 * i + 1 + k
                    gate(2 * n, 0)
                    act.wait_ge(e_in[k], 16 * i + 32)
                    high_weights(n + 1, k, False)
                    select(n + 1, k)
                    gate(2 * n + 1, 1)
            gate(2 * EP - 2, 0)
            act.wait_ge(e_in[0], 16 * (EP // 2 + 1))
            high_weights(EP, 0, False)
            select(EP, 0)
            gate(2 * EP - 1, 1)
            gate(2 * EP, 0)
            gate(2 * EP + 1, 1)
            act.wait_ge(down_done, 2 * EP + 2)
            for n in range(KD * TB):
                nc.scalar.activation(hT[:, n // 2, (n % 2) * BLK:(n % 2 + 1) * BLK], bank[n], ACT.Copy,
                                     scale=tg[:, 3:4]).then_inc(acc_sb, 1)

        def latent_act(act):
            act.wait_ge(c_var, 1)
            nc.scalar.activation(rstd[:], var_eps[:], ACT.Sqrt).then_inc(c_root, 1)
            act.wait_ge(kvT_ready, 1)
            nc.scalar.copy(kvT[0:DC, 0:BLK], bank[0][0:DC, :])
            nc.scalar.copy(kvT[0:DC, BLK:TOK], bank[1][0:DC, :]).then_inc(kvT_sb, 1)
            for n in range(KD * TB):
                act.wait_ge(hT_ready, n + 1)
                nc.scalar.copy(hT[:, n // 2, (n % 2) * BLK:(n % 2 + 1) * BLK], bank[4 + n]).then_inc(hT_sb, 1)

            def project(hp, first):
                act.wait_ge(gq_ready, hp + 1)
                for dk in range(KD):
                    last = nc.scalar.copy(gq[:, dk, :], bank[4 + dk][:, 0:2 * LQ])
                last.then_inc(gq_sb, 1)
                act.wait_ge(mout_ready, hp + 1)
                nc.scalar.copy(mout[:, bass.ds(hp * D, D)], bank[6][:, 0:D]).then_inc(mout_sb, 1)
                act.wait_ge(kr_done, TB * (hp + 1))
                if not first:
                    act.wait_ge(ls_ready, 2 * SEQS * hp)
                for n in range(TB):
                    for j in range(2):
                        rows = slice(j * LR, (j + 1) * LR)
                        last = nc.scalar.copy(krT[j][rows, n * BLK:(n + 1) * BLK], bank[4 + n][rows, :])
                last.then_inc(krT_sb, 1)
                act.wait_ge(qr_step, 6 * (hp + 1))
                for n in range(TB):
                    last = nc.scalar.copy(qrT[:, n * BLK:(n + 1) * BLK], bank[6 + n])
                last.then_inc(qrT_sb, 1)

            def exps(hp, u, early):
                n = 2 * SEQS * hp + u
                act.wait_ge(lneg_ready, n + 1)
                if not early:
                    act.wait_ge(lpT_ready, n - 2)
                for i in range(2):
                    last = nc.scalar.activation(lprobs[u % 3][:, i, :], bank[u % 4][:, i * T:(i + 1) * T], ACT.Exp,
                                                bias=lneg[u % 3][:, i:i + 1], accum_out=lsum[u % 3][:, i:i + 1])
                last.then_inc(lexp_done, 1)

            def evacuate_ctx(hp, b):
                act.wait_ge(lpv_done, SEQS * hp + b + 1)
                nc.scalar.copy(ctxT[:, bass.ds(hp * TOK + b * T, T)], bank[6 + b % 2][:, 0:T]).then_inc(ctxT_sb, 1)

            def pair(hp, first):
                project(hp, first)
                for u in range(2 * SEQS):
                    exps(hp, u, False if not first else u < 3)
                    if u >= 5 and u % 2 == 1:
                        evacuate_ctx(hp, (u - 5) // 2)
                evacuate_ctx(hp, 2)
                evacuate_ctx(hp, 3)

            pair(0, True)
            with act.Fori(1, HP) as hp:
                pair(hp, False)

        @block.scalar
        def _(act):
            attention_a_act(act)
            mlp_act(act)
            latent_act(act)
            experts_act(act)

        def attention_a_pe(pe):
            def transposes(b, c, first):
                if not first:
                    pe.wait_ge(oT_ready, CHUNKS * (b - 1) + 1)
                pe.wait_ge(qrot_ready, b + 1)
                pe.wait_ge(krep_ready, b + 1)
                if not (first and c == 0):
                    pe.wait_ge(qkT_sb, CHUNKS * b + c)
                for i in range(2):
                    q_in = qrot[:, i, c * HPC:(c + 1) * HPC, :]
                    nc.tensor.transpose(bank[6][:, i * P:(i + 1) * P], q_in, ident)
                for i in range(2):
                    k_in = krep[:, i, 2 * c:2 * c + 2]
                    last = nc.tensor.transpose(bank[6][:, T + i * P:T + (i + 1) * P], k_in, ident)
                last.then_inc(qkT_ready, 1)

            def scores(b, s, early):
                c, h = s // 4, 2 * (s % 4)
                if s % 4 == 0:
                    pe.wait_ge(qkT_sb, CHUNKS * b + c + 1)
                    pe.wait_ge(kpad_ready, CHUNKS * b + c + 1)
                if not early:
                    pe.wait_ge(exp_done, PAIRS * b + s - 1)
                for j in range(2):
                    dst = pair_bank[s % 2][:, j]
                    nc.tensor.matmul(dst[:, 0:3 * P], ident_bf[:], mask[:], start=True, stop=False)
                    nc.tensor.matmul(dst[:, 0:P], qT[c][:, 0:P], kpad[c][:, h + j, 0:P], start=False, stop=False)
                    last = nc.tensor.matmul(dst[:, P:3 * P], qT[c][:, P:2 * P], kpad[c][:, h + j, :],
                                            start=False, stop=True)
                last.then_inc(scores_ready, 1)

            def turn_probs(b, s, first):
                pe.wait_ge(probs_ready, PAIRS * b + s + 1)
                for j in range(2):
                    if not (first and s == 0):
                        pe.wait_ge((pT_sb_dve, pT_sb_act)[j], PAIRS * b + s)
                    dst, src = bank[4 + j], probs[s % 2][:, j]
                    nc.tensor.transpose(dst[:, 0:P], src[:, 0:P], ident)
                    nc.tensor.transpose(dst[:, P:2 * P], src[:, P:2 * P], ident)
                    nc.tensor.transpose(dst[:, 2 * P:3 * P], src[:, 2 * P:3 * P], ident).then_inc(pT_ready, 1)

            def values(b, s, first):
                c = s // 4
                if s % 4 == 0:
                    pe.wait_ge(vpad_ready, CHUNKS * b + c + 1)
                    if c == 1 and first:
                        pe.wait_ge(w_scale_ready, 1)
                    if c == 1 and not first:
                        pe.wait_ge(x1_done, b)
                    if c == 0:
                        pe.wait_ge(qkT_sb, CHUNKS * (b + 1))
                pe.wait_ge(pT_sb_dve, PAIRS * b + s + 1)
                pe.wait_ge(pT_sb_act, PAIRS * b + s + 1)
                for j in range(2):
                    h = 2 * (s % 4) + j
                    cols = slice(h * P, (h + 1) * P)
                    nc.tensor.matmul(bank[6 + c][:, 0:T], vpad[c][0][:, cols], probsT[s % 2][j][:, 0:T],
                                     start=(h == 0), stop=False, skip_group_check=True)
                    last = nc.tensor.matmul(bank[6 + c][:, P:T], vpad[c][1][:, cols],
                                            probsT[s % 2][j][:, T:T + P],
                                            start=False, stop=(h == HPC - 1), skip_group_check=True)
                last.then_inc(pv_done, 1)

            def project(b, first):
                pe.wait_ge(oT_ready, CHUNKS * (b + 1))
                if first:
                    pe.wait_ge(wout_in, 16)
                for i in range(2):
                    for c in range(CHUNKS):
                        last = nc.tensor.matmul(bank[7][:, i * D:(i + 1) * D], oT[c][:, i * P:(i + 1) * P],
                                                wout_sb[:, c, :], start=(c == 0), stop=(c == CHUNKS - 1))
                last.then_inc(wout_done, 1)

            def sequence(b, first, last):
                for s in range(PAIRS):
                    scores(b, s, first and s < 2)
                    if s >= 1:
                        turn_probs(b, s - 1, first)
                    if s >= 2:
                        values(b, s - 2, first)
                    if s == 6 and not last:
                        transposes(b + 1, 0, False)
                turn_probs(b, PAIRS - 1, first)
                values(b, PAIRS - 2, first)
                if not last:
                    transposes(b + 1, 1, False)
                values(b, PAIRS - 1, first)
                project(b, first)

            pe.wait_ge(consts_made, 4)
            pe.wait_ge(c_in, 16)
            pe.wait_ge(w_abs_ready, 2)
            nc.tensor.matmul(bank[7][:, 0:2], ones[:], w_abs[:], start=True, stop=True).then_inc(w_sum_ready, 1)
            transposes(0, 0, True)
            transposes(0, 1, True)
            sequence(0, True, False)
            with pe.Fori(1, SEQS - 1) as b:
                sequence(b, False, False)
            sequence(SEQS - 1, False, True)

        def mlp_pe(pe):
            for n in range(2):
                pe.wait_ge(aq_ready, 1)
                dst = bank[6 + n].bitcast(BF16).rearrange("p (k t) -> p k t", k=KD)
                for i in range(4):
                    for k in range(KD):
                        last = nc.tensor.transpose(dst[:, k, i * P:(i + 1) * P],
                                                   aq[:, 4 * n + i, k * P:(k + 1) * P], ident_bf[:])
                last.then_inc(aT_ready, 1)
            pe.wait_ge(aT_sb, 2)
            pe.wait_ge(wq_ready, 2)

            def first(t, k):
                if not (isinstance(t, int) and t < 2):
                    pe.wait_ge(pre_ready, t - 1)
                for half in range(2):
                    for c in range(KD):
                        last = nc.tensor.matmul(pair_bank[k][:, half, :], aT[:, c, bass.ds(t * P, P)],
                                                w1q[:, c, half * 512:(half + 1) * 512],
                                                start=(c == 0), stop=(c == KD - 1))
                last.then_inc(h1_ready, 1)

            def second(t, k):
                pe.wait_ge(hq_ready, t + 1)
                if not (isinstance(t, int) and t == 0):
                    pe.wait_ge(hqT_sb, t)
                for c in range(HK):
                    last = nc.tensor.transpose(bank[4].bitcast(BF16)[:, c * P:(c + 1) * P],
                                               hq[k][:, c * P:(c + 1) * P], ident_bf[:])
                last.then_inc(hqT_ready, 1)
                pe.wait_ge(hqT_sb, t + 1)
                if not (isinstance(t, int) and t < 2):
                    pe.wait_ge(x2_done, t - 1)
                for c in range(HK):
                    last = nc.tensor.matmul(bank[6 + k][:, 0:D], hqT[k][:, c, :], w2q[:, c, :],
                                            start=(c == 0), stop=(c == HK - 1))
                last.then_inc(y_ready, 1)

            first(0, 0)
            first(1, 1)
            second(0, 0)
            with pe.Fori(1, SEQS) as b:
                for k in range(2):
                    first(2 * b + k, k)
                    second(2 * b + k - 1, 1 - k)
            second(TILES - 1, 1)

        def experts_pe(pe):
            pe.wait_ge(xd_ready, 1)
            for n in range(KD * TB):
                k, half = n // 2, n % 2
                for i in range(4):
                    last = nc.tensor.transpose(bank[4 + n][:, i * P:(i + 1) * P],
                                               xn[:, 4 * half + i, k * P:(k + 1) * P], ident)
                last.then_inc(hTd_ready, 1)
            pe.wait_ge(router_in, 32)
            pe.wait_ge(hTd_sb, KD * TB)
            for i in range(TILES):
                for k in range(KD):
                    last = nc.tensor.matmul(bank[7][:, i * E:(i + 1) * E], hT[:, k, i * P:(i + 1) * P], router_sb[:, k, :],
                                            start=(k == 0), stop=(k == KD - 1))
            last.then_inc(logits_ready, 1)

            def split_product(dst, w_cols, moving_hi, moving_lo, ek, start, stop, **kw):
                for n, (w, m) in enumerate(((e_hi, moving_hi), (e_lo, moving_hi), (e_hi, moving_lo))):
                    last = nc.tensor.matmul(dst, w[ek][:, w_cols], m, start=start and n == 0, stop=stop and n == 2, **kw)
                return last

            def gate(n, blk, ek):
                t = 2 * n + blk
                early = isinstance(t, int) and t < 2
                cols = slice(blk * BLK, (blk + 1) * BLK)
                if blk == 0:
                    pe.wait_ge(e_lo_ready, n + 1)
                if not early:
                    pe.wait_ge(silu_done, t - 1)
                gate_bank = bank[(4, 7)[blk]]
                for dk in range(KD):
                    last = split_product(gate_bank, slice(dk * 2 * P, dk * 2 * P + P), hT_hi[:, dk, cols], hT_lo[:, dk, cols],
                                         ek, dk == 0, dk == KD - 1)
                last.then_inc(gate_ready, 1)

            def up(n, blk, ek):
                t = 2 * n + blk
                cols = slice(blk * BLK, (blk + 1) * BLK)
                if not (isinstance(t, int) and t == 0):
                    pe.wait_ge(up_used, t)
                for dk in range(KD):
                    last = split_product(bank[5], slice(dk * 2 * P + P, (dk + 1) * 2 * P), hT_hi[:, dk, cols], hT_lo[:, dk, cols],
                                         ek, dk == 0, dk == KD - 1)
                last.then_inc(up_ready, 1)

            def routed(n, blk, ek):
                t = 2 * n + blk
                if blk == 0:
                    pe.wait_ge(sel_ready, n)
                pe.wait_ge(act_ready, t)
                nc.tensor.matmul(bank[6], sel[ek][:], combT[:, blk * BLK:(blk + 1) * BLK], start=True,
                                 stop=True).then_inc(weight_ready, 1)

            def down(t, blk, ek, stop=False):
                pe.wait_ge(act_hi_ready, t + 1)
                pe.wait_ge(act_lo_ready, t + 1)
                for f in range(KD):
                    last = split_product(bank[2 * f + blk], slice(EW - D + f * P, EW - D + (f + 1) * P), act_hi[blk][:],
                                         act_lo[blk][:], ek, False, stop, skip_group_check=True)
                last.then_inc(down_done, 1)

            pe.wait_ge(hT_split, 1)
            for blk in range(TB):
                if blk == 1:
                    pe.wait_ge(logits_sb, 1)
                gate(0, blk, 0)
                if blk == 1:
                    pe.wait_ge(sgate_done, 1)
                for k in range(KD):
                    last = nc.tensor.matmul(bank[6], wsg_sb[:, k, :], hT[:, k, blk * BLK:(blk + 1) * BLK],
                                            start=(k == 0), stop=(k == KD - 1))
                last.then_inc(weight_ready, 1)
                up(0, blk, 0)
            pe.wait_ge(comb_ready, 1)
            for n in range(TB):
                for i in range(4):
                    last = nc.tensor.transpose(bank[n][:, i * P:(i + 1) * P], comb2[:, 4 * n + i, :], ident)
                last.then_inc(combT_ready, 1)
            pe.wait_ge(zeros_ready, 1)
            pe.wait_ge(combT_sb, TB)
            for n in range(KD * TB):
                nc.tensor.matmul(bank[n], ident_bf[:], zeros_bf[:], start=True, stop=False, skip_group_check=True)
            down(0, 0, 0)
            with pe.Fori(0, EP // 2) as i:
                for k in range(2):
                    n, ek = 2 * i + 1 + k, 1 - k
                    for blk in range(TB):
                        gate(n, blk, ek)
                        up(n, blk, ek)
                        routed(n, blk, ek)
                        down(2 * n + blk - 1, 1 - blk, ek if blk else 1 - ek)
            down(2 * EP + 1, 1, 0, stop=True)
            for b in range(SEQS):
                blk = b // 2
                pe.wait_ge(acc_sb, KD * TB if blk else KD * TB - 1)
                for i in range(2):
                    for f in range(KD):
                        at = (2 * b + i) * P
                        last = nc.tensor.transpose(bank[4 + b][:, i * D + f * P:i * D + (f + 1) * P], hT[:, f, at:at + P], ident)
                last.then_inc(y_turned, 1)

        def latent_pe(pe):
            pe.wait_ge(x2_done, TILES)
            pe.wait_ge(kvr_ready, 5)
            for i in range(TILES):
                last = nc.tensor.transpose(bank[i // 4][0:DC, (i % 4) * P:(i % 4 + 1) * P], kvr[:, i, DC:2 * DC], ident)
            last.then_inc(kvT_ready, 1)
            pe.wait_ge(xn_ready, 1)
            for n in range(KD * TB):
                k, half = n // 2, n % 2
                for i in range(4):
                    last = nc.tensor.transpose(bank[4 + n][:, i * P:(i + 1) * P],
                                               xn[:, 4 * half + i, k * P:(k + 1) * P], ident)
                last.then_inc(hT_ready, 1)
            pe.wait_ge(kvT_sb, 1)
            pe.wait_ge(hT_sb, KD * TB)

            def project(hp, first):
                pe.wait_ge(wq_in, 16 * hp + 16)
                pe.wait_ge(wkcq_in, 16 * hp + 16)
                if not first:
                    pe.wait_ge(lpT_sb, 2 * SEQS * hp)
                    pe.wait_ge(ctxT_sb, SEQS * hp)
                for dk in range(KD):
                    for j in range(2):
                        last = nc.tensor.matmul(bank[4 + dk][:, j * LQ:(j + 1) * LQ], wq_sb[:, j, dk * P:(dk + 1) * P],
                                                wkcq_sb[:, j, :], start=True, stop=True)
                last.then_inc(gq_ready, 1)
                pe.wait_ge(wkckv_in, 16 * hp + 16)
                pe.wait_ge(woT_in, 16 * hp + 16)
                for j in range(2):
                    last = nc.tensor.matmul(bank[6][j * DC:(j + 1) * DC, 0:D], wkckv_sb[:, j, :], woT_sb[:, j, :],
                                            start=True, stop=True)
                last.then_inc(mout_ready, 1)
                pe.wait_ge(wkr_in, 16 * hp + 16)
                pe.wait_ge(gq_sb, hp + 1)
                for n in range(TB):
                    nc.tensor.matmul(bank[4 + n], wkr_sb[:].rearrange("p j r -> p (j r)"), kvT[:, n * BLK:(n + 1) * BLK],
                                     start=True, stop=True).then_inc(kr_done, 1)
                pe.wait_ge(wqr_in, 16 * hp + 16)
                pe.wait_ge(mout_sb, hp + 1)
                if not first:
                    pe.wait_ge(lexp_done, 2 * SEQS * hp)

                def queries(v):
                    f, n = v // TB, v % TB
                    if v >= 4:
                        pe.wait_ge(lq_turned, 6 * hp + v - 3)
                    for dk in range(KD):
                        last = nc.tensor.matmul(bank[v % 4], gq[:, dk, f * P:(f + 1) * P], hT[:, dk, n * BLK:(n + 1) * BLK],
                                                start=(dk == 0), stop=(dk == KD - 1))
                    last.then_inc(lq_ready, 1)

                def reduced(v):
                    f, n = v // TB, v % TB
                    pe.wait_ge(lq_turned, 6 * hp + v + 1)
                    for k in range(2):
                        last = nc.tensor.matmul(bank[6 + n], wqr_sb[:, k, f, :], turned[v % 2][:, k, :],
                                                start=(f == 0 and k == 0), stop=(f == FCH - 1 and k == 1))
                    last.then_inc(qr_step, 1)

                for v in range(6):
                    queries(v)
                    if v >= 2:
                        reduced(v - 2)
                reduced(4)
                reduced(5)

            def scores(hp, u):
                b, j = u // 2, u % 2
                if u == 0:
                    pe.wait_ge(qrT_sb, hp + 1)
                    pe.wait_ge(krT_sb, hp + 1)
                if u >= 4:
                    pe.wait_ge(lexp_done, 2 * SEQS * hp + u - 3)
                for i in range(2):
                    last = nc.tensor.matmul(bank[u % 4][:, i * T:(i + 1) * T], qrT[:, (2 * b + i) * P:(2 * b + i + 1) * P],
                                            krT[j][:, b * T:(b + 1) * T], start=True, stop=True)
                last.then_inc(ls_ready, 1)

            def turn_probs(hp, u):
                pe.wait_ge(lprobs_ready, 2 * SEQS * hp + u + 1)
                if u >= 2:
                    pe.wait_ge(lpT_sb, 2 * SEQS * hp + u - 1)
                for kt in range(2):
                    for i in range(2):
                        last = nc.tensor.transpose(bank[4 + u % 2][:, kt * T + i * P:kt * T + (i + 1) * P],
                                                   lprobs[u % 3][:, i, kt * P:(kt + 1) * P], ident)
                last.then_inc(lpT_ready, 1)

            def values(hp, u):
                b, j = u // 2, u % 2
                pe.wait_ge(lpT_sb, 2 * SEQS * hp + u + 1)
                if j == 0 and b >= 2:
                    pe.wait_ge(ctxT_sb, SEQS * hp + b - 1)
                lo = (1 - j) * DC
                for kt in range(2):
                    last = nc.tensor.matmul(bank[6 + b % 2][:, 0:T], kvr[:, 2 * b + kt, lo:lo + P], lprobsT[u % 2][:, kt, :],
                                            start=(j == 0 and kt == 0), stop=(j == 1 and kt == 1))
                if j == 1:
                    last.then_inc(lpv_done, 1)
                else:
                    last.then_inc(lpv_half, 1)

            def pair(hp, first):
                project(hp, first)
                n = 2 * SEQS
                for u in range(n):
                    scores(hp, u)
                    if u >= 2:
                        turn_probs(hp, u - 2)
                    if u >= 3:
                        values(hp, u - 3)
                turn_probs(hp, n - 2)
                values(hp, n - 3)
                turn_probs(hp, n - 1)
                values(hp, n - 2)
                values(hp, n - 1)

            pair(0, True)
            with pe.Fori(1, HP) as hp:
                pair(hp, False)
            pe.wait_ge(ctxT_sb, SEQS * HP)
            pe.wait_ge(mout_sb, HP)
            pe.wait_ge(lexp_done, 2 * SEQS * HP)
            for i in range(TILES):
                if i >= 4:
                    pe.wait_ge(x3_done, i - 3)
                for hp in range(HP):
                    last = nc.tensor.matmul(bank[i % 4][:, 0:D], ctxT[:, hp * TOK + i * P:hp * TOK + (i + 1) * P],
                                            mout[:, hp * D:(hp + 1) * D], start=(hp == 0), stop=(hp == HP - 1))
                last.then_inc(x3_ready, 1)

        @block.tensor
        def _(pe):
            attention_a_pe(pe)
            mlp_pe(pe)
            latent_pe(pe)
            experts_pe(pe)

        def attention_a_dve(dve):
            link = OwnSteps(dve, dve_setup, 18)
            nc.vector.memset(ones[:], 1.0).then_inc(consts_made, 1)
            dve.wait_ge(x_in, 16)
            for i in range(TILES):
                last = nc.vector.bn_stats(stats[:, i, :], x_sb[:, i, :])
            link(last)
            for i in range(TILES):
                last = nc.vector.bn_aggr(mv[:, i, :], stats[:, i, :])
            link(last)
            v = mv[:, :, 1]
            link(nc.vector.tensor_scalar(var_eps[:], v, EPS, None, ALU.add))
            link(nc.vector.reciprocal(rstd[:], var_eps[:]))
            link(nc.vector.tensor_tensor(var_eps[:], v, rstd[:], ALU.mult))
            link(nc.vector.tensor_scalar(var_eps[:], var_eps[:], EPS, None, ALU.add))
            link(nc.vector.reciprocal(var_eps[:], var_eps[:]))
            link(nc.vector.tensor_tensor(rkr[:, 0:TILES], rstd[:], var_eps[:], ALU.mult))
            dve.wait_ge(ctx_in, 16)
            link(nc.vector.tensor_tensor(kq[:], ctx_sb[:], ctx_sb[:], ALU.mult))
            link(nc.vector.tensor_reduce(rk[:, 0:TILES], kq[:], AX.X, ALU.add))
            link(nc.vector.tensor_scalar(rk[:, 0:TILES], rk[:, 0:TILES], 1.0 / DC, EPS, ALU.mult, ALU.add))
            nc.vector.reciprocal(rkr[:, TILES:], rk[:, 0:TILES]).then_inc(a_var, 1)
            dve.wait_ge(c_in, 16)
            nc.vector.tensor_copy(ident_bf[:], ident).then_inc(consts_made, 1)
            nc.vector.memset(mask[:, P:2 * P], 0.0).then_inc(consts_made, 1)
            nc.vector.tensor_copy(mask[:].rearrange("p (a k) -> p a k", a=3)[:, 0:3:2],
                                  const("causal").unsqueeze(1).broadcast_to([P, 2, P])).then_inc(consts_made, 1)
            dve.wait_ge(par_in, 16)

            def rope_tables(cos, sin, w, heads, scale):
                hw = HD // 2
                c3 = const("cos0").rearrange("p (i d) -> p i d", d=HD)
                s3 = const("sin0").rearrange("p (i d) -> p i d", d=HD)
                w3 = w.rearrange("p (h d) -> p h d", d=HD)
                for i in range(2):
                    nc.vector.scalar_tensor_tensor(out=cos[:, i], in0=c3[:, i].unsqueeze(1).broadcast_to([P, heads, HD]),
                                                   scalar=scale, in1=w3, op0=ALU.mult, op1=ALU.mult)
                    for lo, other in ((0, hw), (hw, 0)):
                        last = nc.vector.scalar_tensor_tensor(
                            out=sin[:, i, :, lo:lo + hw],
                            in0=s3[:, i, lo:lo + hw].unsqueeze(1).broadcast_to([P, heads, hw]),
                            scalar=scale, in1=w3[:, :, other:other + hw], op0=ALU.mult, op1=ALU.mult)
                link(last)

            rope_tables(ck0, sk0, param("kw"), GROUPS, 1.0)
            rope_tables(cq0, sq0, param("qw"), QH, HD ** -0.5)
            dve.wait_ge(a_root, 1)
            link(nc.vector.tensor_tensor(kn[:], ctx_sb[:], rk[:, TILES:].unsqueeze(2).broadcast_to([P, TILES, DC]), ALU.mult))
            k4 = kn[:].rearrange("p (b e) d -> p b (e d)", e=2)
            hw = HD // 2
            link(nc.vector.tensor_tensor(kr[:].rearrange("p (b e) d -> p b (e d)", e=2), k4,
                                         ck0[:].rearrange("p i g d -> p (i g d)").unsqueeze(1).broadcast_to([P, SEQS, 2 * DC]), ALU.mult))
            kh = kn[:].rearrange("p (b e) (g d) -> p b (e g) d", e=2, d=HD)
            th = ktmp[:].rearrange("p (b e) (g d) -> p b (e g) d", e=2, d=HD)
            sh = sk0[:].rearrange("p i g d -> p (i g) d")
            for lo, other in ((0, hw), (hw, 0)):
                last = nc.vector.tensor_tensor(
                    th[:, :, :, lo:lo + hw], kh[:, :, :, other:other + hw],
                    sh[:, :, lo:lo + hw].unsqueeze(1).broadcast_to([P, SEQS, 2 * GROUPS, hw]), ALU.mult)
            link(last)
            nc.vector.tensor_tensor(kr[:], kr[:], ktmp[:], ALU.add).then_inc(kr_ready, 1)
            for i in range(TILES):
                last = nc.vector.tensor_scalar(xn[:, i, :], x_sb[:, i, :], mv[:, i, 0:1], rk[:, i:i + 1],
                                               ALU.subtract, ALU.mult)
            link(last)
            own_q = OwnSteps(dve, dve_q, 1)
            soft = OwnSteps(dve, dve_soft, PAIRS + 1)

            def rotate_queries(b, first):
                own_q.round(b)
                if not first:
                    dve.wait_ge(qkT_ready, CHUNKS * b)
                q4 = xn[:, bass.ds(2 * b, 2), :].rearrange("p i (h d) -> p (i h) d", d=HD)
                flat = lambda t: t[:].rearrange("p i h d -> p (i h) d")
                nc.vector.tensor_tensor(flat(qrot), q4, flat(cq0), ALU.mult)
                for lo, other in ((0, hw), (hw, 0)):
                    last = nc.vector.tensor_tensor(flat(qtmp)[:, :, lo:lo + hw], q4[:, :, other:other + hw],
                                                   flat(sq0)[:, :, lo:lo + hw], ALU.mult)
                own_q(last)
                nc.vector.tensor_tensor(qrot[:], qrot[:], qtmp[:], ALU.add).then_inc(qrot_ready, 1)

            def maxima(b, s):
                dve.wait_ge(scores_ready, PAIRS * b + s + 1)
                nc.vector.tensor_reduce(negmax[s % 2][:, 0:2], pair_bank[s % 2][:, :, P:3 * P],
                                        AX.X, ALU.max, negate=True)
                nc.vector.tensor_reduce(negmax[s % 2][:, 2:4], pair_bank[s % 2][:, :, 0:P],
                                        AX.X, ALU.max, negate=True).then_inc(negmax_ready, 1)

            def normalise(b, s):
                dve.wait_ge(exp_done, PAIRS * b + s + 1)
                soft(nc.vector.reciprocal(pinv[s % 2][:], psums[s % 2][:]))
                for j in range(2):
                    nc.vector.tensor_scalar(probs[s % 2][:, j, P:3 * P], probs[s % 2][:, j, P:3 * P],
                                            pinv[s % 2][:, j:j + 1], None, ALU.mult)
                for j in range(2):
                    last = nc.vector.tensor_scalar(probs[s % 2][:, j, 0:P], probs[s % 2][:, j, 0:P],
                                                   pinv[s % 2][:, 2 + j:3 + j], None, ALU.mult)
                last.then_inc(probs_ready, 1)

            def evacuate_pT(b, s, early):
                dve.wait_ge(pT_ready, 2 * (PAIRS * b + s) + 1)
                if not early:
                    dve.wait_ge(pv_done, PAIRS * b + s - 1)
                nc.vector.tensor_copy(probsT[s % 2][0][:], bank[4][:, 0:3 * P]).then_inc(pT_sb_dve, 1)

            def residual(b):
                dve.wait_ge(wout_done, b + 1)
                xs = x_sb[:, bass.ds(2 * b, 2), :].rearrange("p i d -> p (i d)")
                nc.vector.scalar_tensor_tensor(out=xs, in0=bank[7][:], scalar=tg[:, 0:1], in1=xs,
                                               op0=ALU.mult, op1=ALU.add).then_inc(x1_done, 1)
                soft.n += 1
                dve.wait_ge(x1_done, b + 1)
                for i in range(2):
                    last = nc.vector.bn_stats(stats[:, bass.ds(2 * b + i, 1), :].rearrange("p o s -> p (o s)"),
                                              x_sb[:, bass.ds(2 * b + i, 1), :].rearrange("p o d -> p (o d)"))
                last.then_inc(dve_soft, 1)

            def sequence(b, last):
                soft.round(b)
                for s in range(PAIRS):
                    maxima(b, s)
                    if s >= 1:
                        normalise(b, s - 1)
                    if s >= 2:
                        evacuate_pT(b, s - 2, isinstance(b, int) and b == 0 and s - 2 < 2)
                    if s == 1 and not last:
                        rotate_queries(b + 1, False)
                normalise(b, PAIRS - 1)
                evacuate_pT(b, PAIRS - 2, False)
                evacuate_pT(b, PAIRS - 1, False)
                residual(b)

            rotate_queries(0, True)
            dve.wait_ge(w_sum_ready, 1)
            link(nc.vector.tensor_scalar(w_mean[:], bank[7][:, 0:2], 1.0 / (D * HID), TINY, ALU.mult, ALU.max))
            nc.vector.reciprocal(w_scale[:], w_mean[:]).then_inc(w_scale_ready, 1)
            link.done()
            dve.wait_ge(gains, 1)
            sequence(0, False)
            with dve.Fori(1, SEQS - 1) as b:
                sequence(b, False)
            sequence(SEQS - 1, True)

        def mlp_dve(dve):
            own = OwnSteps(dve, dve_b, 10)
            dve.wait_ge(dve_soft, SEQS * (PAIRS + 1))
            for i in range(TILES):
                last = nc.vector.bn_aggr(mv[:, i, :], stats[:, i, :])
            own(last)
            nc.vector.tensor_scalar(var_eps[:], mv[:, :, 1], EPS, None, ALU.add).then_inc(b_var, 1)
            dve.wait_ge(b_root, 1)
            own(nc.vector.reciprocal(rstd[:], rstd[:]))
            for i in range(TILES):
                last = nc.vector.tensor_scalar(xn[:, i, :], x_sb[:, i, :], mv[:, i, 0:1], rstd[:, i:i + 1],
                                               ALU.subtract, ALU.mult)
            own(last)
            own(nc.vector.tensor_reduce(amax[:], xn[:], AX.X, ALU.max, apply_absolute_value=True))
            own(nc.vector.tensor_scalar(amax[:], amax[:], TINY, None, ALU.max))
            own(nc.vector.reciprocal(ascale[:], amax[:]))
            own(nc.vector.tensor_scalar(ascale[:], ascale[:], 127.0, None, ALU.mult))
            for i in range(TILES):
                last = nc.vector.tensor_scalar(xn[:, i, :], xn[:, i, :], ascale[:, i:i + 1], ROUND, ALU.mult, ALU.add)
            own(last)
            nc.vector.tensor_scalar(aq[:], xn[:], ROUND, 127.0, ALU.subtract, ALU.min).then_inc(aq_ready, 1)
            own(nc.vector.tensor_scalar(adeq[:], amax[:], w_mean[:, 0:1], 1.0 / 127.0, ALU.mult, ALU.mult))
            own_h = OwnSteps(dve, dve_h, 4)

            def before_gelu(t, k):
                dve.wait_ge(h1_ready, t + 1)
                if not (isinstance(t, int) and t < 2):
                    dve.wait_ge(gelu_done, t - 1)
                nc.vector.scalar_tensor_tensor(
                    out=pre[k][:], in0=pair_bank[k][:].rearrange("p a n -> p (a n)"), scalar=adeq[:, bass.ds(t, 1)],
                    in1=param("b1"), op0=ALU.mult, op1=ALU.add).then_inc(pre_ready, 1)

            def row_scale(t, k):
                own_h.round(t)
                dve.wait_ge(gelu_done, t + 1)
                own_h(nc.vector.tensor_reduce(hmax[k][:], hid[k], AX.X, ALU.max, apply_absolute_value=True))
                own_h(nc.vector.tensor_scalar(hmax[k][:], hmax[k][:], TINY, None, ALU.max))
                own_h(nc.vector.reciprocal(hinv[k][:], hmax[k][:]))
                nc.vector.tensor_scalar(hscale[k][:], hinv[k][:], 127.0, None, ALU.mult).then_inc(hscale_ready, 1)
                own_h(nc.vector.tensor_scalar(hdeq[k][:], hmax[k][:], w_mean[:, 1:2], 1.0 / 127.0, ALU.mult, ALU.mult))

            def residual(t, k):
                dve.wait_ge(y_ready, t + 1)
                nc.vector.scalar_tensor_tensor(out=yb[k][:], in0=bank[6 + k][:, 0:D], scalar=hdeq[k][:, 0:1],
                                               in1=param("b2"), op0=ALU.mult, op1=ALU.add).then_inc(yb_ready, 1)
                dve.wait_ge(yb_ready, t + 1)
                xs = x_sb[:, bass.ds(t, 1), :].rearrange("p o d -> p (o d)")
                nc.vector.scalar_tensor_tensor(out=xs, in0=yb[k][:], scalar=tg[:, 2:3], in1=xs,
                                               op0=ALU.mult, op1=ALU.add).then_inc(x2_done, 1)
                dve.wait_ge(x2_done, t + 1)
                nc.vector.bn_stats(stats[:, bass.ds(t, 1), :].rearrange("p o s -> p (o s)"), xs).then_inc(b_stats, 1)

            before_gelu(0, 0)
            row_scale(0, 0)
            before_gelu(1, 1)
            row_scale(1, 1)
            residual(0, 0)
            with dve.Fori(1, SEQS) as b:
                for k in range(2):
                    t = 2 * b + k
                    before_gelu(t, k)
                    row_scale(t, k)
                    residual(t - 1, 1 - k)
            residual(TILES - 1, 1)

        def layer_norm(dve, own, var_ready, root_ready, normed):
            for i in range(TILES):
                last = nc.vector.bn_aggr(mv[:, i, :], stats[:, i, :])
            own(last)
            nc.vector.tensor_scalar(var_eps[:], mv[:, :, 1], EPS, None, ALU.add).then_inc(var_ready, 1)
            dve.wait_ge(root_ready, 1)
            own(nc.vector.reciprocal(rstd[:], rstd[:]))
            for i in range(TILES):
                last = nc.vector.tensor_scalar(xn[:, i, :], x_sb[:, i, :], mv[:, i, 0:1], rstd[:, i:i + 1],
                                               ALU.subtract, ALU.mult)
            last.then_inc(normed, 1)

        def experts_dve(dve):
            dve.wait_ge(c_stats, TILES)
            own = OwnSteps(dve, dve_d, 3)
            layer_norm(dve, own, d_var, d_root, xd_ready)
            dve.wait_ge(hTd_sb, KD * TB)
            own(nc.vector.tensor_copy(hT_hi[:], hT[:]))
            nc.vector.tensor_tensor(hT_lo[:], hT[:], hT_hi[:].bitcast(F32), ALU.subtract).then_inc(hT_split, 1)
            own.done()
            link = OwnSteps(dve, dve_r, 8)
            dve.wait_ge(logits_ready, 1)
            lg = bank[7].rearrange("p (i e) -> p i e", e=E)
            link(nc.vector.tensor_reduce(rmax[:], lg, AX.X, ALU.max))
            nc.vector.tensor_tensor(logits[:], lg, rmax[:].unsqueeze(2).broadcast_to([P, TILES, E]),
                                    ALU.subtract).then_inc(logits_sb, 1)
            dve.wait_ge(rexp_done, 1)
            for i in range(TILES):
                last = nc.vector.max(top8[:, i, :], rexp[:, i, :])
            link(last)
            for i in range(TILES):
                last = nc.vector.match_replace(chosen[:, i, :], top8[:, i, :], rexp[:, i, :], -1.0)
            link(last)
            link(nc.vector.tensor_reduce(tsum[:], top8[:], AX.X, ALU.add))
            link(nc.vector.reciprocal(tinv[:], tsum[:]))
            link(nc.vector.scalar_tensor_tensor(out=comb[:], in0=chosen[:], scalar=0.0, in1=rexp[:],
                                                op0=ALU.is_lt, op1=ALU.mult))
            link(nc.vector.tensor_tensor(comb[:], comb[:], tinv[:].unsqueeze(2).broadcast_to([P, TILES, E]), ALU.mult))
            link(nc.vector.tensor_copy(comb2[:, :, 0:E].bitcast(F32R), comb[:]))
            nc.vector.tensor_tensor(comb2[:, :, E:2 * E].bitcast(F32R), comb[:], comb2[:, :, 0:E],
                                    ALU.subtract).then_inc(comb_ready, 1)
            link.done()

            def weigh(t, k, weights, ready, count):
                dve.wait_ge(silu_done, t + 1)
                dve.wait_ge(up_ready, t + 1)
                nc.vector.tensor_tensor(act_u[:], silu[k][:], bank[5], ALU.mult).then_inc(up_used, 1)
                dve.wait_ge(up_used, t + 1)
                if not (isinstance(t, int) and t < 2):
                    dve.wait_ge(act_lo_ready, t - 1)
                dve.wait_ge(ready, count)
                nc.vector.tensor_tensor(act_w[k][:], act_u[:], weights, ALU.mult).then_inc(act_ready, 1)
                dve.wait_ge(act_ready, t + 1)
                if not (isinstance(t, int) and t < 2):
                    dve.wait_ge(down_done, t - 1)
                nc.vector.tensor_copy(act_hi[k][:], act_w[k][:]).then_inc(act_hi_ready, 1)

            for t in range(2):
                weigh(t, t, sgate[t][:], sgate_done, t + 1)
            with dve.Fori(0, EP) as i:
                for k in range(2):
                    t = 2 * i + 2 + k
                    weigh(t, k, bank[6], weight_ready, t + 1)
            for b in range(SEQS):
                dve.wait_ge(y_turned, b + 1)
                xs = x_sb[:, 2 * b:2 * b + 2, :].rearrange("p i d -> p (i d)")
                nc.vector.tensor_tensor(xs, bank[4 + b], xs, ALU.add).then_inc(x4_done, 1)

        def latent_dve(dve):
            dve.wait_ge(b_stats, TILES)
            own = OwnSteps(dve, dve_c, 2)
            layer_norm(dve, own, c_var, c_root, xn_ready)
            own.done()
            soft = OwnSteps(dve, dve_l, 2 * SEQS)
            cos = const("cosq").rearrange("p (c t) -> p c t", c=FCH)
            sin = const("sinq").rearrange("p (c t) -> p c t", c=FCH)

            def turn(hp, v, first):
                f = v // TB
                dve.wait_ge(lq_ready, 6 * hp + v + 1)
                if not (first and v < 2):
                    dve.wait_ge(qr_step, 6 * hp + v - 1)
                src = bank[v % 4].rearrange("p (b t) -> p b t", b=2)
                for k, table in enumerate((cos, sin)):
                    last = nc.vector.tensor_tensor(turned[v % 2][:, k].rearrange("p (b t) -> p b t", b=2), src,
                                                   table[:, f].unsqueeze(1).broadcast_to([P, 2, T]), ALU.mult)
                last.then_inc(lq_turned, 1)

            def maxima(hp, u):
                dve.wait_ge(ls_ready, 2 * SEQS * hp + u + 1)
                nc.vector.tensor_reduce(lneg[u % 3][:], bank[u % 4].rearrange("p (i k) -> p i k", i=2), AX.X,
                                        ALU.max, negate=True).then_inc(lneg_ready, 1)

            def normalise(hp, u):
                dve.wait_ge(lexp_done, 2 * SEQS * hp + u + 1)
                soft(nc.vector.reciprocal(linv[u % 3][:], lsum[u % 3][:]))
                for i in range(2):
                    last = nc.vector.tensor_scalar(lprobs[u % 3][:, i, :], lprobs[u % 3][:, i, :],
                                                   linv[u % 3][:, i:i + 1], None, ALU.mult)
                last.then_inc(lprobs_ready, 1)

            def evacuate(hp, u, first):
                dve.wait_ge(lpT_ready, 2 * SEQS * hp + u + 1)
                if not (first and u < 2):
                    dve.wait_ge((lpv_half, lpv_done)[u % 2], SEQS * hp + u // 2)
                nc.vector.tensor_copy(lprobsT[u % 2][:].rearrange("p k t -> p (k t)"), bank[4 + u % 2]).then_inc(lpT_sb, 1)

            def pair(hp, first):
                soft.round(hp)
                for v in range(6):
                    turn(hp, v, first)
                n = 2 * SEQS
                for u in range(n):
                    maxima(hp, u)
                    if u >= 1:
                        normalise(hp, u - 1)
                    if u >= 3:
                        evacuate(hp, u - 3, first)
                normalise(hp, n - 1)
                for u in (n - 3, n - 2, n - 1):
                    evacuate(hp, u, first)

            pair(0, True)
            with dve.Fori(1, HP) as hp:
                pair(hp, False)
            for i in range(TILES):
                dve.wait_ge(x3_ready, i + 1)
                nc.vector.scalar_tensor_tensor(out=x_sb[:, i, :], in0=bank[i % 4][:, 0:D], scalar=tg[:, 1:2],
                                               in1=x_sb[:, i, :], op0=ALU.mult, op1=ALU.add).then_inc(x3_done, 1)
                dve.wait_ge(x3_done, i + 1)
                nc.vector.bn_stats(stats[:, i, :], x_sb[:, i, :]).then_inc(c_stats, 1)

        @block.vector
        def _(dve):
            attention_a_dve(dve)
            mlp_dve(dve)
            latent_dve(dve)
            experts_dve(dve)


def laid_out(i):
    f = {k: np.ascontiguousarray(v) for k, v in i.items()}
    c = np.ascontiguousarray

    def rows(*vs):
        return c(np.broadcast_to(np.concatenate([v.reshape(-1) for v in vs])[None], (P, sum(v.size for v in vs))))

    wqr = f["L1_xattn_W_qr"]
    half = LQ // 2
    turned = np.concatenate([wqr[:, half:], wqr[:, :half]], 1)
    both = np.zeros((HP, 2, 2 * LQ, P), wqr.dtype)
    for n, w in enumerate((wqr, turned)):
        for j in range(2):
            both[:, n, j * LQ:(j + 1) * LQ, j * LR:(j + 1) * LR] = w[j::2]
    wqr2 = both.reshape(HP, 2, FCH, P, P).transpose(0, 3, 1, 2, 4)
    wkr = f["L1_xattn_W_kr"].reshape(HP, 2, DC, LR).transpose(0, 2, 1, 3)
    gu = f["L1_ffn_gate_up_proj"].reshape(EP, 2, 2, EI, D)
    shared = np.zeros((1, 2, 2, EI, D), gu.dtype)
    shared[0, 0, 0], shared[0, 0, 1] = f["L1_ffn_shared_gate_w"], f["L1_ffn_shared_up_w"]
    gu = np.concatenate([shared, gu], 0).transpose(0, 4, 2, 1, 3).reshape(EP + 1, KD, P, 2, P)
    gu = gu.transpose(0, 2, 1, 3, 4)
    dn = f["L1_ffn_down_proj"].reshape(EP, 2, D, EI)
    sdn = np.zeros((1, 2, D, EI), dn.dtype)
    sdn[0, 0] = f["L1_ffn_shared_down_w"]
    dn = np.concatenate([sdn, dn], 0).transpose(0, 1, 3, 2).reshape(EP + 1, P, D)
    kmaj = lambda w: c(w.T.reshape(-1, P, w.shape[0]).transpose(1, 0, 2))
    return {
        "x": f["x"].reshape(TOK, D), "ctx": f["ctx_512"].reshape(TOK, DC),
        "consts": shape_constants(),
        "params": rows(f["g_xattn"], f["g_ffn"], f["L0_xattn_q_norm_w"], f["L0_xattn_k_norm_w"],
                       f["L0_ffn_b1"], f["L0_ffn_b2"]),
        "woutT": kmaj(f["L0_xattn_w_out"]), "w1T": kmaj(f["L0_ffn_w1"]), "w2T": kmaj(f["L0_ffn_w2"]),
        "wq": c(f["L1_xattn_Wq"].reshape(HP, 2, LK, D).transpose(0, 2, 1, 3)),
        "wkcq": c(f["L1_xattn_w_kc_q"].reshape(HP, 2, LK, LQ).transpose(0, 2, 1, 3)),
        "wqr": c(wqr2), "wkr": c(wkr),
        "wkckv": c(f["L1_xattn_w_kc_kv"].reshape(HP, 2, LK, DC).transpose(0, 2, 1, 3)),
        "woT": c(f["L1_xattn_Wo"].T.reshape(HP, 2, LK, D).transpose(0, 2, 1, 3)),
        "routerT": kmaj(f["L1_ffn_router_w"]),
        "wsg": c(np.broadcast_to(f["L1_ffn_shared_expert_gate_w"].reshape(KD, P).T[:, :, None], (P, KD, P))),
        "experts": c(np.concatenate([gu.reshape(EP + 1, P, EW - D), dn], 2)),
    }


def kernel(**inputs):
    import concourse.bacc as bacc
    from concourse.bass_utils import run_bass_kernel_spmd

    nc = bacc.Bacc("TRN2", target_bir_lowering=False, num_devices=1)
    arrays = laid_out({k: np.asarray(v) for k, v in inputs.items()})
    args = [nc.dram_tensor(k, a.shape, mybir.dt.from_np(a.dtype), kind="ExternalInput").ap()
            for k, a in arrays.items()]
    out = nc.dram_tensor("y", (TOK, D), F32, kind="ExternalOutput").ap()
    flamingo_program(nc, *args, out)
    r = run_bass_kernel_spmd(nc, [arrays], core_ids=[0])
    return r.results[0]["y"].reshape(SEQS, T, D)
```

```python
from contextlib import ExitStack

import numpy as np

import concourse.bass as bass
from concourse import mybir

ALU = mybir.AluOpType
ACT = mybir.ActivationFunctionType
AX = mybir.AxisListType
F32 = mybir.dt.float32
F32R = mybir.dt.float32r
BF16 = mybir.dt.bfloat16

P = 128
SEQS, T, D = 4, 256, 256
TILES = SEQS * T // P
TOK = SEQS * T
DC = 64
KD = D // P
EPS = 1e-5
NEG = -1e30
ROUND = 12582912.0
TINY = 1e-5

QH, HD = 16, 16
GROUPS = 4
CHUNKS = QH * HD // P
HPC = QH // CHUNKS
PAIRS = QH // 2
DIAG = P + HD
HID = 1024
HK = HID // P
LH, LK, LQ, LR = 16, 128, 192, 64
HP = LH // 2
FCH = 2 * LQ // P
QUERY_UNITS = ((), (), (), (0, 1), (2,), (3, 4), (5,), ())
E, EI, TOPK = 64, 64, 8
EP = E // 2
EW = KD * 2 * P + D
TB = 2
BLK = TOK // TB

PARAMS = (("g", 4), ("qw", D), ("kw", DC), ("b1", HID), ("b2", D))
CONSTS = (("ident", P), ("causal", P), ("headmask", HPC), ("expertsel", E),
          ("cos0", 2 * HD), ("sin0", 2 * HD), ("cosk", 2 * DC), ("sink", 2 * DC),
          ("cosq", FCH * T), ("sinq", FCH * T))


def offsets(table):
    at, out = 0, {}
    for name, w in table:
        out[name] = (at, w)
        at += w
    return out, at


def shape_constants():
    f32 = np.float32
    tabs, width = offsets(CONSTS)
    c = np.zeros((P, width), f32)

    def put(name, a):
        at, w = tabs[name]
        c[:, at:at + w] = np.asarray(a, f32).reshape(P, w)

    p = np.arange(P)
    put("ident", np.eye(P))
    put("causal", np.where(p[None, :] <= p[:, None], 0.0, NEG))
    put("headmask", (p[:, None] // HD == np.arange(HPC)[None, :]))
    put("expertsel", (p[:, None] % E == np.arange(E)[None, :]))
    t = np.arange(T, dtype=f32)

    def angles(dim):
        inv = (f32(1.0) / f32(10000.0) ** (np.arange(0, dim, 2, dtype=f32) / f32(dim))).astype(f32)
        return (t[:, None] * inv[None, :]).astype(f32)

    def by_tile(a):
        return a.reshape(2, P, -1).transpose(1, 0, 2)

    def signed(s):
        h = s.shape[-1] // 2
        return np.concatenate([-s[:, :h], s[:, h:]], -1)

    a0 = np.concatenate([angles(HD)] * 2, -1)
    put("cos0", by_tile(np.cos(a0)))
    put("sin0", by_tile(signed(np.sin(a0))))
    ak = np.repeat(angles(DC), 2, -1)
    put("cosk", by_tile(np.cos(ak)))
    put("sink", by_tile(signed(np.sin(ak))))
    aq = np.repeat(angles(LQ), 2, -1)
    cos, sin = np.cos(aq), np.sin(aq)
    cross = np.concatenate([sin[:, LQ // 2:], -sin[:, :LQ // 2]], -1)
    for name, a in (("cosq", cos), ("sinq", cross)):
        put(name, pair_order(np.stack([a.T, a.T])).transpose(1, 0, 2))
    return c


def pair_order(a):
    half = LQ // 2
    lo, hi = (a[:, n * half:(n + 1) * half].reshape((LQ,) + a.shape[2:]) for n in range(2))
    return np.stack([lo[:P], hi[:P], np.concatenate([lo[P:], hi[P:]])])


class OwnSteps:

    def __init__(self, eng, sem, per_round):
        self.eng, self.sem, self.per_round = eng, sem, per_round
        self.base, self.n = 0, 0

    def round(self, r):
        assert self.n in (0, self.per_round), self.n
        self.base, self.n = r * self.per_round, 0

    def __call__(self, ins):
        self.n += 1
        ins.then_inc(self.sem, 1)
        self.eng.wait_ge(self.sem, self.base + self.n)

    def done(self):
        assert self.n == self.per_round, (self.n, self.per_round)


def flamingo_program(nc, x, ctx, consts, params, woutT, w1T, w2T, wq, wkcq, wqr, wkr, wkckv, woT,
                     routerT, wsg, experts, out):
    tabs, CW = offsets(CONSTS)
    pars, PW = offsets(PARAMS)
    with ExitStack() as stack:
        room = [stack]

        def sb(name, shape, dt=F32):
            return room[0].enter_context(nc.sbuf_tensor(name, shape, dt))

        def sem(name):
            return stack.enter_context(nc.semaphore(name))

        pair_bank = [stack.enter_context(nc.psum_tensor(f"pair_bank{i}", [P, 2, 512], F32)) for i in range(4)]
        bank = [pair_bank[i // 2][:, i % 2, :] for i in range(8)]

        x_sb = sb("x_sb", [P, TILES, D])
        ctx_sb = sb("ctx_sb", [P, TILES, DC])
        c_sb = sb("c_sb", [P, CW])
        par = sb("par", [P, PW])
        eps_col = sb("eps_col", [P, 1])
        tg = sb("tg", [P, 4])
        stats = sb("stats", [P, TILES, 6])
        mv = sb("mv", [P, TILES, 2])
        var_eps = sb("var_eps", [P, TILES])
        rstd = sb("rstd", [P, TILES])
        xn = sb("xn", [P, TILES, D])
        ident_bf = sb("ident_bf", [P, P], BF16)
        mask = sb("mask", [P, 3 * P], BF16)

        def const(name):
            at, w = tabs[name]
            return c_sb[:, at:at + w]

        def param(name):
            at, w = pars[name]
            return par[:, at:at + w]

        ident = const("ident")

        kvr = sb("kvr", [P, TILES, 3 * DC])
        kvT = sb("kvT", [P, TOK])
        wq_sb = sb("wq_sb", [P, 2, D])
        wkcq_sb = sb("wkcq_sb", [P, 2, LQ])
        wqr_sb = sb("wqr_sb", [P, FCH, P])
        wkr_sb = sb("wkr_sb", [P, 2, LR])
        wkckv_sb = sb("wkckv_sb", [P, 2, DC])
        woT_sb = sb("woT_sb", [P, 2, D])
        krT = [[sb(f"krT{e}{j}", [P, TOK]) for j in range(2)] for e in range(2)]
        w_mean = sb("w_mean", [P, 2])

        room[0] = ExitStack()
        kvtmp = sb("kvtmp", [P, TILES, DC])
        kn = sb("kn", [P, TILES, DC])
        kr = sb("kr", [P, TILES, DC])
        ktmp = sb("ktmp", [P, TILES, DC])
        rk = sb("rk", [P, 2 * TILES])
        rkr = sb("rkr", [P, 2 * TILES])
        ck0 = sb("ck0", [P, 2, GROUPS, HD])
        sk0 = sb("sk0", [P, 2, GROUPS, HD])
        cq0 = sb("cq0", [P, 2, QH, HD])
        sq0 = sb("sq0", [P, 2, QH, HD])
        qrot = sb("qrot", [P, 2, QH, HD])
        qtmp = sb("qtmp", [P, 2, QH, HD])
        krep = sb("krep", [P, 2, GROUPS, QH // GROUPS, HD])
        qT = [sb(f"qT{c}", [P, T]) for c in range(CHUNKS)]
        kT = [sb(f"kT{c}", [P, T]) for c in range(CHUNKS)]
        kpad = [sb(f"kpad{c}", [P, HPC, T]) for c in range(CHUNKS)]
        vpad = [[sb(f"vpad{c}{kt}", [P, HPC * DIAG]) for kt in range(2)] for c in range(CHUNKS)]
        probs = [sb(f"probs{s}", [P, 2, 3 * P]) for s in range(4)]
        probsT = [[sb(f"probsT{s}{j}", [P, 3 * P]) for j in range(2)] for s in range(2)]
        negmax = [sb(f"negmax{s}", [P, 4]) for s in range(4)]
        psums = [sb(f"psums{s}", [P, 4]) for s in range(4)]
        pinv = [sb(f"pinv{s}", [P, 4]) for s in range(4)]
        oT = [sb(f"oT{c}", [P, T]) for c in range(CHUNKS)]
        wout_sb = sb("wout_sb", [P, KD, D])

        w1_raw = sb("w1_raw", [P, KD * HID])
        w2_raw = sb("w2_raw", [P, HK * D])
        w1q = sb("w1q", [P, KD, HID], BF16)
        w2q = sb("w2q", [P, HK, D], BF16)
        w_abs = sb("w_abs", [P, 2])
        ones = sb("ones", [P, P])
        round_col = sb("round_col", [P, 1])
        w_scale = sb("w_scale", [P, 2])
        amax = sb("amax", [P, TILES])
        ascale = sb("ascale", [P, TILES])
        adeq = sb("adeq", [P, TILES])
        aq = sb("aq", [P, TILES, D], BF16)
        aT = sb("aT", [P, KD, TOK], BF16)
        pre = [sb(f"pre{k}", [P, HID]) for k in range(2)]
        hid_all = sb("hid_all", [P, 2 * HID])
        hid = [hid_all[:, k * HID:(k + 1) * HID] for k in range(2)]
        hrnd = pre
        hq = [sb(f"hq{k}", [P, HID], BF16) for k in range(2)]
        hqT = [sb(f"hqT{k}", [P, HK, P], BF16) for k in range(2)]
        hmax = [sb(f"hmax{k}", [P, 1]) for k in range(2)]
        hinv = [sb(f"hinv{k}", [P, 1]) for k in range(2)]
        hscale = [sb(f"hscale{k}", [P, 1]) for k in range(2)]
        hdeq = [sb(f"hdeq{k}", [P, 1]) for k in range(2)]
        yb = [sb(f"yb{k}", [P, D]) for k in range(2)]

        room[0].close()
        room[0] = stack
        hT = sb("hT", [P, KD, TOK])
        hT_hi = sb("hT_hi", [P, KD, TOK], F32R)
        hT_lo = sb("hT_lo", [P, KD, TOK], F32R)
        router_sb = sb("router_sb", [P, KD, E])
        wsg_sb = sb("wsg_sb", [P, KD, P])
        zeros_bf = sb("zeros_bf", [P, BLK], BF16)
        e_raw = [sb(f"e_raw{k}", [P, EW]) for k in range(2)]
        room[0] = ExitStack()
        gq = sb("gq", [P, KD, FCH, P])
        gq_hi = sb("gq_hi", [P, KD, FCH, P], F32R)
        gq_lo = sb("gq_lo", [P, KD, FCH, P], F32R)
        own_cos = [sb(f"own_cos{n}", [P, FCH, BLK]) for n in range(TB)]
        partner_sin = [sb(f"partner_sin{n}", [P, FCH, BLK]) for n in range(TB)]
        qrT = [sb(f"qrT{e}", [P, TOK]) for e in range(2)]
        lprobs = [sb(f"lprobs{k}", [P, 2, T]) for k in range(4)]
        lprobsT = [sb(f"lprobsT{k}", [P, 2, T]) for k in range(2)]
        lneg = [sb(f"lneg{k}", [P, 2]) for k in range(4)]
        lsum = [sb(f"lsum{k}", [P, 2]) for k in range(4)]
        linv = [sb(f"linv{k}", [P, 2]) for k in range(4)]
        ctxT = sb("ctxT", [P, HP * TOK])
        mout = sb("mout", [P, HP * D])

        room[0].close()
        room[0] = stack
        logits = sb("logits", [P, TILES, E])
        rmax = sb("rmax", [P, TILES])
        rexp = sb("rexp", [P, TILES, E])
        top8 = sb("top8", [P, TILES, TOPK])
        chosen = sb("chosen", [P, TILES, E])
        tsum = sb("tsum", [P, TILES])
        tinv = sb("tinv", [P, TILES])
        comb = sb("comb", [P, TILES, E])
        comb2 = sb("comb2", [P, TILES, 2 * E])
        combT = sb("combT", [P, TOK], F32R)
        sel = [sb(f"sel{k}", [P, P], F32R) for k in range(2)]
        e_hi = [sb(f"e_hi{k}", [P, EW], F32R) for k in range(2)]
        e_lo = [sb(f"e_lo{k}", [P, EW], F32R) for k in range(2)]
        silu = [sb(f"silu{k}", [P, BLK]) for k in range(2)]
        sgate = [sb(f"sgate{k}", [P, BLK]) for k in range(2)]
        act_u = sb("act_u", [P, BLK])
        act_w = [sb(f"act_w{k}", [P, BLK]) for k in range(2)]
        act_hi = [sb(f"act_hi{k}", [P, BLK], F32R) for k in range(2)]
        act_lo = [sb(f"act_lo{k}", [P, BLK], F32R) for k in range(2)]

        router_in = sem("router_in")
        e_in = [sem(f"e_in{k}") for k in range(2)]
        d_var, d_root, dve_d, xd_ready = sem("d_var"), sem("d_root"), sem("dve_d"), sem("xd_ready")
        hTd_ready, hTd_sb, hT_split = sem("hTd_ready"), sem("hTd_sb"), sem("hT_split")
        logits_ready, logits_sb, rexp_done, comb_ready = sem("logits_ready"), sem("logits_sb"), sem("rexp_done"), sem("comb_ready")
        combT_ready, combT_sb, dve_r, zeros_ready = sem("combT_ready"), sem("combT_sb"), sem("dve_r"), sem("zeros_ready")
        e_hi_ready, e_lo_ready, sel_ready = sem("e_hi_ready"), sem("e_lo_ready"), sem("sel_ready")
        gate_ready, up_ready, weight_ready = sem("gate_ready"), sem("up_ready"), sem("weight_ready")
        silu_done, sgate_done, up_used, act_ready = sem("silu_done"), sem("sgate_done"), sem("up_used"), sem("act_ready")
        act_hi_ready, act_lo_ready, down_done = sem("act_hi_ready"), sem("act_lo_ready"), sem("down_done")
        acc_sb, y_turned, x4_done = sem("acc_sb"), sem("y_turned"), sem("x4_done")
        wq_in, wkcq_in, wqr_in = sem("wq_in"), sem("wkcq_in"), sem("wqr_in")
        wkr_in, wkckv_in, woT_in = sem("wkr_in"), sem("wkckv_in"), sem("woT_in")
        kv_own, kvr_ready, kvT_ready, kvT_sb = sem("kv_own"), sem("kvr_ready"), sem("kvT_ready"), sem("kvT_sb")
        c_var, c_root, dve_c, xn_ready = sem("c_var"), sem("c_root"), sem("dve_c"), sem("xn_ready")
        hT_ready, hT_sb = sem("hT_ready"), sem("hT_sb")
        gq_ready, gq_sb = sem("gq_ready"), sem("gq_sb")
        mout_ready, mout_sb = sem("mout_ready"), sem("mout_sb")
        kr_done, krT_sb = sem("kr_done"), sem("krT_sb")
        gq_hi_ready, gq_lo_ready = sem("gq_hi_ready"), sem("gq_lo_ready")
        hTc_split = sem("hTc_split")
        lq_ready, lq_turned, roped = sem("lq_ready"), sem("lq_turned"), sem("roped")
        qr_done, qrT_sb = sem("qr_done"), sem("qrT_sb")
        ls_ready, lneg_ready, lexp_done, lprobs_ready = sem("ls_ready"), sem("lneg_ready"), sem("lexp_done"), sem("lprobs_ready")
        lpT_ready, lpT_sb, lpv_done, ctxT_sb = sem("lpT_ready"), sem("lpT_sb"), sem("lpv_done"), sem("ctxT_sb")
        dve_l, lpv_half = sem("dve_l"), sem("lpv_half")
        x3_ready, x3_done = sem("x3_ready"), sem("x3_done")
        b_stats, c_stats = sem("b_stats"), sem("c_stats")
        w1_in, w2_in = sem("w1_in"), sem("w2_in")
        w_abs_ready = sem("w_abs_ready")
        w_sum_ready = sem("w_sum_ready")
        w_scale_ready = sem("w_scale_ready")
        pool_w = sem("pool_w")
        wq_ready = sem("wq_ready")
        b_var, b_root = sem("b_var"), sem("b_root")
        dve_b = sem("dve_b")
        aq_ready = sem("aq_ready")
        aT_ready = sem("aT_ready")
        aT_sb = sem("aT_sb")
        h1_ready, pre_ready, gelu_done, hscale_ready = sem("h1_ready"), sem("pre_ready"), sem("gelu_done"), sem("hscale_ready")
        hrnd_ready, hq_ready, hqT_ready, hqT_sb = sem("hrnd_ready"), sem("hq_ready"), sem("hqT_ready"), sem("hqT_sb")
        y_ready, x2_done = sem("y_ready"), sem("x2_done")
        dve_h, yb_ready = sem("dve_h"), sem("yb_ready")
        x_in, c_in, par_in, ctx_in = sem("x_in"), sem("c_in"), sem("par_in"), sem("ctx_in")
        wout_in = sem("wout_in")
        stored = sem("stored")
        consts_made = sem("consts_made")
        dve_setup = sem("dve_setup")
        pool_setup = sem("pool_setup")
        gains = sem("gains")
        a_var = sem("a_var")
        a_root = sem("a_root")
        kr_ready = sem("kr_ready")
        qrot_ready = sem("qrot_ready")
        krep_ready = sem("krep_ready")
        qkT_ready = sem("qkT_ready")
        qkT_sb = sem("qkT_sb")
        kpad_ready = sem("kpad_ready")
        vpad_ready = sem("vpad_ready")
        scores_ready = sem("scores_ready")
        negmax_ready = sem("negmax_ready")
        exp_done = sem("exp_done")
        probs_ready = sem("probs_ready")
        pT_ready = sem("pT_ready")
        pT_sb_dve = sem("pT_sb_dve")
        pT_sb_act = sem("pT_sb_act")
        pv_done = sem("pv_done")
        oT_ready = sem("oT_ready")
        wout_done = sem("wout_done")
        x1_done = sem("x1_done")
        dve_a = sem("dve_a")
        dve_q = sem("dve_q")
        dve_soft = sem("dve_soft")

        block = stack.enter_context(nc.Block())

        @block.sync
        def _(sp):
            sp.dma_start(x_sb[:], x.rearrange("(i p) d -> p i d", p=P)).then_inc(x_in, 16)
            sp.dma_start(ctx_sb[:], ctx.rearrange("(i p) d -> p i d", p=P)).then_inc(ctx_in, 16)
            sp.dma_start(par[:], params).then_inc(par_in, 16)
            sp.dma_start(c_sb[:], consts).then_inc(c_in, 16)
            sp.dma_start(w1_raw[:], w1T.rearrange("p k n -> p (k n)")).then_inc(w1_in, 16)
            sp.dma_start(w2_raw[:], w2T.rearrange("p k n -> p (k n)")).then_inc(w2_in, 16)
            sp.dma_start(wout_sb[:], woutT).then_inc(wout_in, 16)
            def latent_weights(hp, first):
                def load(dst, src, arrived, used, count):
                    if not first:
                        sp.wait_ge(used, hp * count)
                    a = src[bass.ds(hp, 1)].rearrange("o p a b -> p (o a) b")
                    sp.dma_start(dst[:], a).then_inc(arrived, 16)

                load(wq_sb, wq, wq_in, gq_ready, 1)
                load(wkcq_sb, wkcq, wkcq_in, gq_ready, 1)
                load(wkckv_sb, wkckv, wkckv_in, mout_ready, 1)
                load(woT_sb, woT, woT_in, mout_ready, 1)
                if not first:
                    sp.wait_ge(kr_done, TB * hp)
                sp.dma_start(wkr_sb[0:DC], wkr[bass.ds(hp, 1)].rearrange("o p a b -> p (o a) b")).then_inc(wkr_in, 16)
                if not first:
                    sp.wait_ge(qr_done, TB * hp)
                sp.dma_start(wqr_sb[:], wqr[bass.ds(hp, 1)].rearrange("o p c r -> p (o c) r")).then_inc(wqr_in, 16)

            latent_weights(0, True)
            with sp.Fori(1, HP) as hp:
                latent_weights(hp, False)
            sp.wait_ge(x2_done, TILES)
            sp.dma_start(router_sb[:], routerT).then_inc(router_in, 16)
            sp.dma_start(wsg_sb[:], wsg).then_inc(router_in, 16)
            for n in range(2):
                sp.dma_start(e_raw[n][:], experts[n]).then_inc(e_in[n], 16)
            with sp.Fori(0, EP // 2 - 1) as i:
                for k in range(2):
                    n = 2 * i + 2 + k
                    sp.wait_ge(e_lo_ready, n - 1)
                    sp.dma_start(e_raw[k][:], experts[bass.ds(n, 1)].rearrange("o p w -> p (o w)")).then_inc(e_in[k], 16)
            sp.wait_ge(e_lo_ready, EP - 1)
            sp.dma_start(e_raw[0][:], experts[EP]).then_inc(e_in[0], 16)
            for b in range(SEQS):
                sp.wait_ge(x4_done, b + 1)
                rows = out[b * T:(b + 1) * T, :].rearrange("(i p) d -> p i d", p=P)
                sp.dma_start(rows, x_sb[:, 2 * b:2 * b + 2, :]).then_inc(stored, 16)
            sp.wait_ge(stored, 16 * SEQS)
        def attention_a_pool(g):
            vflat = [[vpad[c][kt][:].rearrange("p (h e) -> p h e", e=DIAG) for kt in range(2)]
                     for c in range(CHUNKS)]
            for c in range(CHUNKS):
                for kt in range(2):
                    nc.gpsimd.memset(vpad[c][kt][:], 0.0).then_inc(pool_setup, 1)
            nc.gpsimd.memset(round_col[:], ROUND).then_inc(pool_setup, 1)
            g.wait_ge(pool_setup, 2 * CHUNKS + 1)
            g.wait_ge(c_in, 16)

            def repeat_keys(b):
                g.wait_ge(kr_ready, 1)
                if isinstance(b, int) and b == 0:
                    pass
                else:
                    g.wait_ge(qkT_ready, CHUNKS * b)
                for i in range(2):
                    src = kr[:, bass.ds(2 * b + i, 1), :].rearrange("p o (g d) -> p (o g) d", d=HD)
                    last = nc.gpsimd.tensor_copy(
                        krep[:, i], src.unsqueeze(2).broadcast_to([P, GROUPS, QH // GROUPS, HD]))
                last.then_inc(krep_ready, 1)

            def pads(b, c, first):
                g.wait_ge(qkT_sb, CHUNKS * b + c + 1)
                if not first:
                    g.wait_ge(scores_ready, PAIRS * (b - 1) + 4 * (c + 1))
                nc.gpsimd.tensor_tensor(
                    kpad[c][:], kT[c][:].unsqueeze(1).broadcast_to([P, HPC, T]),
                    const("headmask").unsqueeze(2).broadcast_to([P, HPC, T]), ALU.mult).then_inc(kpad_ready, 1)
                if first:
                    g.wait_ge(ctx_in, 16)
                else:
                    g.wait_ge(pv_done, PAIRS * (b - 1) + 4 * (c + 1))
                for kt in range(2):
                    src = ctx_sb[:, bass.ds(2 * b + kt, 1), 2 * c * HD:2 * (c + 1) * HD]
                    src = src.rearrange("p o (g d) -> p (o g) d", d=HD).unsqueeze(2).broadcast_to([P, 2, 4, HD])
                    dst = vflat[c][kt].rearrange("p (g n) e -> p g n e", g=2)[:, :, :, 0:HD]
                    last = nc.gpsimd.tensor_copy(dst, src)
                last.then_inc(vpad_ready, 1)

            def ternary_weights():
                g.wait_ge(w_scale_ready, 1)
                own = OwnSteps(g, pool_w, 4)
                for n, (w, q) in enumerate(((w1_raw, w1q), (w2_raw, w2q))):
                    own(nc.gpsimd.tensor_scalar(w[:], w[:], w_scale[:, n:n + 1], ROUND, ALU.mult, ALU.add))
                    own(nc.gpsimd.tensor_scalar(w[:], w[:], ROUND + 1, ROUND - 1, ALU.min, ALU.max))
                    nc.gpsimd.tensor_scalar(q[:].rearrange("p k n -> p (k n)"), w[:], -ROUND, 1.0,
                                            ALU.add, ALU.mult).then_inc(wq_ready, 1)

            repeat_keys(0)
            for c in range(CHUNKS):
                pads(0, c, True)
            ternary_weights()
            latent_kv_pool(g)
            with g.Fori(0, SEQS - 1) as b:
                repeat_keys(b + 1)
                for c in range(CHUNKS):
                    pads(b + 1, c, False)

        def latent_kv_pool(g):
            own = OwnSteps(g, kv_own, 4)
            own(nc.gpsimd.memset(kvr[:], 0.0))
            nc.gpsimd.memset(wkr_sb[DC:P], 0.0).then_inc(kvr_ready, 1)
            g.wait_ge(kvr_ready, 1)
            nc.gpsimd.memset(kvT[DC:P], 0.0).then_inc(kvr_ready, 1)
            g.wait_ge(kvr_ready, 2)
            for e in range(2):
                for j, rows in enumerate((slice(LR, P), slice(0, LR))):
                    nc.gpsimd.memset(krT[e][j][rows], 0.0).then_inc(kvr_ready, 1)
                    g.wait_ge(kvr_ready, 3 + 2 * e + j)
            g.wait_ge(kvr_ready, 6)
            half = DC // 2
            cos = const("cosk").rearrange("p (i d) -> p i d", d=DC).unsqueeze(1).broadcast_to([P, SEQS, 2, DC])
            sin = const("sink").rearrange("p (i d) -> p i d", d=DC)
            c4 = ctx_sb[:].rearrange("p (b i) d -> p b i d", i=2)
            t4 = kvtmp[:].rearrange("p (b i) d -> p b i d", i=2)
            for lo, other in ((0, half), (half, 0)):
                own(nc.gpsimd.tensor_tensor(t4[:, :, :, lo:lo + half], c4[:, :, :, other:other + half],
                                            sin[:, :, lo:lo + half].unsqueeze(1).broadcast_to([P, SEQS, 2, half]), ALU.mult))
            mid = kvr[:].rearrange("p (b i) e -> p b i e", i=2)[:, :, :, DC:2 * DC]
            own(nc.gpsimd.tensor_tensor(mid, c4, cos, ALU.mult))
            nc.gpsimd.tensor_tensor(mid, mid, t4, ALU.add).then_inc(kvr_ready, 1)

        def latent_pool(g):
            def low_gq(p):
                g.wait_ge(gq_hi_ready, p + 1)
                nc.gpsimd.tensor_tensor(gq_lo[:], gq[:], gq_hi[:].bitcast(F32), ALU.subtract).then_inc(gq_lo_ready, 1)

            def rope(p, n):
                for part, after in ((slice(0, 2), 2), (slice(2, 3), 3)):
                    g.wait_ge(lq_turned, 6 * p + 3 * n + after)
                    nc.gpsimd.tensor_tensor(own_cos[n][:, part], own_cos[n][:, part], partner_sin[n][:, part],
                                            ALU.add).then_inc(roped, 1)

            low_gq(0)
            rope(0, 0)
            rope(0, 1)
            with g.Fori(1, HP) as p:
                low_gq(p)
                rope(p, 0)
                rope(p, 1)

        def experts_pool(g):
            def low_weights(n, k):
                g.wait_ge(e_hi_ready, n + 1)
                nc.gpsimd.tensor_tensor(e_lo[k][:], e_raw[k][:], e_hi[k][:].bitcast(F32), ALU.subtract).then_inc(e_lo_ready, 1)

            def low_act(t, k):
                if not (isinstance(t, int) and t < 2):
                    g.wait_ge(down_done, t - 1)
                g.wait_ge(act_hi_ready, t + 1)
                nc.gpsimd.tensor_tensor(act_lo[k][:], act_w[k][:], act_hi[k][:].bitcast(F32), ALU.subtract).then_inc(act_lo_ready, 1)

            g.wait_ge(x2_done, TILES)
            nc.gpsimd.memset(zeros_bf[:], 0.0).then_inc(zeros_ready, 1)
            low_weights(0, 0)
            low_act(0, 0)
            low_weights(1, 1)
            low_act(1, 1)
            with g.Fori(0, EP // 2 - 1) as i:
                for k in range(2):
                    n = 2 * i + 1 + k
                    low_act(2 * n, 0)
                    low_weights(n + 1, k)
                    low_act(2 * n + 1, 1)
            low_act(2 * EP - 2, 0)
            low_weights(EP, 0)
            low_act(2 * EP - 1, 1)
            low_act(2 * EP, 0)
            low_act(2 * EP + 1, 1)

        def mlp_pool(g):
            def quantise(t, k):
                g.wait_ge(hrnd_ready, t + 1)
                if not (isinstance(t, int) and t < 2):
                    g.wait_ge(hqT_ready, t - 1)
                nc.gpsimd.tensor_tensor(hq[k][:], hrnd[k][:], round_col[:].broadcast_to([P, HID]),
                                        ALU.subtract).then_inc(hq_ready, 1)

            quantise(0, 0)
            quantise(1, 1)
            with g.Fori(1, SEQS) as b:
                for k in range(2):
                    quantise(2 * b + k, k)

        @block.gpsimd
        def _(g):
            attention_a_pool(g)
            mlp_pool(g)
            latent_pool(g)
            experts_pool(g)

        def attention_a_act(act):
            def evacuate_qk(b, c, first):
                act.wait_ge(qkT_ready, CHUNKS * b + c + 1)
                if not first:
                    act.wait_ge(scores_ready, PAIRS * (b - 1) + 4 * (c + 1))
                    act.wait_ge(kpad_ready, CHUNKS * (b - 1) + c + 1)
                nc.scalar.copy(qT[c][:], bank[6][:, 0:T])
                nc.scalar.copy(kT[c][:], bank[6][:, T:2 * T]).then_inc(qkT_sb, 1)

            def exps(b, s, early):
                act.wait_ge(negmax_ready, PAIRS * b + s + 1)
                if not early:
                    act.wait_ge(pT_ready, 2 * (PAIRS * b + s - 3))
                for j in range(2):
                    for k, lo, hi in ((j, P, 3 * P), (2 + j, 0, P)):
                        last = nc.scalar.activation(probs[s % 4][:, j, lo:hi], pair_bank[s % 2][:, j, lo:hi], ACT.Exp,
                                                    bias=negmax[s % 4][:, k:k + 1], accum_out=psums[s % 4][:, k:k + 1])
                last.then_inc(exp_done, 1)

            def evacuate_pT(b, s, early):
                act.wait_ge(pT_ready, 2 * (PAIRS * b + s) + 2)
                if not early:
                    act.wait_ge(pv_done, PAIRS * b + s - 1)
                nc.scalar.copy(probsT[s % 2][1][:], bank[5][:, 0:3 * P]).then_inc(pT_sb_act, 1)

            def evacuate_oT(b, c, first):
                act.wait_ge(pv_done, PAIRS * b + 4 * (c + 1))
                if not first:
                    act.wait_ge(wout_done, b)
                nc.scalar.copy(oT[c][:], bank[6 + c][:, 0:T]).then_inc(oT_ready, 1)

            def sequence(b, first, last):
                for s in range(PAIRS):
                    if s == 7:
                        evacuate_oT(b, 0, first)
                    exps(b, s, first and s < 4)
                    if s >= 2:
                        evacuate_pT(b, s - 2, first and s - 2 < 2)
                    if s == 7 and not last:
                        evacuate_qk(b + 1, 0, False)
                for s in (PAIRS - 2, PAIRS - 1):
                    evacuate_pT(b, s, False)
                if not last:
                    evacuate_qk(b + 1, 1, False)
                evacuate_oT(b, 1, first)

            act.wait_ge(par_in, 16)
            nc.scalar.activation(tg[:], param("g"), ACT.Tanh).then_inc(gains, 1)
            act.wait_ge(a_var, 1)
            nc.scalar.activation(rk[:], rkr[:], ACT.Sqrt).then_inc(a_root, 1)
            for n, (w, arrived) in enumerate(((w1_raw, w1_in), (w2_raw, w2_in))):
                act.wait_ge(arrived, 16)
                if n:
                    act.wait_ge(w_abs_ready, n)
                nc.scalar.activation(hid_all[:], w[:], ACT.Abs, accum_out=w_abs[:, n:n + 1]).then_inc(w_abs_ready, 1)
            evacuate_qk(0, 0, True)
            evacuate_qk(0, 1, True)
            sequence(0, True, False)
            with act.Fori(1, SEQS - 1) as b:
                sequence(b, False, False)
            sequence(SEQS - 1, False, True)

        def mlp_act(act):
            act.wait_ge(b_var, 1)
            nc.scalar.activation(rstd[:], var_eps[:], ACT.Sqrt).then_inc(b_root, 1)
            for n in range(2):
                act.wait_ge(aT_ready, n + 1)
                src = bank[6 + n].bitcast(BF16).rearrange("p (k t) -> p k t", k=KD)
                nc.scalar.copy(aT[:, :, n * BLK:(n + 1) * BLK], src).then_inc(aT_sb, 1)

            def gelu(t, k):
                act.wait_ge(pre_ready, t + 1)
                nc.scalar.activation(hid[k], pre[k][:], ACT.Gelu).then_inc(gelu_done, 1)

            def scale_and_round(t, k):
                act.wait_ge(hscale_ready, t + 1)
                nc.scalar.activation(hrnd[k][:], hid[k], ACT.Copy, bias=ROUND,
                                     scale=hscale[k][:, 0:1]).then_inc(hrnd_ready, 1)

            def evacuate(t, k):
                act.wait_ge(hqT_ready, t + 1)
                if not (isinstance(t, int) and t < 2):
                    act.wait_ge(y_ready, t - 1)
                nc.scalar.copy(hqT[k][:], bank[4].bitcast(BF16).rearrange("p (c t) -> p c t", c=HK)).then_inc(hqT_sb, 1)

            gelu(0, 0)
            scale_and_round(0, 0)
            gelu(1, 1)
            evacuate(0, 0)
            with act.Fori(1, SEQS) as b:
                for k in range(2):
                    t = 2 * b + k
                    scale_and_round(t - 1, 1 - k)
                    gelu(t, k)
                    evacuate(t - 1, 1 - k)
            scale_and_round(TILES - 1, 1)
            evacuate(TILES - 1, 1)

        def experts_act(act):
            def high_weights(n, k, first):
                if not first:
                    act.wait_ge(down_done, 2 * n - 2)
                nc.scalar.copy(e_hi[k][:], e_raw[k][:]).then_inc(e_hi_ready, 1)

            def select(n, k):
                src = const("expertsel")[:, bass.ds(2 * (n - 1), 2)].unsqueeze(2).broadcast_to([P, 2, EI])
                nc.scalar.copy(sel[k][:].rearrange("p (e i) -> p e i", e=2), src).then_inc(sel_ready, 1)

            def gate(t, k):
                act.wait_ge(gate_ready, t + 1)
                if not (isinstance(t, int) and t < 2):
                    act.wait_ge(up_used, t - 1)
                nc.scalar.activation(silu[k][:], bank[(4, 7)[k]], ACT.Silu).then_inc(silu_done, 1)

            act.wait_ge(d_var, 1)
            nc.scalar.activation(rstd[:], var_eps[:], ACT.Sqrt).then_inc(d_root, 1)
            for n in range(KD * TB):
                act.wait_ge(hTd_ready, n + 1)
                nc.scalar.copy(hT[:, n // 2, (n % 2) * BLK:(n % 2 + 1) * BLK], bank[4 + n]).then_inc(hTd_sb, 1)
            for n in range(2):
                act.wait_ge(e_in[n], 16)
                high_weights(n, n, True)
            select(1, 1)
            act.wait_ge(logits_sb, 1)
            nc.scalar.activation(rexp[:], logits[:], ACT.Exp).then_inc(rexp_done, 1)
            for t in range(2):
                act.wait_ge(weight_ready, t + 1)
                nc.scalar.activation(sgate[t][:], bank[6], ACT.Sigmoid).then_inc(sgate_done, 1)
            for t in range(2):
                gate(t, t)
            for n in range(TB):
                act.wait_ge(combT_ready, n + 1)
                nc.scalar.copy(combT[:, n * BLK:(n + 1) * BLK], bank[n]).then_inc(combT_sb, 1)
            with act.Fori(0, EP // 2 - 1) as i:
                for k in range(2):
                    n = 2 * i + 1 + k
                    gate(2 * n, 0)
                    act.wait_ge(e_in[k], 16 * i + 32)
                    high_weights(n + 1, k, False)
                    select(n + 1, k)
                    gate(2 * n + 1, 1)
            gate(2 * EP - 2, 0)
            act.wait_ge(e_in[0], 16 * (EP // 2 + 1))
            high_weights(EP, 0, False)
            select(EP, 0)
            gate(2 * EP - 1, 1)
            gate(2 * EP, 0)
            gate(2 * EP + 1, 1)
            act.wait_ge(down_done, 2 * EP + 2)
            for n in range(KD * TB):
                nc.scalar.activation(hT[:, n // 2, (n % 2) * BLK:(n % 2 + 1) * BLK], bank[n], ACT.Copy,
                                     scale=tg[:, 3:4]).then_inc(acc_sb, 1)

        def latent_act(act):
            act.wait_ge(c_var, 1)
            nc.scalar.activation(rstd[:], var_eps[:], ACT.Sqrt).then_inc(c_root, 1)
            act.wait_ge(kvT_ready, 1)
            nc.scalar.copy(kvT[0:DC, 0:BLK], bank[0][0:DC, :])
            nc.scalar.copy(kvT[0:DC, BLK:TOK], bank[1][0:DC, :]).then_inc(kvT_sb, 1)
            for n in range(KD * TB):
                act.wait_ge(hT_ready, n + 1)
                nc.scalar.copy(hT[:, n // 2, (n % 2) * BLK:(n % 2 + 1) * BLK], bank[4 + n]).then_inc(hT_sb, 1)

            def evacuate_gq(p):
                act.wait_ge(gq_ready, p + 1)
                half = LQ // 2
                cut = P - half
                for dk in range(KD):
                    src = bank[6 + dk][:, 0:2 * LQ].rearrange("p (j s e) -> p j s e", j=2, s=2)
                    nc.scalar.copy(gq[:, dk, 0:2, 0:half], src[:, 0])
                    nc.scalar.copy(gq[:, dk, 0:2, half:P], src[:, 1, :, 0:cut])
                    last = nc.scalar.copy(gq[:, dk, 2, :].rearrange("p (s e) -> p s e", s=2), src[:, 1, :, cut:half])
                last.then_inc(gq_sb, 1)
                act.wait_ge(gq_sb, p + 1)
                nc.scalar.copy(gq_hi[:], gq[:]).then_inc(gq_hi_ready, 1)

            def evacuate_mout(p):
                act.wait_ge(mout_ready, p + 1)
                nc.scalar.copy(mout[:, bass.ds(p * D, D)], bank[5][:, 0:D]).then_inc(mout_sb, 1)

            def evacuate_keys(p, e, first):
                act.wait_ge(kr_done, TB * (p + 1))
                if not first:
                    act.wait_ge(ls_ready, 2 * SEQS * (p - 1))
                for n in range(TB):
                    for j in range(2):
                        rows = slice(j * LR, (j + 1) * LR)
                        last = nc.scalar.copy(krT[e][j][rows, n * BLK:(n + 1) * BLK], bank[6 + n][rows, :])
                last.then_inc(krT_sb, 1)

            def evacuate_queries(p, n, e):
                act.wait_ge(qr_done, TB * p + n + 1)
                nc.scalar.copy(qrT[e][:, n * BLK:(n + 1) * BLK], bank[5]).then_inc(qrT_sb, 1)

            def exps(hp, u, early):
                n = 2 * SEQS * hp + u
                act.wait_ge(lneg_ready, n + 1)
                if not early:
                    act.wait_ge(lpT_ready, n - 3)
                for i in range(2):
                    last = nc.scalar.activation(lprobs[u % 4][:, i, :], bank[u % 2][:, i * T:(i + 1) * T], ACT.Exp,
                                                bias=lneg[u % 4][:, i:i + 1], accum_out=lsum[u % 4][:, i:i + 1])
                last.then_inc(lexp_done, 1)

            def evacuate_ctx(hp, b):
                act.wait_ge(lpv_done, SEQS * hp + b + 1)
                nc.scalar.copy(ctxT[:, bass.ds(hp * TOK + b * T, T)], bank[4][:, 0:T]).then_inc(ctxT_sb, 1)

            def pair(hp, e, first, last):
                for u in range(2 * SEQS):
                    if u == 5 or u == 7:
                        evacuate_ctx(hp, (u - 5) // 2)
                    exps(hp, u, first and u < 4)
                    if u == 0 and not last:
                        evacuate_gq(hp + 1)
                    if u == 1 and not last:
                        evacuate_keys(hp + 1, 1 - e, first)
                    if u == 2 and not last:
                        evacuate_mout(hp + 1)
                    if u == 7 and not last:
                        evacuate_queries(hp + 1, 0, 1 - e)
                evacuate_ctx(hp, 2)
                if not last:
                    evacuate_queries(hp + 1, 1, 1 - e)
                evacuate_ctx(hp, 3)

            evacuate_gq(0)
            evacuate_mout(0)
            evacuate_keys(0, 0, True)
            evacuate_queries(0, 0, 0)
            evacuate_queries(0, 1, 0)
            pair(0, 0, True, False)
            pair(1, 1, False, False)
            with act.Fori(1, HP // 2 - 1) as i:
                for e in range(2):
                    pair(2 * i + e, e, False, False)
            pair(HP - 2, 0, False, False)
            pair(HP - 1, 1, False, True)

        @block.scalar
        def _(act):
            attention_a_act(act)
            mlp_act(act)
            latent_act(act)
            experts_act(act)

        def attention_a_pe(pe):
            def transposes(b, c, first):
                if not first:
                    pe.wait_ge(oT_ready, CHUNKS * (b - 1) + 1)
                pe.wait_ge(qrot_ready, b + 1)
                pe.wait_ge(krep_ready, b + 1)
                if not (first and c == 0):
                    pe.wait_ge(qkT_sb, CHUNKS * b + c)
                for i in range(2):
                    q_in = qrot[:, i, c * HPC:(c + 1) * HPC, :]
                    nc.tensor.transpose(bank[6][:, i * P:(i + 1) * P], q_in, ident)
                for i in range(2):
                    k_in = krep[:, i, 2 * c:2 * c + 2]
                    last = nc.tensor.transpose(bank[6][:, T + i * P:T + (i + 1) * P], k_in, ident)
                last.then_inc(qkT_ready, 1)

            def scores(b, s, early):
                c, h = s // 4, 2 * (s % 4)
                if s % 4 == 0:
                    pe.wait_ge(qkT_sb, CHUNKS * b + c + 1)
                    pe.wait_ge(kpad_ready, CHUNKS * b + c + 1)
                if not early:
                    pe.wait_ge(exp_done, PAIRS * b + s - 1)
                for j in range(2):
                    dst = pair_bank[s % 2][:, j]
                    nc.tensor.matmul(dst[:, 0:3 * P], ident_bf[:], mask[:], start=True, stop=False)
                    nc.tensor.matmul(dst[:, 0:P], qT[c][:, 0:P], kpad[c][:, h + j, 0:P], start=False, stop=False)
                    last = nc.tensor.matmul(dst[:, P:3 * P], qT[c][:, P:2 * P], kpad[c][:, h + j, :],
                                            start=False, stop=True)
                last.then_inc(scores_ready, 1)

            def turn_probs(b, s, first):
                pe.wait_ge(probs_ready, PAIRS * b + s + 1)
                for j in range(2):
                    if not (first and s == 0):
                        pe.wait_ge((pT_sb_dve, pT_sb_act)[j], PAIRS * b + s)
                    dst, src = bank[4 + j], probs[s % 4][:, j]
                    nc.tensor.transpose(dst[:, 0:P], src[:, 0:P], ident)
                    nc.tensor.transpose(dst[:, P:2 * P], src[:, P:2 * P], ident)
                    nc.tensor.transpose(dst[:, 2 * P:3 * P], src[:, 2 * P:3 * P], ident).then_inc(pT_ready, 1)

            def values(b, s, first):
                c = s // 4
                if s % 4 == 0:
                    pe.wait_ge(vpad_ready, CHUNKS * b + c + 1)
                    if c == 1 and first:
                        pe.wait_ge(w_scale_ready, 1)
                    if c == 1 and not first:
                        pe.wait_ge(x1_done, b)
                    if c == 0:
                        pe.wait_ge(qkT_sb, CHUNKS * (b + 1))
                pe.wait_ge(pT_sb_dve, PAIRS * b + s + 1)
                pe.wait_ge(pT_sb_act, PAIRS * b + s + 1)
                for j in range(2):
                    h = 2 * (s % 4) + j
                    cols = slice(h * P, (h + 1) * P)
                    nc.tensor.matmul(bank[6 + c][:, 0:T], vpad[c][0][:, cols], probsT[s % 2][j][:, 0:T],
                                     start=(h == 0), stop=False, skip_group_check=True)
                    last = nc.tensor.matmul(bank[6 + c][:, P:T], vpad[c][1][:, cols],
                                            probsT[s % 2][j][:, T:T + P],
                                            start=False, stop=(h == HPC - 1), skip_group_check=True)
                last.then_inc(pv_done, 1)

            def project(b, first):
                pe.wait_ge(oT_ready, CHUNKS * (b + 1))
                if first:
                    pe.wait_ge(wout_in, 16)
                for i in range(2):
                    for c in range(CHUNKS):
                        last = nc.tensor.matmul(bank[7][:, i * D:(i + 1) * D], oT[c][:, i * P:(i + 1) * P],
                                                wout_sb[:, c, :], start=(c == 0), stop=(c == CHUNKS - 1))
                last.then_inc(wout_done, 1)

            def sequence(b, first, last):
                for s in range(PAIRS):
                    scores(b, s, first and s < 2)
                    if s >= 2:
                        turn_probs(b, s - 2, first)
                    if s >= 3:
                        values(b, s - 3, first)
                    if s == 7 and not last:
                        transposes(b + 1, 0, False)
                turn_probs(b, PAIRS - 2, first)
                values(b, PAIRS - 3, first)
                turn_probs(b, PAIRS - 1, first)
                values(b, PAIRS - 2, first)
                if not last:
                    transposes(b + 1, 1, False)
                values(b, PAIRS - 1, first)
                project(b, first)

            pe.wait_ge(consts_made, 4)
            pe.wait_ge(c_in, 16)
            pe.wait_ge(w_abs_ready, 2)
            nc.tensor.matmul(bank[7][:, 0:2], ones[:], w_abs[:], start=True, stop=True).then_inc(w_sum_ready, 1)
            transposes(0, 0, True)
            transposes(0, 1, True)
            sequence(0, True, False)
            with pe.Fori(1, SEQS - 1) as b:
                sequence(b, False, False)
            sequence(SEQS - 1, False, True)

        def mlp_pe(pe):
            for n in range(2):
                pe.wait_ge(aq_ready, 1)
                dst = bank[6 + n].bitcast(BF16).rearrange("p (k t) -> p k t", k=KD)
                for i in range(4):
                    for k in range(KD):
                        last = nc.tensor.transpose(dst[:, k, i * P:(i + 1) * P],
                                                   aq[:, 4 * n + i, k * P:(k + 1) * P], ident_bf[:])
                last.then_inc(aT_ready, 1)
            pe.wait_ge(aT_sb, 2)
            pe.wait_ge(wq_ready, 2)

            def first(t, k):
                if not (isinstance(t, int) and t < 2):
                    pe.wait_ge(pre_ready, t - 1)
                for half in range(2):
                    for c in range(KD):
                        last = nc.tensor.matmul(pair_bank[k][:, half, :], aT[:, c, bass.ds(t * P, P)],
                                                w1q[:, c, half * 512:(half + 1) * 512],
                                                start=(c == 0), stop=(c == KD - 1))
                last.then_inc(h1_ready, 1)

            def second(t, k):
                pe.wait_ge(hq_ready, t + 1)
                if not (isinstance(t, int) and t == 0):
                    pe.wait_ge(hqT_sb, t)
                for c in range(HK):
                    last = nc.tensor.transpose(bank[4].bitcast(BF16)[:, c * P:(c + 1) * P],
                                               hq[k][:, c * P:(c + 1) * P], ident_bf[:])
                last.then_inc(hqT_ready, 1)
                pe.wait_ge(hqT_sb, t + 1)
                if not (isinstance(t, int) and t < 2):
                    pe.wait_ge(x2_done, t - 1)
                for c in range(HK):
                    last = nc.tensor.matmul(bank[6 + k][:, 0:D], hqT[k][:, c, :], w2q[:, c, :],
                                            start=(c == 0), stop=(c == HK - 1))
                last.then_inc(y_ready, 1)

            first(0, 0)
            first(1, 1)
            second(0, 0)
            with pe.Fori(1, SEQS) as b:
                for k in range(2):
                    first(2 * b + k, k)
                    second(2 * b + k - 1, 1 - k)
            second(TILES - 1, 1)

        def experts_pe(pe):
            pe.wait_ge(xd_ready, 1)
            for n in range(KD * TB):
                k, half = n // 2, n % 2
                for i in range(4):
                    last = nc.tensor.transpose(bank[4 + n][:, i * P:(i + 1) * P],
                                               xn[:, 4 * half + i, k * P:(k + 1) * P], ident)
                last.then_inc(hTd_ready, 1)
            pe.wait_ge(router_in, 32)
            pe.wait_ge(hTd_sb, KD * TB)
            for i in range(TILES):
                for k in range(KD):
                    last = nc.tensor.matmul(bank[7][:, i * E:(i + 1) * E], hT[:, k, i * P:(i + 1) * P], router_sb[:, k, :],
                                            start=(k == 0), stop=(k == KD - 1))
            last.then_inc(logits_ready, 1)

            def split_product(dst, w_cols, moving_hi, moving_lo, ek, start, stop, **kw):
                for n, (w, m) in enumerate(((e_hi, moving_hi), (e_lo, moving_hi), (e_hi, moving_lo))):
                    last = nc.tensor.matmul(dst, w[ek][:, w_cols], m, start=start and n == 0, stop=stop and n == 2, **kw)
                return last

            def gate(n, blk, ek):
                t = 2 * n + blk
                early = isinstance(t, int) and t < 2
                cols = slice(blk * BLK, (blk + 1) * BLK)
                if blk == 0:
                    pe.wait_ge(e_lo_ready, n + 1)
                if not early:
                    pe.wait_ge(silu_done, t - 1)
                gate_bank = bank[(4, 7)[blk]]
                for dk in range(KD):
                    last = split_product(gate_bank, slice(dk * 2 * P, dk * 2 * P + P), hT_hi[:, dk, cols], hT_lo[:, dk, cols],
                                         ek, dk == 0, dk == KD - 1)
                last.then_inc(gate_ready, 1)

            def up(n, blk, ek):
                t = 2 * n + blk
                cols = slice(blk * BLK, (blk + 1) * BLK)
                if not (isinstance(t, int) and t == 0):
                    pe.wait_ge(up_used, t)
                for dk in range(KD):
                    last = split_product(bank[5], slice(dk * 2 * P + P, (dk + 1) * 2 * P), hT_hi[:, dk, cols], hT_lo[:, dk, cols],
                                         ek, dk == 0, dk == KD - 1)
                last.then_inc(up_ready, 1)

            def routed(n, blk, ek):
                t = 2 * n + blk
                if blk == 0:
                    pe.wait_ge(sel_ready, n)
                pe.wait_ge(act_ready, t)
                nc.tensor.matmul(bank[6], sel[ek][:], combT[:, blk * BLK:(blk + 1) * BLK], start=True,
                                 stop=True).then_inc(weight_ready, 1)

            def down(t, blk, ek, stop=False):
                pe.wait_ge(act_hi_ready, t + 1)
                pe.wait_ge(act_lo_ready, t + 1)
                for f in range(KD):
                    last = split_product(bank[2 * f + blk], slice(EW - D + f * P, EW - D + (f + 1) * P), act_hi[blk][:],
                                         act_lo[blk][:], ek, False, stop, skip_group_check=True)
                last.then_inc(down_done, 1)

            pe.wait_ge(hT_split, 1)
            for blk in range(TB):
                if blk == 1:
                    pe.wait_ge(logits_sb, 1)
                gate(0, blk, 0)
                if blk == 1:
                    pe.wait_ge(sgate_done, 1)
                for k in range(KD):
                    last = nc.tensor.matmul(bank[6], wsg_sb[:, k, :], hT[:, k, blk * BLK:(blk + 1) * BLK],
                                            start=(k == 0), stop=(k == KD - 1))
                last.then_inc(weight_ready, 1)
                up(0, blk, 0)
            pe.wait_ge(comb_ready, 1)
            for n in range(TB):
                for i in range(4):
                    last = nc.tensor.transpose(bank[n][:, i * P:(i + 1) * P], comb2[:, 4 * n + i, :], ident)
                last.then_inc(combT_ready, 1)
            pe.wait_ge(zeros_ready, 1)
            pe.wait_ge(combT_sb, TB)
            for n in range(KD * TB):
                nc.tensor.matmul(bank[n], ident_bf[:], zeros_bf[:], start=True, stop=False, skip_group_check=True)
            down(0, 0, 0)
            with pe.Fori(0, EP // 2) as i:
                for k in range(2):
                    n, ek = 2 * i + 1 + k, 1 - k
                    for blk in range(TB):
                        gate(n, blk, ek)
                        up(n, blk, ek)
                        routed(n, blk, ek)
                        down(2 * n + blk - 1, 1 - blk, ek if blk else 1 - ek)
            down(2 * EP + 1, 1, 0, stop=True)
            for b in range(SEQS):
                blk = b // 2
                pe.wait_ge(acc_sb, KD * TB if blk else KD * TB - 1)
                for i in range(2):
                    for f in range(KD):
                        at = (2 * b + i) * P
                        last = nc.tensor.transpose(bank[4 + b][:, i * D + f * P:i * D + (f + 1) * P], hT[:, f, at:at + P], ident)
                last.then_inc(y_turned, 1)

        def latent_pe(pe):
            pe.wait_ge(x2_done, TILES)
            pe.wait_ge(kvr_ready, 7)
            for i in range(TILES):
                last = nc.tensor.transpose(bank[i // 4][0:DC, (i % 4) * P:(i % 4 + 1) * P], kvr[:, i, DC:2 * DC], ident)
            last.then_inc(kvT_ready, 1)
            pe.wait_ge(xn_ready, 1)
            for n in range(KD * TB):
                k, half = n // 2, n % 2
                for i in range(4):
                    last = nc.tensor.transpose(bank[4 + n][:, i * P:(i + 1) * P],
                                               xn[:, 4 * half + i, k * P:(k + 1) * P], ident)
                last.then_inc(hT_ready, 1)
            pe.wait_ge(kvT_sb, 1)

            def fold_queries(p, first):
                pe.wait_ge(wq_in, 16 * p + 16)
                pe.wait_ge(wkcq_in, 16 * p + 16)
                if first:
                    pe.wait_ge(hT_sb, KD * TB)
                else:
                    pe.wait_ge(lq_turned, 6 * p)
                for dk in range(KD):
                    for j in range(2):
                        last = nc.tensor.matmul(bank[6 + dk][:, j * LQ:(j + 1) * LQ], wq_sb[:, j, dk * P:(dk + 1) * P],
                                                wkcq_sb[:, j, :], start=True, stop=True)
                last.then_inc(gq_ready, 1)

            def fold_output(p, first):
                pe.wait_ge(wkckv_in, 16 * p + 16)
                pe.wait_ge(woT_in, 16 * p + 16)
                if not first:
                    pe.wait_ge(qrT_sb, TB * p)
                for j in range(2):
                    last = nc.tensor.matmul(bank[5][j * DC:(j + 1) * DC, 0:D], wkckv_sb[:, j, :], woT_sb[:, j, :],
                                            start=True, stop=True)
                last.then_inc(mout_ready, 1)

            def keys(p):
                pe.wait_ge(wkr_in, 16 * p + 16)
                pe.wait_ge(gq_sb, p + 1)
                for n in range(TB):
                    nc.tensor.matmul(bank[6 + n], wkr_sb[:].rearrange("p j r -> p (j r)"), kvT[:, n * BLK:(n + 1) * BLK],
                                     start=True, stop=True).then_inc(kr_done, 1)

            def queries(p, v):
                n, f = v // FCH, v % FCH
                cols = slice(n * BLK, (n + 1) * BLK)
                if v == 0:
                    pe.wait_ge(gq_lo_ready, p + 1)
                    pe.wait_ge(krT_sb, p + 1)
                if v >= 2:
                    pe.wait_ge(lq_turned, 6 * p + v - 1)
                for dk in range(KD):
                    for m, (w, h) in enumerate(((gq_hi, hT_hi), (gq_lo, hT_hi), (gq_hi, hT_lo))):
                        last = nc.tensor.matmul(bank[6 + v % 2], w[:, dk, f, :], h[:, dk, cols],
                                                start=(dk == 0 and m == 0), stop=(dk == KD - 1 and m == 2))
                last.then_inc(lq_ready, 1)

            def reduced(p, n):
                if n == 0:
                    pe.wait_ge(wqr_in, 16 * p + 16)
                    pe.wait_ge(mout_sb, p + 1)
                else:
                    pe.wait_ge(qrT_sb, TB * p + 1)
                pe.wait_ge(roped, 2 * (TB * p + n + 1))
                for f in range(FCH):
                    last = nc.tensor.matmul(bank[5], wqr_sb[:, f, :], own_cos[n][:, f, :],
                                            start=(f == 0), stop=(f == FCH - 1))
                last.then_inc(qr_done, 1)

            def scores(hp, u, e, early):
                b, j = u // 2, u % 2
                if u == 0:
                    pe.wait_ge(krT_sb, hp + 1)
                if u % SEQS == 0:
                    pe.wait_ge(qrT_sb, TB * hp + u // SEQS + 1)
                if not early:
                    pe.wait_ge(lexp_done, 2 * SEQS * hp + u - 1)
                for i in range(2):
                    last = nc.tensor.matmul(bank[u % 2][:, i * T:(i + 1) * T], qrT[e][:, (2 * b + i) * P:(2 * b + i + 1) * P],
                                            krT[e][j][:, b * T:(b + 1) * T], start=True, stop=True)
                last.then_inc(ls_ready, 1)

            def turn_probs(hp, u, early):
                pe.wait_ge(lprobs_ready, 2 * SEQS * hp + u + 1)
                if not early:
                    pe.wait_ge(lpT_sb, 2 * SEQS * hp + u - 1)
                for kt in range(2):
                    for i in range(2):
                        last = nc.tensor.transpose(bank[2 + u % 2][:, kt * T + i * P:kt * T + (i + 1) * P],
                                                   lprobs[u % 4][:, i, kt * P:(kt + 1) * P], ident)
                last.then_inc(lpT_ready, 1)

            def values(hp, u, early):
                b, j = u // 2, u % 2
                pe.wait_ge(lpT_sb, 2 * SEQS * hp + u + 1)
                if j == 0 and not early:
                    pe.wait_ge(ctxT_sb, SEQS * hp + b)
                lo = (1 - j) * DC
                for kt in range(2):
                    last = nc.tensor.matmul(bank[4][:, 0:T], kvr[:, 2 * b + kt, lo:lo + P], lprobsT[u % 2][:, kt, :],
                                            start=(j == 0 and kt == 0), stop=(j == 1 and kt == 1))
                if j == 1:
                    last.then_inc(lpv_done, 1)
                else:
                    last.then_inc(lpv_half, 1)

            def pair(hp, e, first, last):
                n, p = 2 * SEQS, hp + 1
                for u in range(n):
                    scores(hp, u, e, first and u < 2)
                    if u >= 2:
                        turn_probs(hp, u - 2, first and u < 4)
                    if u >= 3:
                        values(hp, u - 3, first and u == 3)
                    if last:
                        continue
                    if u == 0:
                        fold_queries(p, False)
                    if u == 1:
                        keys(p)
                    if u == 2:
                        fold_output(p, False)
                    for v in QUERY_UNITS[u]:
                        queries(p, v)
                    if u == 6:
                        reduced(p, 0)
                turn_probs(hp, n - 2, False)
                values(hp, n - 3, False)
                if not last:
                    reduced(p, 1)
                turn_probs(hp, n - 1, False)
                values(hp, n - 2, False)
                values(hp, n - 1, False)

            fold_queries(0, True)
            fold_output(0, True)
            keys(0)
            pe.wait_ge(hTc_split, 1)
            for v in range(2 * FCH):
                queries(0, v)
                if v == 4:
                    reduced(0, 0)
            reduced(0, 1)
            pair(0, 0, True, False)
            pair(1, 1, False, False)
            with pe.Fori(1, HP // 2 - 1) as i:
                for e in range(2):
                    pair(2 * i + e, e, False, False)
            pair(HP - 2, 0, False, False)
            pair(HP - 1, 1, False, True)
            pe.wait_ge(ctxT_sb, SEQS * HP)
            pe.wait_ge(mout_sb, HP)
            pe.wait_ge(lexp_done, 2 * SEQS * HP)
            for i in range(TILES):
                if i >= 4:
                    pe.wait_ge(x3_done, i - 3)
                for hp in range(HP):
                    last = nc.tensor.matmul(bank[i % 4][:, 0:D], ctxT[:, hp * TOK + i * P:hp * TOK + (i + 1) * P],
                                            mout[:, hp * D:(hp + 1) * D], start=(hp == 0), stop=(hp == HP - 1))
                last.then_inc(x3_ready, 1)

        @block.tensor
        def _(pe):
            attention_a_pe(pe)
            mlp_pe(pe)
            latent_pe(pe)
            experts_pe(pe)

        def attention_a_dve(dve):
            link = OwnSteps(dve, dve_setup, 18)
            nc.vector.memset(ones[:], 1.0).then_inc(consts_made, 1)
            dve.wait_ge(x_in, 16)
            for i in range(TILES):
                last = nc.vector.bn_stats(stats[:, i, :], x_sb[:, i, :])
            link(last)
            for i in range(TILES):
                last = nc.vector.bn_aggr(mv[:, i, :], stats[:, i, :])
            link(last)
            v = mv[:, :, 1]
            link(nc.vector.tensor_scalar(var_eps[:], v, EPS, None, ALU.add))
            link(nc.vector.reciprocal(rstd[:], var_eps[:]))
            link(nc.vector.tensor_tensor(var_eps[:], v, rstd[:], ALU.mult))
            link(nc.vector.tensor_scalar(var_eps[:], var_eps[:], EPS, None, ALU.add))
            link(nc.vector.reciprocal(var_eps[:], var_eps[:]))
            link(nc.vector.tensor_tensor(rkr[:, 0:TILES], rstd[:], var_eps[:], ALU.mult))
            dve.wait_ge(ctx_in, 16)
            link(nc.vector.tensor_tensor(ktmp[:], ctx_sb[:], ctx_sb[:], ALU.mult))
            link(nc.vector.tensor_reduce(rk[:, 0:TILES], ktmp[:], AX.X, ALU.add))
            link(nc.vector.tensor_scalar(rk[:, 0:TILES], rk[:, 0:TILES], 1.0 / DC, EPS, ALU.mult, ALU.add))
            nc.vector.reciprocal(rkr[:, TILES:], rk[:, 0:TILES]).then_inc(a_var, 1)
            dve.wait_ge(c_in, 16)
            nc.vector.tensor_copy(ident_bf[:], ident).then_inc(consts_made, 1)
            nc.vector.memset(mask[:, P:2 * P], 0.0).then_inc(consts_made, 1)
            nc.vector.tensor_copy(mask[:].rearrange("p (a k) -> p a k", a=3)[:, 0:3:2],
                                  const("causal").unsqueeze(1).broadcast_to([P, 2, P])).then_inc(consts_made, 1)
            dve.wait_ge(par_in, 16)

            def rope_tables(cos, sin, w, heads, scale):
                hw = HD // 2
                c3 = const("cos0").rearrange("p (i d) -> p i d", d=HD)
                s3 = const("sin0").rearrange("p (i d) -> p i d", d=HD)
                w3 = w.rearrange("p (h d) -> p h d", d=HD)
                for i in range(2):
                    nc.vector.scalar_tensor_tensor(out=cos[:, i], in0=c3[:, i].unsqueeze(1).broadcast_to([P, heads, HD]),
                                                   scalar=scale, in1=w3, op0=ALU.mult, op1=ALU.mult)
                    for lo, other in ((0, hw), (hw, 0)):
                        last = nc.vector.scalar_tensor_tensor(
                            out=sin[:, i, :, lo:lo + hw],
                            in0=s3[:, i, lo:lo + hw].unsqueeze(1).broadcast_to([P, heads, hw]),
                            scalar=scale, in1=w3[:, :, other:other + hw], op0=ALU.mult, op1=ALU.mult)
                link(last)

            rope_tables(ck0, sk0, param("kw"), GROUPS, 1.0)
            rope_tables(cq0, sq0, param("qw"), QH, HD ** -0.5)
            dve.wait_ge(a_root, 1)
            link(nc.vector.tensor_tensor(kn[:], ctx_sb[:], rk[:, TILES:].unsqueeze(2).broadcast_to([P, TILES, DC]), ALU.mult))
            k4 = kn[:].rearrange("p (b e) d -> p b (e d)", e=2)
            hw = HD // 2
            link(nc.vector.tensor_tensor(kr[:].rearrange("p (b e) d -> p b (e d)", e=2), k4,
                                         ck0[:].rearrange("p i g d -> p (i g d)").unsqueeze(1).broadcast_to([P, SEQS, 2 * DC]), ALU.mult))
            kh = kn[:].rearrange("p (b e) (g d) -> p b (e g) d", e=2, d=HD)
            th = ktmp[:].rearrange("p (b e) (g d) -> p b (e g) d", e=2, d=HD)
            sh = sk0[:].rearrange("p i g d -> p (i g) d")
            for lo, other in ((0, hw), (hw, 0)):
                last = nc.vector.tensor_tensor(
                    th[:, :, :, lo:lo + hw], kh[:, :, :, other:other + hw],
                    sh[:, :, lo:lo + hw].unsqueeze(1).broadcast_to([P, SEQS, 2 * GROUPS, hw]), ALU.mult)
            link(last)
            nc.vector.tensor_tensor(kr[:], kr[:], ktmp[:], ALU.add).then_inc(kr_ready, 1)
            for i in range(TILES):
                last = nc.vector.tensor_scalar(xn[:, i, :], x_sb[:, i, :], mv[:, i, 0:1], rk[:, i:i + 1],
                                               ALU.subtract, ALU.mult)
            link(last)
            own_q = OwnSteps(dve, dve_q, 1)
            soft = OwnSteps(dve, dve_soft, PAIRS + 1)

            def rotate_queries(b, first):
                own_q.round(b)
                if not first:
                    dve.wait_ge(qkT_ready, CHUNKS * b)
                q4 = xn[:, bass.ds(2 * b, 2), :].rearrange("p i (h d) -> p (i h) d", d=HD)
                flat = lambda t: t[:].rearrange("p i h d -> p (i h) d")
                nc.vector.tensor_tensor(flat(qrot), q4, flat(cq0), ALU.mult)
                for lo, other in ((0, hw), (hw, 0)):
                    last = nc.vector.tensor_tensor(flat(qtmp)[:, :, lo:lo + hw], q4[:, :, other:other + hw],
                                                   flat(sq0)[:, :, lo:lo + hw], ALU.mult)
                own_q(last)
                nc.vector.tensor_tensor(qrot[:], qrot[:], qtmp[:], ALU.add).then_inc(qrot_ready, 1)

            def maxima(b, s):
                dve.wait_ge(scores_ready, PAIRS * b + s + 1)
                nc.vector.tensor_reduce(negmax[s % 4][:, 0:2], pair_bank[s % 2][:, :, P:3 * P],
                                        AX.X, ALU.max, negate=True)
                nc.vector.tensor_reduce(negmax[s % 4][:, 2:4], pair_bank[s % 2][:, :, 0:P],
                                        AX.X, ALU.max, negate=True).then_inc(negmax_ready, 1)

            def normalise(b, s):
                dve.wait_ge(exp_done, PAIRS * b + s + 1)
                soft(nc.vector.reciprocal(pinv[s % 4][:], psums[s % 4][:]))
                for j in range(2):
                    nc.vector.tensor_scalar(probs[s % 4][:, j, P:3 * P], probs[s % 4][:, j, P:3 * P],
                                            pinv[s % 4][:, j:j + 1], None, ALU.mult)
                for j in range(2):
                    last = nc.vector.tensor_scalar(probs[s % 4][:, j, 0:P], probs[s % 4][:, j, 0:P],
                                                   pinv[s % 4][:, 2 + j:3 + j], None, ALU.mult)
                last.then_inc(probs_ready, 1)

            def evacuate_pT(b, s, early):
                dve.wait_ge(pT_ready, 2 * (PAIRS * b + s) + 1)
                if not early:
                    dve.wait_ge(pv_done, PAIRS * b + s - 1)
                nc.vector.tensor_copy(probsT[s % 2][0][:], bank[4][:, 0:3 * P]).then_inc(pT_sb_dve, 1)

            def residual(b):
                dve.wait_ge(wout_done, b + 1)
                xs = x_sb[:, bass.ds(2 * b, 2), :].rearrange("p i d -> p (i d)")
                nc.vector.scalar_tensor_tensor(out=xs, in0=bank[7][:], scalar=tg[:, 0:1], in1=xs,
                                               op0=ALU.mult, op1=ALU.add).then_inc(x1_done, 1)
                soft.n += 1
                dve.wait_ge(x1_done, b + 1)
                for i in range(2):
                    last = nc.vector.bn_stats(stats[:, bass.ds(2 * b + i, 1), :].rearrange("p o s -> p (o s)"),
                                              x_sb[:, bass.ds(2 * b + i, 1), :].rearrange("p o d -> p (o d)"))
                last.then_inc(dve_soft, 1)

            def sequence(b, last):
                soft.round(b)
                for s in range(PAIRS):
                    maxima(b, s)
                    if s >= 1:
                        normalise(b, s - 1)
                    if s >= 2:
                        evacuate_pT(b, s - 2, isinstance(b, int) and b == 0 and s - 2 < 2)
                    if s == 1 and not last:
                        rotate_queries(b + 1, False)
                normalise(b, PAIRS - 1)
                evacuate_pT(b, PAIRS - 2, False)
                evacuate_pT(b, PAIRS - 1, False)
                residual(b)

            rotate_queries(0, True)
            dve.wait_ge(w_sum_ready, 1)
            link(nc.vector.tensor_scalar(w_mean[:], bank[7][:, 0:2], 1.0 / (D * HID), TINY, ALU.mult, ALU.max))
            nc.vector.reciprocal(w_scale[:], w_mean[:]).then_inc(w_scale_ready, 1)
            link.done()
            dve.wait_ge(gains, 1)
            sequence(0, False)
            with dve.Fori(1, SEQS - 1) as b:
                sequence(b, False)
            sequence(SEQS - 1, True)

        def mlp_dve(dve):
            own = OwnSteps(dve, dve_b, 10)
            dve.wait_ge(dve_soft, SEQS * (PAIRS + 1))
            for i in range(TILES):
                last = nc.vector.bn_aggr(mv[:, i, :], stats[:, i, :])
            own(last)
            nc.vector.tensor_scalar(var_eps[:], mv[:, :, 1], EPS, None, ALU.add).then_inc(b_var, 1)
            dve.wait_ge(b_root, 1)
            own(nc.vector.reciprocal(rstd[:], rstd[:]))
            for i in range(TILES):
                last = nc.vector.tensor_scalar(xn[:, i, :], x_sb[:, i, :], mv[:, i, 0:1], rstd[:, i:i + 1],
                                               ALU.subtract, ALU.mult)
            own(last)
            own(nc.vector.tensor_reduce(amax[:], xn[:], AX.X, ALU.max, apply_absolute_value=True))
            own(nc.vector.tensor_scalar(amax[:], amax[:], TINY, None, ALU.max))
            own(nc.vector.reciprocal(ascale[:], amax[:]))
            own(nc.vector.tensor_scalar(ascale[:], ascale[:], 127.0, None, ALU.mult))
            for i in range(TILES):
                last = nc.vector.tensor_scalar(xn[:, i, :], xn[:, i, :], ascale[:, i:i + 1], ROUND, ALU.mult, ALU.add)
            own(last)
            nc.vector.tensor_scalar(aq[:], xn[:], ROUND, 127.0, ALU.subtract, ALU.min).then_inc(aq_ready, 1)
            own(nc.vector.tensor_scalar(adeq[:], amax[:], w_mean[:, 0:1], 1.0 / 127.0, ALU.mult, ALU.mult))
            own_h = OwnSteps(dve, dve_h, 4)

            def before_gelu(t, k):
                dve.wait_ge(h1_ready, t + 1)
                if not (isinstance(t, int) and t < 2):
                    dve.wait_ge(hq_ready, t - 1)
                nc.vector.scalar_tensor_tensor(
                    out=pre[k][:], in0=pair_bank[k][:].rearrange("p a n -> p (a n)"), scalar=adeq[:, bass.ds(t, 1)],
                    in1=param("b1"), op0=ALU.mult, op1=ALU.add).then_inc(pre_ready, 1)

            def row_scale(t, k):
                own_h.round(t)
                dve.wait_ge(gelu_done, t + 1)
                own_h(nc.vector.tensor_reduce(hmax[k][:], hid[k], AX.X, ALU.max, apply_absolute_value=True))
                own_h(nc.vector.tensor_scalar(hmax[k][:], hmax[k][:], TINY, None, ALU.max))
                own_h(nc.vector.reciprocal(hinv[k][:], hmax[k][:]))
                nc.vector.tensor_scalar(hscale[k][:], hinv[k][:], 127.0, None, ALU.mult).then_inc(hscale_ready, 1)
                own_h(nc.vector.tensor_scalar(hdeq[k][:], hmax[k][:], w_mean[:, 1:2], 1.0 / 127.0, ALU.mult, ALU.mult))

            def residual(t, k):
                dve.wait_ge(y_ready, t + 1)
                nc.vector.scalar_tensor_tensor(out=yb[k][:], in0=bank[6 + k][:, 0:D], scalar=hdeq[k][:, 0:1],
                                               in1=param("b2"), op0=ALU.mult, op1=ALU.add).then_inc(yb_ready, 1)
                dve.wait_ge(yb_ready, t + 1)
                xs = x_sb[:, bass.ds(t, 1), :].rearrange("p o d -> p (o d)")
                nc.vector.scalar_tensor_tensor(out=xs, in0=yb[k][:], scalar=tg[:, 2:3], in1=xs,
                                               op0=ALU.mult, op1=ALU.add).then_inc(x2_done, 1)
                dve.wait_ge(x2_done, t + 1)
                nc.vector.bn_stats(stats[:, bass.ds(t, 1), :].rearrange("p o s -> p (o s)"), xs).then_inc(b_stats, 1)

            before_gelu(0, 0)
            row_scale(0, 0)
            before_gelu(1, 1)
            row_scale(1, 1)
            residual(0, 0)
            with dve.Fori(1, SEQS) as b:
                for k in range(2):
                    t = 2 * b + k
                    before_gelu(t, k)
                    row_scale(t, k)
                    residual(t - 1, 1 - k)
            residual(TILES - 1, 1)

        def layer_norm(dve, own, var_ready, root_ready, normed):
            for i in range(TILES):
                last = nc.vector.bn_aggr(mv[:, i, :], stats[:, i, :])
            own(last)
            nc.vector.tensor_scalar(var_eps[:], mv[:, :, 1], EPS, None, ALU.add).then_inc(var_ready, 1)
            dve.wait_ge(root_ready, 1)
            own(nc.vector.reciprocal(rstd[:], rstd[:]))
            for i in range(TILES):
                last = nc.vector.tensor_scalar(xn[:, i, :], x_sb[:, i, :], mv[:, i, 0:1], rstd[:, i:i + 1],
                                               ALU.subtract, ALU.mult)
            last.then_inc(normed, 1)

        def experts_dve(dve):
            dve.wait_ge(c_stats, TILES)
            own = OwnSteps(dve, dve_d, 3)
            layer_norm(dve, own, d_var, d_root, xd_ready)
            dve.wait_ge(hTd_sb, KD * TB)
            own(nc.vector.tensor_copy(hT_hi[:], hT[:]))
            nc.vector.tensor_tensor(hT_lo[:], hT[:], hT_hi[:].bitcast(F32), ALU.subtract).then_inc(hT_split, 1)
            own.done()
            link = OwnSteps(dve, dve_r, 8)
            dve.wait_ge(logits_ready, 1)
            lg = bank[7].rearrange("p (i e) -> p i e", e=E)
            link(nc.vector.tensor_reduce(rmax[:], lg, AX.X, ALU.max))
            nc.vector.tensor_tensor(logits[:], lg, rmax[:].unsqueeze(2).broadcast_to([P, TILES, E]),
                                    ALU.subtract).then_inc(logits_sb, 1)
            dve.wait_ge(rexp_done, 1)
            for i in range(TILES):
                last = nc.vector.max(top8[:, i, :], rexp[:, i, :])
            link(last)
            for i in range(TILES):
                last = nc.vector.match_replace(chosen[:, i, :], top8[:, i, :], rexp[:, i, :], -1.0)
            link(last)
            link(nc.vector.tensor_reduce(tsum[:], top8[:], AX.X, ALU.add))
            link(nc.vector.reciprocal(tinv[:], tsum[:]))
            link(nc.vector.scalar_tensor_tensor(out=comb[:], in0=chosen[:], scalar=0.0, in1=rexp[:],
                                                op0=ALU.is_lt, op1=ALU.mult))
            link(nc.vector.tensor_tensor(comb[:], comb[:], tinv[:].unsqueeze(2).broadcast_to([P, TILES, E]), ALU.mult))
            link(nc.vector.tensor_copy(comb2[:, :, 0:E].bitcast(F32R), comb[:]))
            nc.vector.tensor_tensor(comb2[:, :, E:2 * E].bitcast(F32R), comb[:], comb2[:, :, 0:E],
                                    ALU.subtract).then_inc(comb_ready, 1)
            link.done()

            def weigh(t, k, weights, ready, count):
                dve.wait_ge(silu_done, t + 1)
                dve.wait_ge(up_ready, t + 1)
                nc.vector.tensor_tensor(act_u[:], silu[k][:], bank[5], ALU.mult).then_inc(up_used, 1)
                dve.wait_ge(up_used, t + 1)
                if not (isinstance(t, int) and t < 2):
                    dve.wait_ge(act_lo_ready, t - 1)
                dve.wait_ge(ready, count)
                nc.vector.tensor_tensor(act_w[k][:], act_u[:], weights, ALU.mult).then_inc(act_ready, 1)
                dve.wait_ge(act_ready, t + 1)
                if not (isinstance(t, int) and t < 2):
                    dve.wait_ge(down_done, t - 1)
                nc.vector.tensor_copy(act_hi[k][:], act_w[k][:]).then_inc(act_hi_ready, 1)

            for t in range(2):
                weigh(t, t, sgate[t][:], sgate_done, t + 1)
            with dve.Fori(0, EP) as i:
                for k in range(2):
                    t = 2 * i + 2 + k
                    weigh(t, k, bank[6], weight_ready, t + 1)
            for b in range(SEQS):
                dve.wait_ge(y_turned, b + 1)
                xs = x_sb[:, 2 * b:2 * b + 2, :].rearrange("p i d -> p (i d)")
                nc.vector.tensor_tensor(xs, bank[4 + b], xs, ALU.add).then_inc(x4_done, 1)

        def latent_dve(dve):
            dve.wait_ge(b_stats, TILES)
            own = OwnSteps(dve, dve_c, 3)
            layer_norm(dve, own, c_var, c_root, xn_ready)
            dve.wait_ge(hT_sb, KD * TB)
            own(nc.vector.tensor_copy(hT_hi[:], hT[:]))
            nc.vector.tensor_tensor(hT_lo[:], hT[:], hT_hi[:].bitcast(F32), ALU.subtract).then_inc(hTc_split, 1)
            own.done()
            soft = OwnSteps(dve, dve_l, 2 * SEQS)
            cos = const("cosq").rearrange("p (c t) -> p c t", c=FCH)
            sin = const("sinq").rearrange("p (c t) -> p c t", c=FCH)

            def turn(p, v, first):
                n, f = v // FCH, v % FCH
                dve.wait_ge(lq_ready, 6 * p + v + 1)
                if f == 0 and not first:
                    dve.wait_ge(qr_done, TB * (p - 1) + n + 1)
                by_seq = lambda a: a.rearrange("p (b t) -> p b t", b=2)
                src = by_seq(bank[6 + v % 2])

                def times(dst, table, rows, to):
                    shape = [rows.stop - rows.start, 2, T]
                    return nc.vector.tensor_tensor(by_seq(dst[to]), src[rows], table[rows, f].unsqueeze(1).broadcast_to(shape),
                                                   ALU.mult)

                every, low, high = slice(0, P), slice(0, P // 2), slice(P // 2, P)
                times(own_cos[n][:, f], cos, every, every)
                if f < 2:
                    last = times(partner_sin[n][:, 1 - f], sin, every, every)
                else:
                    times(partner_sin[n][:, 2], sin, low, high)
                    last = times(partner_sin[n][:, 2], sin, high, low)
                last.then_inc(lq_turned, 1)

            def maxima(hp, u):
                dve.wait_ge(ls_ready, 2 * SEQS * hp + u + 1)
                nc.vector.tensor_reduce(lneg[u % 4][:], bank[u % 2].rearrange("p (i k) -> p i k", i=2), AX.X,
                                        ALU.max, negate=True).then_inc(lneg_ready, 1)

            def normalise(hp, u):
                dve.wait_ge(lexp_done, 2 * SEQS * hp + u + 1)
                soft(nc.vector.reciprocal(linv[u % 4][:], lsum[u % 4][:]))
                for i in range(2):
                    last = nc.vector.tensor_scalar(lprobs[u % 4][:, i, :], lprobs[u % 4][:, i, :],
                                                   linv[u % 4][:, i:i + 1], None, ALU.mult)
                last.then_inc(lprobs_ready, 1)

            def evacuate(hp, u, first):
                dve.wait_ge(lpT_ready, 2 * SEQS * hp + u + 1)
                if not (first and u < 2):
                    dve.wait_ge((lpv_half, lpv_done)[u % 2], SEQS * hp + u // 2)
                nc.vector.tensor_copy(lprobsT[u % 2][:].rearrange("p k t -> p (k t)"), bank[2 + u % 2]).then_inc(lpT_sb, 1)

            def pair(hp, first, last):
                soft.round(hp)
                n = 2 * SEQS
                for u in range(n):
                    maxima(hp, u)
                    if u >= 1:
                        normalise(hp, u - 1)
                    if u >= 2:
                        evacuate(hp, u - 2, first)
                    for v in () if last else QUERY_UNITS[u]:
                        turn(hp + 1, v, False)
                normalise(hp, n - 1)
                evacuate(hp, n - 2, first)
                evacuate(hp, n - 1, first)

            for v in range(2 * FCH):
                turn(0, v, True)
            pair(0, True, False)
            with dve.Fori(1, HP - 1) as hp:
                pair(hp, False, False)
            pair(HP - 1, False, True)
            for i in range(TILES):
                dve.wait_ge(x3_ready, i + 1)
                nc.vector.scalar_tensor_tensor(out=x_sb[:, i, :], in0=bank[i % 4][:, 0:D], scalar=tg[:, 1:2],
                                               in1=x_sb[:, i, :], op0=ALU.mult, op1=ALU.add).then_inc(x3_done, 1)
                dve.wait_ge(x3_done, i + 1)
                nc.vector.bn_stats(stats[:, i, :], x_sb[:, i, :]).then_inc(c_stats, 1)

        @block.vector
        def _(dve):
            attention_a_dve(dve)
            mlp_dve(dve)
            latent_dve(dve)
            experts_dve(dve)


def laid_out(i):
    f = {k: np.ascontiguousarray(v) for k, v in i.items()}
    c = np.ascontiguousarray

    def rows(*vs):
        return c(np.broadcast_to(np.concatenate([v.reshape(-1) for v in vs])[None], (P, sum(v.size for v in vs))))

    wqr = f["L1_xattn_W_qr"]
    both = np.zeros((HP, 2, LQ, P), wqr.dtype)
    for j in range(2):
        both[:, j, :, j * LR:(j + 1) * LR] = wqr[j::2]
    wqr2 = np.stack([pair_order(w) for w in both]).transpose(0, 2, 1, 3)
    wkr = f["L1_xattn_W_kr"].reshape(HP, 2, DC, LR).transpose(0, 2, 1, 3)
    gu = f["L1_ffn_gate_up_proj"].reshape(EP, 2, 2, EI, D)
    shared = np.zeros((1, 2, 2, EI, D), gu.dtype)
    shared[0, 0, 0], shared[0, 0, 1] = f["L1_ffn_shared_gate_w"], f["L1_ffn_shared_up_w"]
    gu = np.concatenate([shared, gu], 0).transpose(0, 4, 2, 1, 3).reshape(EP + 1, KD, P, 2, P)
    gu = gu.transpose(0, 2, 1, 3, 4)
    dn = f["L1_ffn_down_proj"].reshape(EP, 2, D, EI)
    sdn = np.zeros((1, 2, D, EI), dn.dtype)
    sdn[0, 0] = f["L1_ffn_shared_down_w"]
    dn = np.concatenate([sdn, dn], 0).transpose(0, 1, 3, 2).reshape(EP + 1, P, D)
    kmaj = lambda w: c(w.T.reshape(-1, P, w.shape[0]).transpose(1, 0, 2))
    return {
        "x": f["x"].reshape(TOK, D), "ctx": f["ctx_512"].reshape(TOK, DC),
        "consts": shape_constants(),
        "params": rows(f["g_xattn"], f["g_ffn"], f["L0_xattn_q_norm_w"], f["L0_xattn_k_norm_w"],
                       f["L0_ffn_b1"], f["L0_ffn_b2"]),
        "woutT": kmaj(f["L0_xattn_w_out"]), "w1T": kmaj(f["L0_ffn_w1"]), "w2T": kmaj(f["L0_ffn_w2"]),
        "wq": c(f["L1_xattn_Wq"].reshape(HP, 2, LK, D).transpose(0, 2, 1, 3)),
        "wkcq": c(f["L1_xattn_w_kc_q"].reshape(HP, 2, LK, LQ).transpose(0, 2, 1, 3)),
        "wqr": c(wqr2), "wkr": c(wkr),
        "wkckv": c(f["L1_xattn_w_kc_kv"].reshape(HP, 2, LK, DC).transpose(0, 2, 1, 3)),
        "woT": c(f["L1_xattn_Wo"].T.reshape(HP, 2, LK, D).transpose(0, 2, 1, 3)),
        "routerT": kmaj(f["L1_ffn_router_w"]),
        "wsg": c(np.broadcast_to(f["L1_ffn_shared_expert_gate_w"].reshape(KD, P).T[:, :, None], (P, KD, P))),
        "experts": c(np.concatenate([gu.reshape(EP + 1, P, EW - D), dn], 2)),
    }


def kernel(**inputs):
    import concourse.bacc as bacc
    from concourse.bass_utils import run_bass_kernel_spmd

    nc = bacc.Bacc("TRN2", target_bir_lowering=False, num_devices=1)
    arrays = laid_out({k: np.asarray(v) for k, v in inputs.items()})
    args = [nc.dram_tensor(k, a.shape, mybir.dt.from_np(a.dtype), kind="ExternalInput").ap()
            for k, a in arrays.items()]
    out = nc.dram_tensor("y", (TOK, D), F32, kind="ExternalOutput").ap()
    flamingo_program(nc, *args, out)
    r = run_bass_kernel_spmd(nc, [arrays], core_ids=[0])
    return r.results[0]["y"].reshape(SEQS, T, D)
```

```python
from contextlib import ExitStack

import numpy as np

import concourse.bass as bass
from concourse import mybir

ALU = mybir.AluOpType
ACT = mybir.ActivationFunctionType
AX = mybir.AxisListType
F32 = mybir.dt.float32
F32R = mybir.dt.float32r
BF16 = mybir.dt.bfloat16

P = 128
SEQS, T, D = 4, 256, 256
TILES = SEQS * T // P
TOK = SEQS * T
DC = 64
KD = D // P
EPS = 1e-5
NEG = -1e30
ROUND = 12582912.0
TINY = 1e-5

QH, HD = 16, 16
GROUPS = 4
CHUNKS = QH * HD // P
HPC = QH // CHUNKS
PAIRS = QH // 2
DIAG = P + HD
PARTS = 4
ROWS = PARTS * HD
ROUNDS = 6
HID = 1024
HK = HID // P
EARLY = TILES - 2
TURNS = ((0, 4), (4, EARLY), (EARLY, TILES))
LH, LK, LQ, LR = 16, 128, 192, 64
HP = LH // 2
FCH = 2 * LQ // P
QUERY_UNITS = ((), (0,), (1,), (2,), (3,), (4,), (5,), ())
E, EI, TOPK = 64, 64, 8
EP = E // 2
EW = KD * 2 * P + D
TB = 2
BLK = TOK // TB

ACT_STEPS = 8

PARAMS = (("g", 4), ("qw", D), ("kw", DC), ("b1", HID), ("b2", D))
CONSTS = (("ident", P), ("causal", P), ("expertsel", E),
          ("cos0", 2 * HD), ("sin0", 2 * HD), ("cosk", 2 * DC), ("sink", 2 * DC),
          ("cosq", FCH * T), ("sinq", FCH * T))


def offsets(table):
    at, out = 0, {}
    for name, w in table:
        out[name] = (at, w)
        at += w
    return out, at


def shape_constants():
    f32 = np.float32
    tabs, width = offsets(CONSTS)
    c = np.zeros((P, width), f32)

    def put(name, a):
        at, w = tabs[name]
        c[:, at:at + w] = np.asarray(a, f32).reshape(P, w)

    p = np.arange(P)
    put("ident", np.eye(P))
    put("causal", np.where(p[None, :] <= p[:, None], 0.0, NEG))
    put("expertsel", (p[:, None] % E == np.arange(E)[None, :]))
    t = np.arange(T, dtype=f32)

    def angles(dim):
        inv = (f32(1.0) / f32(10000.0) ** (np.arange(0, dim, 2, dtype=f32) / f32(dim))).astype(f32)
        return (t[:, None] * inv[None, :]).astype(f32)

    def by_tile(a):
        return a.reshape(2, P, -1).transpose(1, 0, 2)

    def signed(s):
        h = s.shape[-1] // 2
        return np.concatenate([-s[:, :h], s[:, h:]], -1)

    a0 = np.concatenate([angles(HD)] * 2, -1)
    put("cos0", by_tile(np.cos(a0)))
    put("sin0", by_tile(signed(np.sin(a0))))
    ak = np.repeat(angles(DC), 2, -1)
    put("cosk", by_tile(np.cos(ak)))
    put("sink", by_tile(signed(np.sin(ak))))
    aq = np.repeat(angles(LQ), 2, -1)
    cos, sin = np.cos(aq), np.sin(aq)
    cross = np.concatenate([sin[:, LQ // 2:], -sin[:, :LQ // 2]], -1)
    for name, a in (("cosq", cos), ("sinq", cross)):
        put(name, pair_order(np.stack([a.T, a.T])).transpose(1, 0, 2))
    return c


def pair_order(a):
    half = LQ // 2
    lo, hi = (a[:, n * half:(n + 1) * half].reshape((LQ,) + a.shape[2:]) for n in range(2))
    return np.stack([lo[:P], hi[:P], np.concatenate([lo[P:], hi[P:]])])


class OwnSteps:

    def __init__(self, eng, sem, per_round):
        self.eng, self.sem, self.per_round = eng, sem, per_round
        self.base, self.n = 0, 0

    def round(self, r):
        assert self.n in (0, self.per_round), self.n
        self.base, self.n = r * self.per_round, 0

    def __call__(self, ins):
        self.n += 1
        ins.then_inc(self.sem, 1)
        self.eng.wait_ge(self.sem, self.base + self.n)

    def done(self):
        assert self.n == self.per_round, (self.n, self.per_round)


def flamingo_program(nc, x, ctx, consts, params, woutT, w1T, w2T, wq, wkcq, wqr, wkr, wkckv, woT,
                     routerT, wsg, experts, out):
    tabs, CW = offsets(CONSTS)
    pars, PW = offsets(PARAMS)
    with ExitStack() as stack:
        room = [stack]

        def sb(name, shape, dt=F32):
            return room[0].enter_context(nc.sbuf_tensor(name, shape, dt))

        def sem(name):
            return stack.enter_context(nc.semaphore(name))

        pair_bank = [stack.enter_context(nc.psum_tensor(f"pair_bank{i}", [P, 2, 512], F32)) for i in range(4)]
        bank = [pair_bank[i // 2][:, i % 2, :] for i in range(8)]

        x_sb = sb("x_sb", [P, TILES, D])
        ctx_sb = sb("ctx_sb", [P, TILES, DC])
        c_sb = sb("c_sb", [P, CW])
        par = sb("par", [P, PW])
        eps_col = sb("eps_col", [P, 1])
        tg = sb("tg", [P, 4])
        stats = sb("stats", [P, TILES, 6])
        mv = sb("mv", [P, TILES, 2])
        var_eps = sb("var_eps", [P, TILES])
        rstd = sb("rstd", [P, TILES])
        xn = sb("xn", [P, TILES, D])
        ident_bf = sb("ident_bf", [P, P], BF16)
        mask = sb("mask", [P, 2, P], BF16)

        def const(name):
            at, w = tabs[name]
            return c_sb[:, at:at + w]

        def param(name):
            at, w = pars[name]
            return par[:, at:at + w]

        ident = const("ident")

        kv_both = sb("kv_both", [P, TILES, 2, DC])
        wq_sb = sb("wq_sb", [P, 2, D])
        wkcq_sb = sb("wkcq_sb", [P, 2, LQ])
        wqrT_sb = sb("wqrT_sb", [P, FCH * P])
        wkrT_sb = sb("wkrT_sb", [P, P])
        wkckv_sb = sb("wkckv_sb", [P, 2, DC])
        woT_sb = sb("woT_sb", [P, 2, D])
        w_mean = sb("w_mean", [P, 2])
        w2_gain = sb("w2_gain", [P, 1])
        b2_gain = sb("b2_gain", [P, D])

        room[0] = ExitStack()
        kvtmp = sb("kvtmp", [P, TILES, DC])
        kn = sb("kn", [P, TILES, DC])
        kr = sb("kr", [P, TILES, DC])
        ktmp = sb("ktmp", [P, TILES, DC])
        rk = sb("rk", [P, 2 * TILES])
        rkr = sb("rkr", [P, 2 * TILES])
        ck0 = sb("ck0", [P, 2, GROUPS, HD])
        sk0 = sb("sk0", [P, 2, GROUPS, HD])
        cq0 = sb("cq0", [P, 2, QH, HD])
        sq0 = sb("sq0", [P, 2, QH, HD])
        qrot = sb("qrot", [P, 2, QH, HD])
        qtmp = sb("qtmp", [P, 2, QH, HD])
        k_now = sb("k_now", [P, 2, DC])
        k_parts = sb("k_parts", [P, 2, GROUPS, PARTS, HD])
        qT = sb("qT", [P, PAIRS, T], F32R)
        keys_a = sb("keys_a", [P, GROUPS, 2, T], F32R)
        vpad = [[sb(f"vpad{c}{kt}", [P, HPC * DIAG]) for kt in range(2)] for c in range(CHUNKS)]
        probs = [sb(f"probs{s}", [P, 2, 3 * P]) for s in range(4)]
        probsT = [[sb(f"probsT{s}{j}", [P, 3 * P]) for j in range(2)] for s in range(2)]
        negmax = [sb(f"negmax{s}", [P, 4]) for s in range(4)]
        psums = [sb(f"psums{s}", [P, 4]) for s in range(4)]
        pinv = [sb(f"pinv{s}", [P, 4]) for s in range(4)]
        oT = [sb(f"oT{c}", [P, T]) for c in range(CHUNKS)]
        wout_sb = sb("wout_sb", [P, KD, D])

        w1_raw = sb("w1_raw", [P, KD * HID])
        w2_raw = sb("w2_raw", [P, HK * D])
        w1q = sb("w1q", [P, KD, HID], BF16)
        w2q = sb("w2q", [P, HK, D], BF16)
        w_abs = sb("w_abs", [P, 2])
        ones = sb("ones", [P, P])
        round_col = sb("round_col", [P, 1])
        w_scale = sb("w_scale", [P, 2])
        amax = sb("amax", [P, TILES])
        ascale = sb("ascale", [P, TILES])
        adeq = sb("adeq", [P, TILES])
        aq = sb("aq", [P, TILES, D], BF16)
        aT = sb("aT", [P, KD, TOK], BF16)
        pre_all = sb("pre_all", [P, 2 * HID])
        pre = [pre_all[:, k * HID:(k + 1) * HID] for k in range(2)]
        q_parts = pre_all[:].rearrange("p (i h a d) -> p i h a d", i=2, h=QH, a=PARTS)
        hid_all = sb("hid_all", [P, 2 * HID])
        hid = [hid_all[:, k * HID:(k + 1) * HID] for k in range(2)]
        hrnd = hid
        hq = [sb(f"hq{k}", [P, HID], BF16) for k in range(2)]
        hqT = [sb(f"hqT{k}", [P, HK, P], BF16) for k in range(2)]
        hmax = [sb(f"hmax{k}", [P, 1]) for k in range(2)]
        hinv = [sb(f"hinv{k}", [P, 1]) for k in range(2)]
        hscale = [sb(f"hscale{k}", [P, 1]) for k in range(2)]
        hdeq = sb("hdeq", [P, TILES])

        room[0].close()
        room[0] = stack
        hT_hi = sb("hT_hi", [P, KD, TOK], F32R)
        hT_lo = sb("hT_lo", [P, KD, TOK], F32R)
        router_sb = sb("router_sb", [P, KD, E])
        wsg_sb = sb("wsg_sb", [P, KD, P])
        zeros_bf = sb("zeros_bf", [P, BLK], BF16)
        e_raw = [sb(f"e_raw{k}", [P, EW]) for k in range(2)]
        room[0] = ExitStack()
        gq = sb("gq", [P, KD, FCH, P])
        gq_hi = sb("gq_hi", [P, KD, FCH, P], F32R)
        gq_lo = sb("gq_lo", [P, KD, FCH, P], F32R)
        own_cos = [sb(f"own_cos{n}", [P, FCH, BLK]) for n in range(TB)]
        partner_sin = [sb(f"partner_sin{n}", [P, FCH, BLK]) for n in range(TB)]
        qk = sb("qk", [P, FCH, P])
        kv_both_hi = sb("kv_both_hi", [P, TILES, P], F32R)
        kv_both_lo = sb("kv_both_lo", [P, TILES, P], F32R)
        keys_hi = sb("keys_hi", [P, SEQS, 2, T], F32R)
        keys_lo = sb("keys_lo", [P, SEQS, 2, T], F32R)
        q_hi = sb("q_hi", [P, TOK], F32R)
        q_lo = sb("q_lo", [P, TOK], F32R)
        lprobs = [sb(f"lprobs{k}", [P, 2, T]) for k in range(4)]
        pT_hi = [sb(f"pT_hi{k}", [P, 2, 2, T], F32R) for k in range(2)]
        pT_lo = [sb(f"pT_lo{k}", [P, 2, 2, T], F32R) for k in range(2)]
        lneg = [sb(f"lneg{k}", [P, 2]) for k in range(4)]
        lsum = [sb(f"lsum{k}", [P, 2]) for k in range(4)]
        linv = [sb(f"linv{k}", [P, 2]) for k in range(4)]
        ctxT = sb("ctxT", [P, HP * TOK])
        mout = sb("mout", [P, HP * D])

        room[0].close()
        room[0] = stack
        hT = sb("hT", [P, KD, TOK])
        logits = sb("logits", [P, TILES, E])
        rmax = sb("rmax", [P, TILES])
        rexp = sb("rexp", [P, TILES, E])
        top8 = sb("top8", [P, TILES, TOPK])
        chosen = sb("chosen", [P, TILES, E])
        tsum = sb("tsum", [P, TILES])
        tinv = sb("tinv", [P, TILES])
        comb = sb("comb", [P, TILES, E])
        comb2 = sb("comb2", [P, TILES, 2 * E])
        combT = sb("combT", [P, TOK], F32R)
        sel = [sb(f"sel{k}", [P, P], F32R) for k in range(2)]
        e_hi = [sb(f"e_hi{k}", [P, EW], F32R) for k in range(2)]
        e_lo = [sb(f"e_lo{k}", [P, EW], F32R) for k in range(2)]
        silu = [sb(f"silu{k}", [P, BLK]) for k in range(2)]
        sgate = [sb(f"sgate{k}", [P, BLK]) for k in range(2)]
        act_u = sb("act_u", [P, BLK])
        act_w = [sb(f"act_w{k}", [P, BLK]) for k in range(2)]
        act_hi = [sb(f"act_hi{k}", [P, BLK], F32R) for k in range(2)]
        act_lo = [sb(f"act_lo{k}", [P, BLK], F32R) for k in range(2)]

        router_in = sem("router_in")
        e_in = [sem(f"e_in{k}") for k in range(2)]
        d_var, d_root, dve_d, dve_ds, xd_ready = sem("d_var"), sem("d_root"), sem("dve_d"), sem("dve_ds"), sem("xd_ready")
        hTd_ready, hTd_sb, hT_split = sem("hTd_ready"), sem("hTd_sb"), sem("hT_split")
        logits_ready, logits_sb, rexp_done, comb_ready = sem("logits_ready"), sem("logits_sb"), sem("rexp_done"), sem("comb_ready")
        combT_ready, combT_sb, dve_r, zeros_ready = sem("combT_ready"), sem("combT_sb"), sem("dve_r"), sem("zeros_ready")
        e_hi_ready, e_lo_ready, sel_ready = sem("e_hi_ready"), sem("e_lo_ready"), sem("sel_ready")
        gate_ready, up_ready, weight_ready = sem("gate_ready"), sem("up_ready"), sem("weight_ready")
        silu_done, sgate_done, up_used, act_ready = sem("silu_done"), sem("sgate_done"), sem("up_used"), sem("act_ready")
        act_hi_ready, act_lo_ready, down_done = sem("act_hi_ready"), sem("act_lo_ready"), sem("down_done")
        acc_sb, acc_sb_dve, y_turned, x4_done = sem("acc_sb"), sem("acc_sb_dve"), sem("y_turned"), sem("x4_done")
        wq_in, wkcq_in, wqr_in = sem("wq_in"), sem("wkcq_in"), sem("wqr_in")
        wkr_in, wkckv_in, woT_in = sem("wkr_in"), sem("wkckv_in"), sem("woT_in")
        kv_own, kv_ready, kv_split = sem("kv_own"), sem("kv_ready"), sem("kv_split")
        keysT_ready, keys_hi_ready, keys_lo_ready, keys_zero = (
            sem("keysT_ready"), sem("keys_hi_ready"), sem("keys_lo_ready"), sem("keys_zero"))
        c_var, c_root, dve_c, xn_ready = sem("c_var"), sem("c_root"), sem("dve_c"), sem("xn_ready")
        hT_ready, hT_hi_ready, hT_lo_ready = sem("hT_ready"), sem("hT_hi_ready"), sem("hT_lo_ready")
        gq_ready, gq_sb = sem("gq_ready"), sem("gq_sb")
        mout_ready, mout_sb = sem("mout_ready"), sem("mout_sb")
        qk_ready, qk_sb = sem("qk_ready"), sem("qk_sb")
        gq_hi_ready, gq_lo_ready = sem("gq_hi_ready"), sem("gq_lo_ready")
        lq_ready, lq_turned, roped = sem("lq_ready"), sem("lq_turned"), sem("roped")
        qr_done, q_hi_ready, q_lo_ready = sem("qr_done"), sem("q_hi_ready"), sem("q_lo_ready")
        ls_ready, lneg_ready, lexp_done, lprobs_ready = sem("ls_ready"), sem("lneg_ready"), sem("lexp_done"), sem("lprobs_ready")
        lpT_ready, pT_hi_ready, pT_lo_ready = sem("lpT_ready"), sem("pT_hi_ready"), sem("pT_lo_ready")
        lpv_done, ctxT_sb, dve_l = sem("lpv_done"), sem("ctxT_sb"), sem("dve_l")
        x3_ready, x3_done = sem("x3_ready"), sem("x3_done")
        a_stats, b_stats, c_stats = sem("a_stats"), sem("b_stats"), sem("c_stats")
        w1_in, w2_in = sem("w1_in"), sem("w2_in")
        w_abs_ready = sem("w_abs_ready")
        w_sum_ready = sem("w_sum_ready")
        w_scale_ready = sem("w_scale_ready")
        pool_w = sem("pool_w")
        wq_ready = sem("wq_ready")
        b_var, b_root = sem("b_var"), sem("b_root")
        dve_b = sem("dve_b")
        arnd_ready = sem("arnd_ready")
        aq_ready = sem("aq_ready")
        aT_ready = sem("aT_ready")
        aT_sb = sem("aT_sb")
        h1_ready, pre_ready, gelu_done, hscale_ready = sem("h1_ready"), sem("pre_ready"), sem("gelu_done"), sem("hscale_ready")
        hrnd_ready, hq_ready, hqT_ready, hqT_sb = sem("hrnd_ready"), sem("hq_ready"), sem("hqT_ready"), sem("hqT_sb")
        y_ready, x2_done = sem("y_ready"), sem("x2_done")
        dve_h = sem("dve_h")
        x_in, c_in, par_in, ctx_in = sem("x_in"), sem("c_in"), sem("par_in"), sem("ctx_in")
        wout_in = sem("wout_in")
        stored = sem("stored")
        consts_made = sem("consts_made")
        dve_setup = sem("dve_setup")
        pool_setup = sem("pool_setup")
        gains_made = sem("gains_made")
        x_biased = sem("x_biased")
        gains = sem("gains")
        a_var = sem("a_var")
        a_root = sem("a_root")
        kr_ready = sem("kr_ready")
        qrot_ready = sem("qrot_ready")
        parts_ready = sem("parts_ready")
        parts_own = sem("parts_own")
        q_high_ready = sem("q_high_ready")
        keys_a_zero = sem("keys_a_zero")
        turned = sem("turned")
        turned_sb = sem("turned_sb")
        vpad_ready = sem("vpad_ready")
        scores_ready = sem("scores_ready")
        negmax_ready = sem("negmax_ready")
        exp_done = sem("exp_done")
        probs_ready = sem("probs_ready")
        pT_ready = sem("pT_ready")
        pT_sb_dve = sem("pT_sb_dve")
        pT_sb_act = sem("pT_sb_act")
        pv_done = sem("pv_done")
        oT_ready = sem("oT_ready")
        wout_done = sem("wout_done")
        x1_done = sem("x1_done")
        dve_a = sem("dve_a")
        dve_q = sem("dve_q")
        dve_soft = sem("dve_soft")

        block = stack.enter_context(nc.Block())

        @block.sync
        def _(sp):
            sp.dma_start(x_sb[:], x.rearrange("(i p) d -> p i d", p=P)).then_inc(x_in, 16)
            sp.dma_start(ctx_sb[:], ctx.rearrange("(i p) d -> p i d", p=P)).then_inc(ctx_in, 16)
            sp.dma_start(par[:], params).then_inc(par_in, 16)
            sp.dma_start(c_sb[:], consts).then_inc(c_in, 16)
            sp.dma_start(w1_raw[:], w1T.rearrange("p k n -> p (k n)")).then_inc(w1_in, 16)
            sp.dma_start(w2_raw[:], w2T.rearrange("p k n -> p (k n)")).then_inc(w2_in, 16)
            sp.dma_start(wout_sb[:], woutT).then_inc(wout_in, 16)
            def latent_weights(hp, first):
                def load(dst, src, arrived, used, count):
                    if not first:
                        sp.wait_ge(used, hp * count)
                    a = src[bass.ds(hp, 1)].rearrange("o p w -> p (o w)")
                    sp.dma_start(dst[:].rearrange("p a b -> p (a b)") if len(dst.shape) == 3 else dst[:], a).then_inc(arrived, 16)

                load(wq_sb, wq, wq_in, gq_ready, 1)
                load(wkcq_sb, wkcq, wkcq_in, gq_ready, 1)
                load(wkckv_sb, wkckv, wkckv_in, mout_ready, 1)
                load(woT_sb, woT, woT_in, mout_ready, 1)
                load(wkrT_sb, wkr, wkr_in, qk_ready, 1)
                load(wqrT_sb, wqr, wqr_in, qk_ready, 1)

            latent_weights(0, True)
            with sp.Fori(1, HP) as hp:
                latent_weights(hp, False)
            sp.wait_ge(x2_done, TILES)
            sp.dma_start(router_sb[:], routerT).then_inc(router_in, 16)
            sp.dma_start(wsg_sb[:], wsg).then_inc(router_in, 16)
            for n in range(2):
                sp.dma_start(e_raw[n][:], experts[n]).then_inc(e_in[n], 16)
            with sp.Fori(0, EP // 2 - 1) as i:
                for k in range(2):
                    n = 2 * i + 2 + k
                    sp.wait_ge(e_lo_ready, n - 1)
                    sp.dma_start(e_raw[k][:], experts[bass.ds(n, 1)].rearrange("o p w -> p (o w)")).then_inc(e_in[k], 16)
            sp.wait_ge(e_lo_ready, EP - 1)
            sp.dma_start(e_raw[0][:], experts[EP]).then_inc(e_in[0], 16)
            for b in range(SEQS):
                sp.wait_ge(x4_done, b + 1)
                rows = out[b * T:(b + 1) * T, :].rearrange("(i p) d -> p i d", p=P)
                sp.dma_start(rows, x_sb[:, 2 * b:2 * b + 2, :]).then_inc(stored, 16)
            sp.wait_ge(stored, 16 * SEQS)
        q_flat = qrot[:].rearrange("p i h d -> p (i h) d").unsqueeze(2).broadcast_to([P, 2 * QH, 2, HD])
        q_split = q_parts.rearrange("p i h a d -> p (i h) a d").bitcast(F32R)

        def attention_a_pool(g):
            vflat = [[vpad[c][kt][:].rearrange("p (h e) -> p h e", e=DIAG) for kt in range(2)]
                     for c in range(CHUNKS)]
            for c in range(CHUNKS):
                for kt in range(2):
                    nc.gpsimd.memset(vpad[c][kt][:], 0.0).then_inc(pool_setup, 1)
            nc.gpsimd.memset(round_col[:], ROUND).then_inc(pool_setup, 1)
            g.wait_ge(pool_setup, 2 * CHUNKS + 1)
            g.wait_ge(c_in, 16)

            def zero_keys():
                for j in range(2):
                    rows = (slice(ROWS, P), slice(0, ROWS))[j]
                    nc.gpsimd.memset(keys_a[rows, :, j, :].bitcast(F32), 0.0).then_inc(keys_a_zero, 1)
                    g.wait_ge(keys_a_zero, j + 1)

            def split(b, first):
                g.wait_ge(kr_ready, 1)
                if not first:
                    g.wait_ge(turned, ROUNDS * b)
                nc.gpsimd.tensor_copy(k_now[:], kr[:, bass.ds(2 * b, 2), :]).then_inc(parts_own, 1)
                k = k_now[:].rearrange("p i (g d) -> p (i g) d", d=HD).unsqueeze(2).broadcast_to([P, 2 * GROUPS, 2, HD])
                kp = k_parts[:].rearrange("p i g a d -> p (i g) a d").bitcast(F32R)
                k_hi = kp[:, :, 0:1].bitcast(F32).broadcast_to([P, 2 * GROUPS, 2, HD])
                g.wait_ge(parts_own, 2 * b + 1)
                nc.gpsimd.tensor_tensor(kp[:, :, 0:2], k, ones[:, 0:HD].unsqueeze(1).unsqueeze(1).broadcast_to(
                    [P, 2 * GROUPS, 2, HD]), ALU.mult).then_inc(parts_own, 1)
                g.wait_ge(parts_own, 2 * b + 2)
                nc.gpsimd.tensor_tensor(kp[:, :, 2:4], k, k_hi, ALU.subtract)
                g.wait_ge(q_high_ready, b + 1)
                nc.gpsimd.tensor_tensor(q_split[:, :, 1:PARTS:2], q_flat, q_split[:, :, 0:1].bitcast(F32).broadcast_to(
                    [P, 2 * QH, 2, HD]), ALU.subtract).then_inc(parts_ready, 1)

            def pads(b, c, first):
                if first:
                    g.wait_ge(ctx_in, 16)
                else:
                    g.wait_ge(pv_done, PAIRS * (b - 1) + 4 * (c + 1))
                for kt in range(2):
                    src = ctx_sb[:, bass.ds(2 * b + kt, 1), 2 * c * HD:2 * (c + 1) * HD]
                    src = src.rearrange("p o (g d) -> p (o g) d", d=HD).unsqueeze(2).broadcast_to([P, 2, 4, HD])
                    dst = vflat[c][kt].rearrange("p (g n) e -> p g n e", g=2)[:, :, :, 0:HD]
                    last = nc.gpsimd.tensor_copy(dst, src)
                last.then_inc(vpad_ready, 1)

            def ternary_weights():
                g.wait_ge(w_scale_ready, 1)
                own = OwnSteps(g, pool_w, 4)
                for n, (w, q) in enumerate(((w1_raw, w1q), (w2_raw, w2q))):
                    own(nc.gpsimd.tensor_scalar(w[:], w[:], w_scale[:, n:n + 1], ROUND, ALU.mult, ALU.add))
                    own(nc.gpsimd.tensor_scalar(w[:], w[:], ROUND + 1, ROUND - 1, ALU.min, ALU.max))
                    nc.gpsimd.tensor_scalar(q[:].rearrange("p k n -> p (k n)"), w[:], -ROUND, 1.0,
                                            ALU.add, ALU.mult).then_inc(wq_ready, 1)

            zero_keys()
            g.wait_ge(consts_made, 1)
            split(0, True)
            for c in range(CHUNKS):
                pads(0, c, True)
            split(1, False)
            ternary_weights()
            latent_kv_pool(g)
            for c in range(CHUNKS):
                pads(1, c, False)
            with g.Fori(2, SEQS) as b:
                split(b, False)
                for c in range(CHUNKS):
                    pads(b, c, False)

        def latent_kv_pool(g):
            own = OwnSteps(g, kv_own, 4)
            half = DC // 2
            cos = const("cosk").rearrange("p (i d) -> p i d", d=DC).unsqueeze(1).broadcast_to([P, SEQS, 2, DC])
            sin = const("sink").rearrange("p (i d) -> p i d", d=DC)
            c4 = ctx_sb[:].rearrange("p (b i) d -> p b i d", i=2)
            t4 = kvtmp[:].rearrange("p (b i) d -> p b i d", i=2)
            kv4 = kv_both[:, :, 0, :].rearrange("p (b i) d -> p b i d", i=2)
            for lo, other in ((0, half), (half, 0)):
                own(nc.gpsimd.tensor_tensor(t4[:, :, :, lo:lo + half], c4[:, :, :, other:other + half],
                                            sin[:, :, lo:lo + half].unsqueeze(1).broadcast_to([P, SEQS, 2, half]), ALU.mult))
            own(nc.gpsimd.tensor_tensor(kv4, c4, cos, ALU.mult))
            own(nc.gpsimd.tensor_tensor(kv4, kv4, t4, ALU.add))
            own.done()
            nc.gpsimd.tensor_copy(kv_both[:, :, 1, :], kv_both[:, :, 0, :]).then_inc(kv_ready, 1)

        def latent_pool(g):
            def low_gq(p):
                g.wait_ge(gq_hi_ready, p + 1)
                nc.gpsimd.tensor_tensor(gq_lo[:], gq[:], gq_hi[:].bitcast(F32), ALU.subtract).then_inc(gq_lo_ready, 1)

            def rope(p, n):
                for part, after in ((slice(0, 2), 2), (slice(2, 3), 3)):
                    g.wait_ge(lq_turned, 6 * p + 3 * n + after)
                    nc.gpsimd.tensor_tensor(own_cos[n][:, part], own_cos[n][:, part], partner_sin[n][:, part],
                                            ALU.add).then_inc(roped, 1)

            g.wait_ge(x2_done, TILES)
            for n in range(4):
                keys, j = (keys_hi, keys_lo)[n // 2], n % 2
                rows = (slice(DC, P), slice(0, DC))[j]
                nc.gpsimd.memset(keys[rows, :, j, :].bitcast(F32), 0.0).then_inc(keys_zero, 1)
                g.wait_ge(keys_zero, n + 1)
            low_gq(0)
            rope(0, 0)
            rope(0, 1)
            kv = kv_both[:].rearrange("p i j d -> p i (j d)")
            nc.gpsimd.tensor_copy(kv_both_hi[:], kv).then_inc(kv_split, 1)
            g.wait_ge(kv_split, 1)
            nc.gpsimd.tensor_tensor(kv_both_lo[:], kv, kv_both_hi[:].bitcast(F32), ALU.subtract).then_inc(kv_split, 1)
            with g.Fori(1, HP) as p:
                low_gq(p)
                rope(p, 0)
                rope(p, 1)

        def experts_pool(g):
            def low_weights(n, k):
                g.wait_ge(e_hi_ready, n + 1)
                nc.gpsimd.tensor_tensor(e_lo[k][:], e_raw[k][:], e_hi[k][:].bitcast(F32), ALU.subtract).then_inc(e_lo_ready, 1)

            def low_act(t, k):
                if not (isinstance(t, int) and t < 2):
                    g.wait_ge(down_done, t - 1)
                g.wait_ge(act_hi_ready, t + 1)
                nc.gpsimd.tensor_tensor(act_lo[k][:], act_w[k][:], act_hi[k][:].bitcast(F32), ALU.subtract).then_inc(act_lo_ready, 1)

            g.wait_ge(x2_done, TILES)
            nc.gpsimd.memset(zeros_bf[:], 0.0).then_inc(zeros_ready, 1)
            low_weights(0, 0)
            low_act(0, 0)
            low_weights(1, 1)
            low_act(1, 1)
            with g.Fori(0, EP // 2 - 1) as i:
                for k in range(2):
                    n = 2 * i + 1 + k
                    low_act(2 * n, 0)
                    low_weights(n + 1, k)
                    low_act(2 * n + 1, 1)
            low_act(2 * EP - 2, 0)
            low_weights(EP, 0)
            low_act(2 * EP - 1, 1)
            low_act(2 * EP, 0)
            low_act(2 * EP + 1, 1)

        def mlp_pool(g):
            g.wait_ge(gains_made, 1)
            for part, tiles in enumerate((slice(0, EARLY), slice(EARLY, TILES))):
                g.wait_ge(arnd_ready, part + 1)
                shape = [P, tiles.stop - tiles.start, D]
                nc.gpsimd.tensor_tensor(aq[:, tiles], xn[:, tiles], round_col[:].unsqueeze(2).broadcast_to(shape),
                                        ALU.subtract).then_inc(aq_ready, 1)
                nc.gpsimd.tensor_tensor(x_sb[:, tiles], x_sb[:, tiles], b2_gain[:].unsqueeze(1).broadcast_to(shape),
                                        ALU.add).then_inc(x_biased, 1)

            def quantise(t, k):
                g.wait_ge(hrnd_ready, t + 1)
                if not (isinstance(t, int) and t < 2):
                    g.wait_ge(hqT_ready, t - 1)
                nc.gpsimd.tensor_tensor(hq[k][:], hrnd[k], round_col[:].broadcast_to([P, HID]),
                                        ALU.subtract).then_inc(hq_ready, 1)

            quantise(0, 0)
            quantise(1, 1)
            with g.Fori(1, SEQS) as b:
                for k in range(2):
                    quantise(2 * b + k, k)

        @block.gpsimd
        def _(g):
            attention_a_pool(g)
            mlp_pool(g)
            latent_pool(g)
            experts_pool(g)

        def root(act, part, var_ready, root_ready):
            tiles = (slice(0, EARLY), slice(EARLY, TILES))[part]
            act.wait_ge(var_ready, part + 1)
            nc.scalar.activation(rstd[:, tiles], var_eps[:, tiles], ACT.Sqrt).then_inc(root_ready, 1)

        def attention_a_act(act):
            def evacuate_turned(b, r, first):
                c, kind = r // 3, r % 3
                act.wait_ge(turned, ROUNDS * b + r + 1)
                if not first:
                    act.wait_ge(scores_ready, PAIRS * (b - 1) + 4 * (c + 1))
                if kind == 0:
                    for n in range(2):
                        src = bank[6][n * ROWS:(n + 1) * ROWS, 0:T]
                        for j in range(2):
                            last = nc.scalar.copy(keys_a[j * ROWS:(j + 1) * ROWS, 2 * c + n, j, :], src)
                else:
                    s = 4 * c + 2 * (kind - 1)
                    last = nc.scalar.copy(qT[:, s:s + 2, :], bank[6].rearrange("p (s t) -> p s t", s=2))
                last.then_inc(turned_sb, 1)

            def high_queries(b, first):
                act.wait_ge(qrot_ready, b + 1)
                if not first:
                    act.wait_ge(turned, ROUNDS * b)
                nc.scalar.copy(q_split[:, :, 0:PARTS:2], q_flat).then_inc(q_high_ready, 1)

            def exps(b, s, early):
                act.wait_ge(negmax_ready, PAIRS * b + s + 1)
                if not early:
                    act.wait_ge(pT_ready, 2 * (PAIRS * b + s - 3))
                for j in range(2):
                    for k, lo, hi in ((j, P, 3 * P), (2 + j, 0, P)):
                        src = pair_bank[s % 2][:, k // 2, j * (hi - lo):(j + 1) * (hi - lo)]
                        last = nc.scalar.activation(probs[s % 4][:, j, lo:hi], src, ACT.Exp,
                                                    bias=negmax[s % 4][:, k:k + 1], accum_out=psums[s % 4][:, k:k + 1])
                last.then_inc(exp_done, 1)

            def evacuate_pT(b, s, early):
                act.wait_ge(pT_ready, 2 * (PAIRS * b + s) + 2)
                if not early:
                    act.wait_ge(pv_done, PAIRS * b + s - 1)
                nc.scalar.copy(probsT[s % 2][1][:], bank[5][:, 0:3 * P]).then_inc(pT_sb_act, 1)

            def evacuate_oT(b, c, first):
                act.wait_ge(pv_done, PAIRS * b + 4 * (c + 1))
                if not first:
                    act.wait_ge(wout_done, b)
                nc.scalar.copy(oT[c][:], bank[6 + c][:, 0:T]).then_inc(oT_ready, 1)

            def sequence(b, first, last):
                for s in range(PAIRS):
                    if s == 7:
                        evacuate_oT(b, 0, first)
                    if s < 3:
                        evacuate_turned(b, 3 + s, first)
                    if s > 0:
                        exps(b, s, first and s < 4)
                    if s >= 2:
                        evacuate_pT(b, s - 2, first and s - 2 < 2)
                    if s == 2 and not last:
                        high_queries(b + 1, False)
                    if s == 7 and not last:
                        evacuate_turned(b + 1, 0, False)
                    if s == 4 and last:
                        root(act, 0, b_var, b_root)
                evacuate_pT(b, PAIRS - 2, False)
                if not last:
                    evacuate_turned(b + 1, 1, False)
                evacuate_pT(b, PAIRS - 1, False)
                if not last:
                    evacuate_turned(b + 1, 2, False)
                    exps(b + 1, 0, False)
                evacuate_oT(b, 1, first)

            act.wait_ge(par_in, 16)
            nc.scalar.activation(tg[:], param("g"), ACT.Tanh).then_inc(gains, 1)
            act.wait_ge(a_var, 1)
            nc.scalar.activation(rk[:], rkr[:], ACT.Sqrt).then_inc(a_root, 1)
            for n, (w, arrived) in enumerate(((w1_raw, w1_in), (w2_raw, w2_in))):
                act.wait_ge(arrived, 16)
                if n:
                    act.wait_ge(w_abs_ready, n)
                nc.scalar.activation(hid_all[:], w[:], ACT.Abs, accum_out=w_abs[:, n:n + 1]).then_inc(w_abs_ready, 1)
            act.wait_ge(keys_a_zero, 2)
            high_queries(0, True)
            for r in range(3):
                evacuate_turned(0, r, True)
            exps(0, 0, True)
            sequence(0, True, False)
            with act.Fori(1, SEQS - 1) as b:
                sequence(b, False, False)
            sequence(SEQS - 1, False, True)

        def mlp_act(act):
            def evacuate_aT(n):
                lo, hi = TURNS[n]
                act.wait_ge(aT_ready, n + 1)
                src = bank[(4, 5, 5)[n]].bitcast(BF16)[:, 0:KD * (hi - lo) * P].rearrange("p (k t) -> p k t", k=KD)
                nc.scalar.copy(aT[:, :, lo * P:hi * P], src).then_inc(aT_sb, 1)

            def gelu(t, k):
                act.wait_ge(pre_ready, t + 1)
                if not (isinstance(t, int) and t < 2):
                    act.wait_ge(hq_ready, t - 1)
                nc.scalar.activation(hid[k], pre[k], ACT.Gelu).then_inc(gelu_done, 1)

            def scale_and_round(t, k):
                act.wait_ge(hscale_ready, t + 1)
                nc.scalar.activation(hrnd[k], hid[k], ACT.Copy, bias=ROUND,
                                     scale=hscale[k][:, 0:1]).then_inc(hrnd_ready, 1)

            def evacuate(t, k):
                act.wait_ge(hqT_ready, t + 1)
                if not (isinstance(t, int) and t < 2):
                    act.wait_ge(y_ready, t - 1)
                nc.scalar.copy(hqT[k][:], bank[4].bitcast(BF16).rearrange("p (c t) -> p c t", c=HK)).then_inc(hqT_sb, 1)

            def step(j, k, head, tail):
                if not tail:
                    gelu(j + 1, 1 - k)
                if not head:
                    evacuate(j - 1, 1 - k)
                scale_and_round(j, k)

            evacuate_aT(0)
            evacuate_aT(1)
            root(act, 1, b_var, b_root)
            gelu(0, 0)
            step(0, 0, True, False)
            step(1, 1, False, False)
            evacuate_aT(2)
            with act.Fori(1, SEQS - 1) as b:
                for k in range(2):
                    step(2 * b + k, k, False, False)
            step(TILES - 2, 0, False, False)
            step(TILES - 1, 1, False, True)
            evacuate(TILES - 1, 1)
            root(act, 0, c_var, c_root)
            root(act, 1, c_var, c_root)

        def experts_act(act):
            def high_weights(n, k, first):
                if not first:
                    act.wait_ge(down_done, 2 * n - 2)
                nc.scalar.copy(e_hi[k][:], e_raw[k][:]).then_inc(e_hi_ready, 1)

            def select(n, k):
                src = const("expertsel")[:, bass.ds(2 * (n - 1), 2)].unsqueeze(2).broadcast_to([P, 2, EI])
                nc.scalar.copy(sel[k][:].rearrange("p (e i) -> p e i", e=2), src).then_inc(sel_ready, 1)

            def gate(t, k):
                act.wait_ge(gate_ready, t + 1)
                if not (isinstance(t, int) and t < 2):
                    act.wait_ge(up_used, t - 1)
                nc.scalar.activation(silu[k][:], bank[(4, 7)[k]], ACT.Silu).then_inc(silu_done, 1)

            for part in range(2):
                root(act, part, d_var, d_root)
                for n in range(2 * part, 2 * part + 2):
                    act.wait_ge(hTd_ready, n + 1)
                    nc.scalar.copy(hT[:, n % 2, (n // 2) * BLK:(n // 2 + 1) * BLK], bank[4 + n]).then_inc(hTd_sb, 1)
            for n in range(2):
                act.wait_ge(e_in[n], 16)
                high_weights(n, n, True)
            select(1, 1)
            act.wait_ge(logits_sb, 1)
            nc.scalar.activation(rexp[:], logits[:], ACT.Exp).then_inc(rexp_done, 1)
            for t in range(2):
                act.wait_ge(weight_ready, t + 1)
                nc.scalar.activation(sgate[t][:], bank[6], ACT.Sigmoid).then_inc(sgate_done, 1)
            for t in range(2):
                gate(t, t)
            for n in range(TB):
                act.wait_ge(combT_ready, n + 1)
                nc.scalar.copy(combT[:, n * BLK:(n + 1) * BLK], bank[n]).then_inc(combT_sb, 1)
            with act.Fori(0, EP // 2 - 1) as i:
                for k in range(2):
                    n = 2 * i + 1 + k
                    gate(2 * n, 0)
                    act.wait_ge(e_in[k], 16 * i + 32)
                    high_weights(n + 1, k, False)
                    select(n + 1, k)
                    gate(2 * n + 1, 1)
            gate(2 * EP - 2, 0)
            act.wait_ge(e_in[0], 16 * (EP // 2 + 1))
            high_weights(EP, 0, False)
            select(EP, 0)
            gate(2 * EP - 1, 1)
            gate(2 * EP, 0)
            gate(2 * EP + 1, 1)
            for blk in range(TB):
                act.wait_ge(down_done, 2 * EP + 1 + blk)
                nc.scalar.activation(hT[:, 0, blk * BLK:(blk + 1) * BLK], bank[blk], ACT.Copy,
                                     scale=tg[:, 3:4]).then_inc(acc_sb, 1)

        def latent_act(act):

            def evacuate_gq(p):
                act.wait_ge(gq_ready, p + 1)
                half = LQ // 2
                cut = P - half
                for dk in range(KD):
                    src = bank[6 + dk][:, 0:2 * LQ].rearrange("p (j s e) -> p j s e", j=2, s=2)
                    nc.scalar.copy(gq[:, dk, 0:2, 0:half], src[:, 0])
                    nc.scalar.copy(gq[:, dk, 0:2, half:P], src[:, 1, :, 0:cut])
                    last = nc.scalar.copy(gq[:, dk, 2, :].rearrange("p (s e) -> p s e", s=2), src[:, 1, :, cut:half])
                last.then_inc(gq_sb, 1)
                act.wait_ge(gq_sb, p + 1)
                nc.scalar.copy(gq_hi[:], gq[:]).then_inc(gq_hi_ready, 1)

            def evacuate_mout(p):
                act.wait_ge(mout_ready, p + 1)
                nc.scalar.copy(mout[:, bass.ds(p * D, D)], bank[5][:, 0:D]).then_inc(mout_sb, 1)

            def evacuate_qk(p):
                act.wait_ge(qk_ready, p + 1)
                nc.scalar.copy(qk[:], bank[5][:, 0:FCH * P].rearrange("p (c d) -> p c d", c=FCH)).then_inc(qk_sb, 1)

            def high_queries(p, n):
                act.wait_ge(qr_done, TB * p + n + 1)
                nc.scalar.copy(q_hi[:, n * BLK:(n + 1) * BLK], bank[5]).then_inc(q_hi_ready, 1)

            def high_probs(hp, u, first):
                b, i = u // 2, u % 2
                act.wait_ge(lpT_ready, 2 * SEQS * hp + u + 1)
                if not (first and b < 2):
                    act.wait_ge(lpv_done, SEQS * hp + b - 1)
                nc.scalar.copy(pT_hi[b % 2][:, :, i, :], bank[2 + u % 2].rearrange("p (k t) -> p k t", k=2)
                               ).then_inc(pT_hi_ready, 1)

            def exps(hp, u, early):
                n = 2 * SEQS * hp + u
                act.wait_ge(lneg_ready, n + 1)
                if not early:
                    act.wait_ge(lpT_ready, n - 3)
                for i in range(2):
                    last = nc.scalar.activation(lprobs[u % 4][:, i, :], bank[u % 2][:, i * T:(i + 1) * T], ACT.Exp,
                                                bias=lneg[u % 4][:, i:i + 1], accum_out=lsum[u % 4][:, i:i + 1])
                last.then_inc(lexp_done, 1)

            def evacuate_ctx(hp, b):
                act.wait_ge(lpv_done, SEQS * hp + b + 1)
                src = bank[4].rearrange("p (i j t) -> p i j t", i=2, j=2)
                for j in range(2):
                    rows = slice(j * DC, (j + 1) * DC)
                    dst = ctxT[rows, bass.ds(hp * TOK + b * T, T)].rearrange("p (i t) -> p i t", i=2)
                    last = nc.scalar.copy(dst, src[rows, :, j, :])
                last.then_inc(ctxT_sb, 1)

            def pair(hp, first, fold, last):
                for u in range(2 * SEQS):
                    if u >= 2:
                        high_probs(hp, u - 2, first)
                    exps(hp, u, first and u < 4)
                    if u == 6:
                        evacuate_ctx(hp, 0)
                    if last:
                        continue
                    if u == 1:
                        evacuate_qk(hp + 1)
                    if u == 3:
                        evacuate_mout(hp + 1)
                    if u == 6:
                        high_queries(hp + 1, 0)
                evacuate_ctx(hp, 1)
                high_probs(hp, 6, first)
                if fold:
                    evacuate_gq(hp + 2)
                high_probs(hp, 7, first)
                evacuate_ctx(hp, 2)
                if not last:
                    high_queries(hp + 1, 1)
                evacuate_ctx(hp, 3)

            def high_activations(n):
                act.wait_ge(hT_ready, n + 1)
                nc.scalar.copy(hT_hi[:, n % 2, (n // 2) * BLK:(n // 2 + 1) * BLK], bank[n]).then_inc(hT_hi_ready, 1)

            act.wait_ge(x2_done, TILES)
            for n in range(KD):
                high_activations(n)
            evacuate_gq(0)
            for n in range(KD, KD * TB):
                high_activations(n)
            for n in range(TB):
                act.wait_ge(keysT_ready, n + 1)
                for j in range(2):
                    rows = slice(j * DC, (j + 1) * DC)
                    last = nc.scalar.copy(keys_hi[rows, 2 * n:2 * n + 2, j, :],
                                          bank[4 + n][rows].rearrange("p (b t) -> p b t", b=2))
                last.then_inc(keys_hi_ready, 1)
            evacuate_qk(0)
            evacuate_mout(0)
            high_queries(0, 0)
            evacuate_gq(1)
            high_queries(0, 1)
            pair(0, True, True, False)
            with act.Fori(1, HP - 2) as hp:
                pair(hp, False, True, False)
            pair(HP - 2, False, False, False)
            pair(HP - 1, False, False, True)

        @block.scalar
        def _(act):
            attention_a_act(act)
            mlp_act(act)
            latent_act(act)
            experts_act(act)

        def attention_a_pe(pe):
            def transposes(b, r, first):
                c, kind = r // 3, r % 3
                if r == 0:
                    pe.wait_ge(parts_ready, b + 1)
                    if not first:
                        pe.wait_ge(oT_ready, CHUNKS * (b - 1) + 1)
                if not (first and r == 0):
                    pe.wait_ge(turned_sb, ROUNDS * b + r)
                if kind == 0:
                    for i in range(2):
                        src = k_parts[:, i, 2 * c:2 * c + 2].rearrange("p g a d -> p (g a d)")
                        last = nc.tensor.transpose(bank[6][:, i * P:(i + 1) * P], src, ident)
                else:
                    for n in range(2):
                        s = 4 * c + 2 * (kind - 1) + n
                        for i in range(2):
                            src = q_parts[:, i, 2 * s:2 * s + 2].rearrange("p h a d -> p (h a d)")
                            last = nc.tensor.transpose(bank[6][:, n * T + i * P:n * T + (i + 1) * P], src, ident)
                last.then_inc(turned, 1)

            def scores(b, s, early):
                if s % 2 == 0:
                    pe.wait_ge(turned_sb, ROUNDS * b + 3 * (s // 4) + 2 + s % 4 // 2)
                if not early:
                    pe.wait_ge(exp_done, PAIRS * b + s - 1)
                for n, keys in ((0, T), (1, P)):
                    dst = pair_bank[s % 2][:, n, 0:2 * keys].rearrange("p (j k) -> p j k", j=2)
                    q = qT[:, s, (1 - n) * P:(2 - n) * P]
                    nc.tensor.matmul(dst, q, keys_a[:, s // 2, :, 0:keys], start=True, stop=False, skip_group_check=True)
                    last = nc.tensor.matmul(dst[:, :, keys - P:keys], ident_bf[:], mask[:], start=False, stop=True,
                                            skip_group_check=True)
                last.then_inc(scores_ready, 1)

            def turn_probs(b, s, first):
                pe.wait_ge(probs_ready, PAIRS * b + s + 1)
                for j in range(2):
                    if not (first and s == 0):
                        pe.wait_ge((pT_sb_dve, pT_sb_act)[j], PAIRS * b + s)
                    dst, src = bank[4 + j], probs[s % 4][:, j]
                    nc.tensor.transpose(dst[:, 0:P], src[:, 0:P], ident)
                    nc.tensor.transpose(dst[:, P:2 * P], src[:, P:2 * P], ident)
                    nc.tensor.transpose(dst[:, 2 * P:3 * P], src[:, 2 * P:3 * P], ident).then_inc(pT_ready, 1)

            def values(b, s, first):
                c = s // 4
                if s % 4 == 0:
                    pe.wait_ge(vpad_ready, CHUNKS * b + c + 1)
                    if c == 1 and first:
                        pe.wait_ge(w_scale_ready, 1)
                    if c == 1 and not first:
                        pe.wait_ge(x1_done, b)
                    if c == 0:
                        pe.wait_ge(turned_sb, ROUNDS * (b + 1))
                pe.wait_ge(pT_sb_dve, PAIRS * b + s + 1)
                pe.wait_ge(pT_sb_act, PAIRS * b + s + 1)
                for j in range(2):
                    h = 2 * (s % 4) + j
                    cols = slice(h * P, (h + 1) * P)
                    nc.tensor.matmul(bank[6 + c][:, 0:T], vpad[c][0][:, cols], probsT[s % 2][j][:, 0:T],
                                     start=(h == 0), stop=False, skip_group_check=True)
                    last = nc.tensor.matmul(bank[6 + c][:, P:T], vpad[c][1][:, cols],
                                            probsT[s % 2][j][:, T:T + P],
                                            start=False, stop=(h == HPC - 1), skip_group_check=True)
                last.then_inc(pv_done, 1)

            def project(b):
                pe.wait_ge(oT_ready, CHUNKS * (b + 1))
                pe.wait_ge(wout_in, 16)
                for i in range(2):
                    for c in range(CHUNKS):
                        last = nc.tensor.matmul(bank[7][:, i * D:(i + 1) * D], oT[c][:, i * P:(i + 1) * P],
                                                wout_sb[:, c, :], start=(c == 0), stop=(c == CHUNKS - 1))
                last.then_inc(wout_done, 1)

            def sequence(b, first, last):
                for s in range(PAIRS):
                    if s >= 2:
                        scores(b, s, False)
                    if s < 3:
                        transposes(b, 3 + s, first)
                    if s == 0 and not first:
                        project(b - 1)
                    if s >= 2:
                        turn_probs(b, s - 2, first)
                    if s >= 3:
                        values(b, s - 3, first)
                    if s == 7 and not last:
                        transposes(b + 1, 0, False)
                turn_probs(b, PAIRS - 2, first)
                values(b, PAIRS - 3, first)
                if not last:
                    transposes(b + 1, 1, False)
                turn_probs(b, PAIRS - 1, first)
                if not last:
                    transposes(b + 1, 2, False)
                values(b, PAIRS - 2, first)
                if not last:
                    scores(b + 1, 0, False)
                values(b, PAIRS - 1, first)
                if not last:
                    scores(b + 1, 1, False)
                if last:
                    turn_activations(pe, 0)
                    turn_activations(pe, 1)
                    project(b)

            pe.wait_ge(consts_made, 3)
            pe.wait_ge(c_in, 16)
            pe.wait_ge(w_abs_ready, 2)
            nc.tensor.matmul(bank[7][:, 0:2], ones[:], w_abs[:], start=True, stop=True).then_inc(w_sum_ready, 1)
            for r in range(3):
                transposes(0, r, True)
            scores(0, 0, True)
            scores(0, 1, True)
            sequence(0, True, False)
            with pe.Fori(1, SEQS - 1) as b:
                sequence(b, False, False)
            sequence(SEQS - 1, False, True)

        def turn_activations(pe, n):
            lo, hi = TURNS[n]
            pe.wait_ge(aq_ready, n // 2 + 1)
            if n == 2:
                pe.wait_ge(aT_sb, 2)
            dst = bank[(4, 5, 5)[n]].bitcast(BF16)[:, 0:KD * (hi - lo) * P].rearrange("p (k t) -> p k t", k=KD)
            for i in range(lo, hi):
                for k in range(KD):
                    last = nc.tensor.transpose(dst[:, k, (i - lo) * P:(i - lo + 1) * P], aq[:, i, k * P:(k + 1) * P],
                                               ident_bf[:])
            last.then_inc(aT_ready, 1)

        def mlp_pe(pe):
            pe.wait_ge(aT_sb, 2)
            pe.wait_ge(wq_ready, 2)

            def first(t, k):
                if not (isinstance(t, int) and t < 2):
                    pe.wait_ge(pre_ready, t - 1)
                for half in range(2):
                    for c in range(KD):
                        last = nc.tensor.matmul(pair_bank[k][:, half, :], aT[:, c, bass.ds(t * P, P)],
                                                w1q[:, c, half * 512:(half + 1) * 512],
                                                start=(c == 0), stop=(c == KD - 1))
                last.then_inc(h1_ready, 1)

            def turn(t, k):
                pe.wait_ge(hq_ready, t + 1)
                if not (isinstance(t, int) and t == 0):
                    pe.wait_ge(hqT_sb, t)
                for c in range(HK):
                    last = nc.tensor.transpose(bank[4].bitcast(BF16)[:, c * P:(c + 1) * P],
                                               hq[k][:, c * P:(c + 1) * P], ident_bf[:])
                last.then_inc(hqT_ready, 1)

            def second(t, k):
                pe.wait_ge(hqT_sb, t + 1)
                if not (isinstance(t, int) and t < 2):
                    pe.wait_ge(x2_done, t - 1)
                for c in range(HK):
                    last = nc.tensor.matmul(bank[6 + k][:, 0:D], hqT[k][:, c, :], w2q[:, c, :],
                                            start=(c == 0), stop=(c == HK - 1))
                last.then_inc(y_ready, 1)

            first(0, 0)
            first(1, 1)
            pe.wait_ge(x1_done, SEQS)
            def step(j, k, head, tail):
                if not tail:
                    first(j + 2, k)
                if not head:
                    second(j - 1, 1 - k)
                turn(j, k)

            step(0, 0, True, False)
            step(1, 1, False, False)
            turn_activations(pe, 2)
            with pe.Fori(1, SEQS - 1) as b:
                pe.wait_ge(aT_sb, b + 1)
                for k in range(2):
                    step(2 * b + k, k, False, False)
            step(TILES - 2, 0, False, True)
            step(TILES - 1, 1, False, True)
            second(TILES - 1, 1)

        def turn_expert_activations(pe, half):
            pe.wait_ge(xd_ready, half + 1)
            for k in range(KD):
                n = 2 * half + k
                for i in range(4):
                    last = nc.tensor.transpose(bank[4 + n][:, i * P:(i + 1) * P],
                                               xn[:, 4 * half + i, k * P:(k + 1) * P], ident)
                last.then_inc(hTd_ready, 1)

        def experts_pe(pe):
            pe.wait_ge(router_in, 32)
            pe.wait_ge(x3_done, 5)
            for i in range(TILES):
                if i == 4:
                    turn_expert_activations(pe, 1)
                if i % 4 == 0:
                    pe.wait_ge(hTd_sb, KD * (i // 4 + 1))
                for k in range(KD):
                    last = nc.tensor.matmul(bank[0][:, i * E:(i + 1) * E], hT[:, k, i * P:(i + 1) * P], router_sb[:, k, :],
                                            start=(k == 0), stop=(k == KD - 1))
            last.then_inc(logits_ready, 1)

            def split_product(dst, w_cols, moving_hi, moving_lo, ek, start, stop, **kw):
                for n, (w, m) in enumerate(((e_hi, moving_hi), (e_lo, moving_hi), (e_hi, moving_lo))):
                    last = nc.tensor.matmul(dst, w[ek][:, w_cols], m, start=start and n == 0, stop=stop and n == 2, **kw)
                return last

            def gate(n, blk, ek):
                t = 2 * n + blk
                early = isinstance(t, int) and t < 2
                cols = slice(blk * BLK, (blk + 1) * BLK)
                if blk == 0:
                    pe.wait_ge(e_lo_ready, n + 1)
                if not early:
                    pe.wait_ge(silu_done, t - 1)
                gate_bank = bank[(4, 7)[blk]]
                for dk in range(KD):
                    last = split_product(gate_bank, slice(dk * 2 * P, dk * 2 * P + P), hT_hi[:, dk, cols], hT_lo[:, dk, cols],
                                         ek, dk == 0, dk == KD - 1)
                last.then_inc(gate_ready, 1)

            def up(n, blk, ek):
                t = 2 * n + blk
                early = isinstance(t, int) and t < 2
                cols = slice(blk * BLK, (blk + 1) * BLK)
                if not early:
                    pe.wait_ge(up_used, t)
                dst = bank[3] if early and blk else bank[5]
                for dk in range(KD):
                    last = split_product(dst, slice(dk * 2 * P + P, (dk + 1) * 2 * P), hT_hi[:, dk, cols], hT_lo[:, dk, cols],
                                         ek, dk == 0, dk == KD - 1)
                last.then_inc(up_ready, 1)

            def routed(n, blk, ek):
                t = 2 * n + blk
                if blk == 0:
                    pe.wait_ge(sel_ready, n)
                pe.wait_ge(act_ready, t)
                nc.tensor.matmul(bank[6], sel[ek][:], combT[:, blk * BLK:(blk + 1) * BLK], start=True,
                                 stop=True).then_inc(weight_ready, 1)

            def down(t, blk, ek, stop=False):
                pe.wait_ge(act_hi_ready, t + 1)
                pe.wait_ge(act_lo_ready, t + 1)
                for f in range(KD):
                    last = split_product(bank[2 * f + blk], slice(EW - D + f * P, EW - D + (f + 1) * P), act_hi[blk][:],
                                         act_lo[blk][:], ek, False, stop, skip_group_check=True)
                last.then_inc(down_done, 1)

            pe.wait_ge(hT_split, 1)
            for blk in range(TB):
                gate(0, blk, 0)
                if blk == 1:
                    pe.wait_ge(sgate_done, 1)
                for k in range(KD):
                    last = nc.tensor.matmul(bank[6], wsg_sb[:, k, :], hT[:, k, blk * BLK:(blk + 1) * BLK],
                                            start=(k == 0), stop=(k == KD - 1))
                last.then_inc(weight_ready, 1)
                up(0, blk, 0)
            pe.wait_ge(comb_ready, 1)
            for n in range(TB):
                for i in range(4):
                    last = nc.tensor.transpose(bank[n][:, i * P:(i + 1) * P], comb2[:, 4 * n + i, :], ident)
                last.then_inc(combT_ready, 1)
            pe.wait_ge(zeros_ready, 1)
            pe.wait_ge(combT_sb, TB)
            for n in range(KD * TB):
                if n == 3:
                    pe.wait_ge(up_used, 2)
                nc.tensor.matmul(bank[n], ident_bf[:], zeros_bf[:], start=True, stop=False, skip_group_check=True)
            down(0, 0, 0)
            with pe.Fori(0, EP // 2) as i:
                for k in range(2):
                    n, ek = 2 * i + 1 + k, 1 - k
                    for blk in range(TB):
                        gate(n, blk, ek)
                        up(n, blk, ek)
                        routed(n, blk, ek)
                        down(2 * n + blk - 1, 1 - blk, ek if blk else 1 - ek)
            def turn_sums(blk):
                pe.wait_ge(acc_sb, blk + 1)
                pe.wait_ge(acc_sb_dve, blk + 1)
                for b in (2 * blk, 2 * blk + 1):
                    for i in range(2):
                        for f in range(KD):
                            at = (2 * b + i) * P
                            last = nc.tensor.transpose(bank[(5, 6, 4, 7)[b]][:, i * D + f * P:i * D + (f + 1) * P],
                                                       hT[:, f, at:at + P], ident)
                    last.then_inc(y_turned, 1)

            turn_sums(0)
            down(2 * EP + 1, 1, 0, stop=True)
            turn_sums(1)

        def latent_pe(pe):
            def fold_queries(p, first):
                pe.wait_ge(wq_in, 16 * p + 16)
                pe.wait_ge(wkcq_in, 16 * p + 16)
                if not first:
                    pe.wait_ge(lq_turned, 6 * p)
                for dk in range(KD):
                    for j in range(2):
                        last = nc.tensor.matmul(bank[6 + dk][:, j * LQ:(j + 1) * LQ], wq_sb[:, j, dk * P:(dk + 1) * P],
                                                wkcq_sb[:, j, :], start=True, stop=True)
                last.then_inc(gq_ready, 1)

            def fold_output(p):
                pe.wait_ge(wkckv_in, 16 * p + 16)
                pe.wait_ge(woT_in, 16 * p + 16)
                pe.wait_ge(qk_sb, p + 1)
                for j in range(2):
                    last = nc.tensor.matmul(bank[5][j * DC:(j + 1) * DC, 0:D], wkckv_sb[:, j, :], woT_sb[:, j, :],
                                            start=True, stop=True)
                last.then_inc(mout_ready, 1)

            def fold_keys(p, first):
                pe.wait_ge(wqr_in, 16 * p + 16)
                pe.wait_ge(wkr_in, 16 * p + 16)
                if first:
                    pe.wait_ge(keys_lo_ready, 1)
                else:
                    pe.wait_ge(q_lo_ready, TB * p)
                for f in range(FCH):
                    last = nc.tensor.matmul(bank[5][:, f * P:(f + 1) * P], wqrT_sb[:, f * P:(f + 1) * P], wkrT_sb[:],
                                            start=True, stop=True)
                last.then_inc(qk_ready, 1)

            def queries(p, v):
                n, f = v // FCH, v % FCH
                cols = slice(n * BLK, (n + 1) * BLK)
                if v == 0:
                    pe.wait_ge(gq_lo_ready, p + 1)
                if v >= 2:
                    pe.wait_ge(lq_turned, 6 * p + v - 1)
                for dk in range(KD):
                    for m, (w, h) in enumerate(((gq_hi, hT_hi), (gq_lo, hT_hi), (gq_hi, hT_lo))):
                        last = nc.tensor.matmul(bank[6 + v % 2], w[:, dk, f, :], h[:, dk, cols],
                                                start=(dk == 0 and m == 0), stop=(dk == KD - 1 and m == 2))
                last.then_inc(lq_ready, 1)

            def reduced(p, n):
                if n == 0:
                    pe.wait_ge(mout_sb, p + 1)
                else:
                    pe.wait_ge(q_lo_ready, TB * p + 1)
                pe.wait_ge(roped, 2 * (TB * p + n + 1))
                for f in range(FCH):
                    last = nc.tensor.matmul(bank[5], qk[:, f, :], own_cos[n][:, f, :],
                                            start=(f == 0), stop=(f == FCH - 1))
                last.then_inc(qr_done, 1)

            def scores(hp, u, early):
                b = u // 2
                if u % SEQS == 0:
                    pe.wait_ge(q_lo_ready, TB * hp + u // SEQS + 1)
                if not early:
                    pe.wait_ge(lexp_done, 2 * SEQS * hp + u - 1)
                cols = slice(u * P, (u + 1) * P)
                for m, (q, k) in enumerate(((q_hi, keys_hi), (q_lo, keys_hi), (q_hi, keys_lo))):
                    last = nc.tensor.matmul(bank[u % 2], q[:, cols], k[:, b].rearrange("p j t -> p (j t)"),
                                            start=(m == 0), stop=(m == 2))
                last.then_inc(ls_ready, 1)

            def turn_probs(hp, u, early):
                pe.wait_ge(lprobs_ready, 2 * SEQS * hp + u + 1)
                if not early:
                    pe.wait_ge(pT_lo_ready, 2 * SEQS * hp + u - 1)
                for kt in range(2):
                    for j in range(2):
                        last = nc.tensor.transpose(bank[2 + u % 2][:, kt * T + j * P:kt * T + (j + 1) * P],
                                                   lprobs[u % 4][:, j, kt * P:(kt + 1) * P], ident)
                last.then_inc(lpT_ready, 1)

            def values(hp, b, first):
                pe.wait_ge(pT_lo_ready, 2 * SEQS * hp + 2 * b + 2)
                if first and b == 0:
                    pe.wait_ge(kv_split, 2)
                else:
                    pe.wait_ge(ctxT_sb, SEQS * hp + b)
                for kt in range(2):
                    for m, (kv, p) in enumerate(((kv_both_hi, pT_hi), (kv_both_lo, pT_hi), (kv_both_hi, pT_lo))):
                        last = nc.tensor.matmul(bank[4], kv[:, 2 * b + kt, :], p[b % 2][:, kt].rearrange("p i t -> p (i t)"),
                                                start=(kt == 0 and m == 0), stop=(kt == 1 and m == 2))
                last.then_inc(lpv_done, 1)

            def pair(hp, first, fold, last):
                p = hp + 1
                for u in range(2 * SEQS):
                    scores(hp, u, first and u < 2)
                    if u >= 2 and u not in (5,):
                        turn_probs(hp, u - 2, first and u < 4)
                    if not last:
                        for v in QUERY_UNITS[u]:
                            queries(p, v)
                    if u == 5:
                        turn_probs(hp, u - 2, False)
                    if u in (5, 7):
                        values(hp, (u - 5) // 2, first)
                    if last:
                        continue
                    if u == 1:
                        fold_keys(p, False)
                    if u == 3:
                        fold_output(p)
                    if u == 5:
                        reduced(p, 0)
                if fold:
                    fold_queries(hp + 2, False)
                turn_probs(hp, 6, False)
                values(hp, 2, False)
                turn_probs(hp, 7, False)
                if not last:
                    reduced(p, 1)
                values(hp, 3, False)

            pe.wait_ge(pre_ready, TILES)
            pe.wait_ge(hqT_sb, TILES)
            pe.wait_ge(kv_ready, 1)
            for n in range(TB):
                for i in range(4):
                    last = nc.tensor.transpose(bank[4 + n][:, i * P:(i + 1) * P],
                                               kv_both[:, 4 * n + i].rearrange("p j d -> p (j d)"), ident)
                last.then_inc(keysT_ready, 1)
            for n in range(KD * TB):
                half, k = n // 2, n % 2
                if n == KD:
                    pe.wait_ge(x2_done, TILES)
                    fold_queries(0, True)
                pe.wait_ge(xn_ready, half + 1)
                for i in range(4):
                    last = nc.tensor.transpose(bank[n][:, i * P:(i + 1) * P],
                                               xn[:, 4 * half + i, k * P:(k + 1) * P], ident)
                last.then_inc(hT_ready, 1)
            for v in range(2 * FCH):
                if v % FCH == 0:
                    pe.wait_ge(hT_lo_ready, v // FCH * KD + KD)
                queries(0, v)
                if v == 1:
                    fold_keys(0, True)
                if v == 2:
                    fold_output(0)
                if v == 4:
                    reduced(0, 0)
            fold_queries(1, False)
            reduced(0, 1)
            pe.wait_ge(keys_zero, 4)
            pair(0, True, True, False)
            with pe.Fori(1, HP - 2) as hp:
                pair(hp, False, True, False)
            pair(HP - 2, False, False, False)
            pair(HP - 1, False, False, True)
            pe.wait_ge(ctxT_sb, SEQS * HP)
            pe.wait_ge(mout_sb, HP)
            pe.wait_ge(lexp_done, 2 * SEQS * HP)
            for i in range(TILES):
                if i == TILES - 1:
                    turn_expert_activations(pe, 0)
                if i >= 4:
                    pe.wait_ge(x3_done, i - 3)
                for hp in range(HP):
                    last = nc.tensor.matmul(bank[i % 4][:, 0:D], ctxT[:, hp * TOK + i * P:hp * TOK + (i + 1) * P],
                                            mout[:, hp * D:(hp + 1) * D], start=(hp == 0), stop=(hp == HP - 1))
                last.then_inc(x3_ready, 1)

        @block.tensor
        def _(pe):
            attention_a_pe(pe)
            mlp_pe(pe)
            latent_pe(pe)
            experts_pe(pe)

        def attention_a_dve(dve):
            link = OwnSteps(dve, dve_setup, 19)
            nc.vector.memset(ones[:], 1.0).then_inc(consts_made, 1)
            dve.wait_ge(x_in, 16)
            for i in range(TILES):
                last = nc.vector.bn_stats(stats[:, i, :], x_sb[:, i, :])
            link(last)
            for i in range(TILES):
                last = nc.vector.bn_aggr(mv[:, i, :], stats[:, i, :])
            link(last)
            v = mv[:, :, 1]
            link(nc.vector.tensor_scalar(var_eps[:], v, EPS, None, ALU.add))
            link(nc.vector.reciprocal(rstd[:], var_eps[:]))
            link(nc.vector.tensor_tensor(var_eps[:], v, rstd[:], ALU.mult))
            link(nc.vector.tensor_scalar(var_eps[:], var_eps[:], EPS, None, ALU.add))
            link(nc.vector.reciprocal(var_eps[:], var_eps[:]))
            link(nc.vector.tensor_tensor(rkr[:, 0:TILES], rstd[:], var_eps[:], ALU.mult))
            dve.wait_ge(ctx_in, 16)
            link(nc.vector.tensor_tensor(ktmp[:], ctx_sb[:], ctx_sb[:], ALU.mult))
            link(nc.vector.tensor_reduce(rk[:, 0:TILES], ktmp[:], AX.X, ALU.add))
            link(nc.vector.tensor_scalar(rk[:, 0:TILES], rk[:, 0:TILES], 1.0 / DC, EPS, ALU.mult, ALU.add))
            nc.vector.reciprocal(rkr[:, TILES:], rk[:, 0:TILES]).then_inc(a_var, 1)
            dve.wait_ge(c_in, 16)
            nc.vector.tensor_copy(ident_bf[:], ident).then_inc(consts_made, 1)
            nc.vector.tensor_copy(mask[:], const("causal").unsqueeze(1).broadcast_to([P, 2, P])).then_inc(consts_made, 1)
            dve.wait_ge(par_in, 16)

            def rope_tables(cos, sin, w, heads, scale):
                hw = HD // 2
                c3 = const("cos0").rearrange("p (i d) -> p i d", d=HD)
                s3 = const("sin0").rearrange("p (i d) -> p i d", d=HD)
                w3 = w.rearrange("p (h d) -> p h d", d=HD)
                for i in range(2):
                    nc.vector.scalar_tensor_tensor(out=cos[:, i], in0=c3[:, i].unsqueeze(1).broadcast_to([P, heads, HD]),
                                                   scalar=scale, in1=w3, op0=ALU.mult, op1=ALU.mult)
                    for lo, other in ((0, hw), (hw, 0)):
                        last = nc.vector.scalar_tensor_tensor(
                            out=sin[:, i, :, lo:lo + hw],
                            in0=s3[:, i, lo:lo + hw].unsqueeze(1).broadcast_to([P, heads, hw]),
                            scalar=scale, in1=w3[:, :, other:other + hw], op0=ALU.mult, op1=ALU.mult)
                link(last)

            rope_tables(ck0, sk0, param("kw"), GROUPS, 1.0)
            rope_tables(cq0, sq0, param("qw"), QH, HD ** -0.5)
            dve.wait_ge(a_root, 1)
            link(nc.vector.tensor_tensor(kn[:], ctx_sb[:], rk[:, TILES:].unsqueeze(2).broadcast_to([P, TILES, DC]), ALU.mult))
            k4 = kn[:].rearrange("p (b e) d -> p b (e d)", e=2)
            hw = HD // 2
            link(nc.vector.tensor_tensor(kr[:].rearrange("p (b e) d -> p b (e d)", e=2), k4,
                                         ck0[:].rearrange("p i g d -> p (i g d)").unsqueeze(1).broadcast_to([P, SEQS, 2 * DC]), ALU.mult))
            kh = kn[:].rearrange("p (b e) (g d) -> p b (e g) d", e=2, d=HD)
            th = ktmp[:].rearrange("p (b e) (g d) -> p b (e g) d", e=2, d=HD)
            sh = sk0[:].rearrange("p i g d -> p (i g) d")
            for lo, other in ((0, hw), (hw, 0)):
                last = nc.vector.tensor_tensor(
                    th[:, :, :, lo:lo + hw], kh[:, :, :, other:other + hw],
                    sh[:, :, lo:lo + hw].unsqueeze(1).broadcast_to([P, SEQS, 2 * GROUPS, hw]), ALU.mult)
            link(last)
            nc.vector.tensor_tensor(kr[:], kr[:], ktmp[:], ALU.add).then_inc(kr_ready, 1)
            def scale_queries(tiles):
                for i in tiles:
                    last = nc.vector.tensor_scalar(xn[:, i, :], x_sb[:, i, :], mv[:, i, 0:1], rk[:, i:i + 1],
                                                   ALU.subtract, ALU.mult)
                link(last)

            scale_queries(range(2))
            own_q = OwnSteps(dve, dve_q, 1)
            soft = OwnSteps(dve, dve_soft, PAIRS)

            def rotate_queries(b, first):
                own_q.round(b)
                if not first:
                    dve.wait_ge(parts_ready, b)
                q4 = xn[:, bass.ds(2 * b, 2), :].rearrange("p i (h d) -> p (i h) d", d=HD)
                flat = lambda t: t[:].rearrange("p i h d -> p (i h) d")
                nc.vector.tensor_tensor(flat(qrot), q4, flat(cq0), ALU.mult)
                for lo, other in ((0, hw), (hw, 0)):
                    last = nc.vector.tensor_tensor(flat(qtmp)[:, :, lo:lo + hw], q4[:, :, other:other + hw],
                                                   flat(sq0)[:, :, lo:lo + hw], ALU.mult)
                own_q(last)
                nc.vector.tensor_tensor(qrot[:], qrot[:], qtmp[:], ALU.add).then_inc(qrot_ready, 1)

            def maxima(b, s):
                dve.wait_ge(scores_ready, PAIRS * b + s + 1)
                for n, keys in ((0, T), (1, P)):
                    last = nc.vector.tensor_reduce(
                        negmax[s % 4][:, 2 * n:2 * n + 2],
                        pair_bank[s % 2][:, n, 0:2 * keys].rearrange("p (j k) -> p j k", j=2), AX.X, ALU.max, negate=True)
                last.then_inc(negmax_ready, 1)

            def normalise(b, s):
                dve.wait_ge(exp_done, PAIRS * b + s + 1)
                soft(nc.vector.reciprocal(pinv[s % 4][:], psums[s % 4][:]))
                for j in range(2):
                    nc.vector.tensor_scalar(probs[s % 4][:, j, P:3 * P], probs[s % 4][:, j, P:3 * P],
                                            pinv[s % 4][:, j:j + 1], None, ALU.mult)
                for j in range(2):
                    last = nc.vector.tensor_scalar(probs[s % 4][:, j, 0:P], probs[s % 4][:, j, 0:P],
                                                   pinv[s % 4][:, 2 + j:3 + j], None, ALU.mult)
                last.then_inc(probs_ready, 1)

            def evacuate_pT(b, s, early):
                dve.wait_ge(pT_ready, 2 * (PAIRS * b + s) + 1)
                if not early:
                    dve.wait_ge(pv_done, PAIRS * b + s - 1)
                nc.vector.tensor_copy(probsT[s % 2][0][:], bank[4][:, 0:3 * P]).then_inc(pT_sb_dve, 1)

            def residual(b):
                dve.wait_ge(wout_done, b + 1)
                xs = x_sb[:, bass.ds(2 * b, 2), :].rearrange("p i d -> p (i d)")
                nc.vector.scalar_tensor_tensor(out=xs, in0=bank[7][:], scalar=tg[:, 0:1], in1=xs,
                                               op0=ALU.mult, op1=ALU.add).then_inc(x1_done, 1)
                dve.wait_ge(x1_done, b + 1)
                for i in range(2):
                    last = nc.vector.bn_stats(stats[:, bass.ds(2 * b + i, 1), :].rearrange("p o s -> p (o s)"),
                                              x_sb[:, bass.ds(2 * b + i, 1), :].rearrange("p o d -> p (o d)"))
                last.then_inc(a_stats, 1)

            def sequence(b, first, last):
                soft.round(b)
                for s in range(PAIRS):
                    if s >= 2:
                        maxima(b, s)
                    if s >= 1:
                        normalise(b, s - 1)
                    if s >= 2:
                        evacuate_pT(b, s - 2, isinstance(b, int) and b == 0 and s - 2 < 2)
                    if s == 1 and not last:
                        rotate_queries(b + 1, False)
                    if s == 3 and not first:
                        residual(b - 1)
                    if last:
                        if s == 4:
                            dve.wait_ge(a_stats, SEQS - 1)
                            activation_statistics(own_a, 0)
                        elif s == 5:
                            activations(own_a, 0)
                        elif s == 6:
                            activation_scales(own_a, 0)
                        elif s == 7:
                            activations_rounded(own_a, 0)
                normalise(b, PAIRS - 1)
                evacuate_pT(b, PAIRS - 2, False)
                evacuate_pT(b, PAIRS - 1, False)
                if last:
                    residual(b)
                else:
                    maxima(b + 1, 0)
                    maxima(b + 1, 1)

            own_a = OwnSteps(dve, dve_b, ACT_STEPS)
            rotate_queries(0, True)
            scale_queries(range(2, TILES))
            dve.wait_ge(w_sum_ready, 1)
            link(nc.vector.tensor_scalar(w_mean[:], bank[7][:, 0:2], 1.0 / (D * HID), TINY, ALU.mult, ALU.max))
            nc.vector.reciprocal(w_scale[:], w_mean[:]).then_inc(w_scale_ready, 1)
            link.done()
            dve.wait_ge(gains, 1)
            nc.vector.tensor_scalar(b2_gain[:], param("b2"), tg[:, 2:3], None, ALU.mult)
            nc.vector.tensor_scalar(w2_gain[:], w_mean[:, 1:2], tg[:, 2:3], None, ALU.mult).then_inc(gains_made, 1)
            dve.wait_ge(gains_made, 1)
            maxima(0, 0)
            maxima(0, 1)
            sequence(0, True, False)
            with dve.Fori(1, SEQS - 1) as b:
                sequence(b, False, False)
            sequence(SEQS - 1, False, True)

        parts = (slice(0, EARLY), slice(EARLY, TILES))

        def activation_statistics(own, part):
            own.round(part)
            tiles = parts[part]
            for i in range(tiles.start, tiles.stop):
                last = nc.vector.bn_aggr(mv[:, i, :], stats[:, i, :])
            own(last)
            nc.vector.tensor_scalar(var_eps[:, tiles], mv[:, tiles, 1], EPS, None, ALU.add).then_inc(b_var, 1)

        def activations(own, part):
            tiles = parts[part]
            own.eng.wait_ge(b_root, part + 1)
            own(nc.vector.reciprocal(rstd[:, tiles], rstd[:, tiles]))
            for i in range(tiles.start, tiles.stop):
                last = nc.vector.tensor_scalar(xn[:, i, :], x_sb[:, i, :], mv[:, i, 0:1], rstd[:, i:i + 1],
                                               ALU.subtract, ALU.mult)
            own(last)

        def activation_scales(own, part):
            tiles = parts[part]
            own(nc.vector.tensor_reduce(amax[:, tiles], xn[:, tiles], AX.X, ALU.max, apply_absolute_value=True))
            own(nc.vector.tensor_scalar(amax[:, tiles], amax[:, tiles], TINY, None, ALU.max))
            own(nc.vector.reciprocal(ascale[:, tiles], amax[:, tiles]))
            own(nc.vector.tensor_scalar(ascale[:, tiles], ascale[:, tiles], 127.0, None, ALU.mult))

        def activations_rounded(own, part):
            tiles = parts[part]
            for i in range(tiles.start, tiles.stop):
                last = nc.vector.tensor_scalar(xn[:, i, :], xn[:, i, :], ascale[:, i:i + 1], ROUND, ALU.mult, ALU.add)
            last.then_inc(arnd_ready, 1)
            own(nc.vector.tensor_scalar(adeq[:, tiles], amax[:, tiles], w_mean[:, 0:1], 1.0 / 127.0, ALU.mult, ALU.mult))
            own.done()

        def mlp_dve(dve):
            own = OwnSteps(dve, dve_b, ACT_STEPS)
            dve.wait_ge(a_stats, SEQS)
            activation_statistics(own, 1)
            own_h = OwnSteps(dve, dve_h, 4)

            def before_gelu(t, k):
                dve.wait_ge(h1_ready, t + 1)
                if not (isinstance(t, int) and t < 2):
                    dve.wait_ge(gelu_done, t - 1)
                nc.vector.scalar_tensor_tensor(
                    out=pre[k], in0=pair_bank[k][:].rearrange("p a n -> p (a n)"), scalar=adeq[:, bass.ds(t, 1)],
                    in1=param("b1"), op0=ALU.mult, op1=ALU.add).then_inc(pre_ready, 1)

            def row_scale(t, k):
                own_h.round(t)
                dve.wait_ge(gelu_done, t + 1)
                own_h(nc.vector.tensor_reduce(hmax[k][:], hid[k], AX.X, ALU.max, apply_absolute_value=True))
                own_h(nc.vector.tensor_scalar(hmax[k][:], hmax[k][:], TINY, None, ALU.max))
                own_h(nc.vector.reciprocal(hinv[k][:], hmax[k][:]))
                nc.vector.tensor_scalar(hscale[k][:], hinv[k][:], 127.0, None, ALU.mult).then_inc(hscale_ready, 1)
                own_h(nc.vector.tensor_scalar(hdeq[:, bass.ds(t, 1)], hmax[k][:], w2_gain[:], 1.0 / 127.0, ALU.mult, ALU.mult))

            def residual(t, k):
                dve.wait_ge(y_ready, t + 1)
                dve.wait_ge(x_biased, 2)
                xs = x_sb[:, bass.ds(t, 1), :].rearrange("p o d -> p (o d)")
                nc.vector.scalar_tensor_tensor(out=xs, in0=bank[6 + k][:, 0:D], scalar=hdeq[:, bass.ds(t, 1)], in1=xs,
                                               op0=ALU.mult, op1=ALU.add).then_inc(x2_done, 1)
                dve.wait_ge(x2_done, t + 1)
                nc.vector.bn_stats(stats[:, bass.ds(t, 1), :].rearrange("p o s -> p (o s)"), xs).then_inc(b_stats, 1)

            before_gelu(0, 0)
            activations(own, 1)
            before_gelu(1, 1)
            activation_scales(own, 1)
            activations_rounded(own, 1)
            row_scale(0, 0)
            before_gelu(2, 0)
            row_scale(1, 1)
            with dve.Fori(1, SEQS - 1) as b:
                for k in range(2):
                    j = 2 * b + k
                    before_gelu(j + 1, 1 - k)
                    row_scale(j, k)
                    residual(j - 2, k)
            before_gelu(TILES - 1, 1)
            row_scale(TILES - 2, 0)
            residual(TILES - 4, 0)
            row_scale(TILES - 1, 1)
            own_c = OwnSteps(dve, dve_c, 2)
            residual(TILES - 3, 1)
            dve.wait_ge(b_stats, EARLY)
            variances(own_c, 0, c_var)
            residual(TILES - 2, 0)
            normalised(own_c, 0, c_root, xn_ready)
            residual(TILES - 1, 1)
            dve.wait_ge(b_stats, TILES)
            variances(own_c, 1, c_var)
            normalised(own_c, 1, c_root, xn_ready)


        def variances(own, part, var_ready):
            own.round(part)
            tiles = parts[part]
            for i in range(tiles.start, tiles.stop):
                last = nc.vector.bn_aggr(mv[:, i, :], stats[:, i, :])
            own(last)
            nc.vector.tensor_scalar(var_eps[:, tiles], mv[:, tiles, 1], EPS, None, ALU.add).then_inc(var_ready, 1)

        def normalised(own, part, root_ready, normed):
            tiles = parts[part]
            own.eng.wait_ge(root_ready, part + 1)
            own(nc.vector.reciprocal(rstd[:, tiles], rstd[:, tiles]))
            for i in range(tiles.start, tiles.stop):
                last = nc.vector.tensor_scalar(xn[:, i, :], x_sb[:, i, :], mv[:, i, 0:1], rstd[:, i:i + 1],
                                               ALU.subtract, ALU.mult)
            last.then_inc(normed, 1)
            own.done()

        def experts_dve(dve):
            own = OwnSteps(dve, dve_ds, 1)
            dve.wait_ge(hTd_sb, KD * TB)
            own(nc.vector.tensor_copy(hT_hi[:], hT[:]))
            nc.vector.tensor_tensor(hT_lo[:], hT[:], hT_hi[:].bitcast(F32), ALU.subtract).then_inc(hT_split, 1)
            own.done()
            link = OwnSteps(dve, dve_r, 8)
            dve.wait_ge(logits_ready, 1)
            lg = bank[0].rearrange("p (i e) -> p i e", e=E)
            link(nc.vector.tensor_reduce(rmax[:], lg, AX.X, ALU.max))
            nc.vector.tensor_tensor(logits[:], lg, rmax[:].unsqueeze(2).broadcast_to([P, TILES, E]),
                                    ALU.subtract).then_inc(logits_sb, 1)
            dve.wait_ge(rexp_done, 1)
            for i in range(TILES):
                last = nc.vector.max(top8[:, i, :], rexp[:, i, :])
            link(last)
            for i in range(TILES):
                last = nc.vector.match_replace(chosen[:, i, :], top8[:, i, :], rexp[:, i, :], -1.0)
            link(last)
            link(nc.vector.tensor_reduce(tsum[:], top8[:], AX.X, ALU.add))
            link(nc.vector.reciprocal(tinv[:], tsum[:]))
            link(nc.vector.scalar_tensor_tensor(out=comb[:], in0=chosen[:], scalar=0.0, in1=rexp[:],
                                                op0=ALU.is_lt, op1=ALU.mult))
            link(nc.vector.tensor_tensor(comb[:], comb[:], tinv[:].unsqueeze(2).broadcast_to([P, TILES, E]), ALU.mult))
            link(nc.vector.tensor_copy(comb2[:, :, 0:E].bitcast(F32R), comb[:]))
            nc.vector.tensor_tensor(comb2[:, :, E:2 * E].bitcast(F32R), comb[:], comb2[:, :, 0:E],
                                    ALU.subtract).then_inc(comb_ready, 1)
            link.done()

            def weigh(t, k, weights, ready, count, up_bank=bank[5]):
                dve.wait_ge(silu_done, t + 1)
                dve.wait_ge(up_ready, t + 1)
                nc.vector.tensor_tensor(act_u[:], silu[k][:], up_bank, ALU.mult).then_inc(up_used, 1)
                dve.wait_ge(up_used, t + 1)
                if not (isinstance(t, int) and t < 2):
                    dve.wait_ge(act_lo_ready, t - 1)
                dve.wait_ge(ready, count)
                nc.vector.tensor_tensor(act_w[k][:], act_u[:], weights, ALU.mult).then_inc(act_ready, 1)
                dve.wait_ge(act_ready, t + 1)
                if not (isinstance(t, int) and t < 2):
                    dve.wait_ge(down_done, t - 1)
                nc.vector.tensor_copy(act_hi[k][:], act_w[k][:]).then_inc(act_hi_ready, 1)

            for t in range(2):
                weigh(t, t, sgate[t][:], sgate_done, t + 1, bank[(5, 3)[t]])
            with dve.Fori(0, EP) as i:
                for k in range(2):
                    t = 2 * i + 2 + k
                    weigh(t, k, bank[6], weight_ready, t + 1)
            for blk in range(TB):
                dve.wait_ge(down_done, 2 * EP + 1 + blk)
                nc.vector.tensor_scalar(hT[:, 1, blk * BLK:(blk + 1) * BLK], bank[2 + blk], tg[:, 3:4], None,
                                        ALU.mult).then_inc(acc_sb_dve, 1)
                for b in (2 * blk, 2 * blk + 1):
                    dve.wait_ge(y_turned, b + 1)
                    xs = x_sb[:, 2 * b:2 * b + 2, :].rearrange("p i d -> p (i d)")
                    nc.vector.tensor_tensor(xs, bank[(5, 6, 4, 7)[b]], xs, ALU.add).then_inc(x4_done, 1)

        def latent_dve(dve):
            def low_activations(n):
                dve.wait_ge(hT_hi_ready, n + 1)
                to = (slice(0, P), n % 2, slice(n // 2 * BLK, (n // 2 + 1) * BLK))
                nc.vector.tensor_tensor(hT_lo[to], bank[n], hT_hi[to].bitcast(F32), ALU.subtract).then_inc(hT_lo_ready, 1)

            for n in range(KD):
                low_activations(n)
            for n in range(KD, KD * TB):
                low_activations(n)
            dve.wait_ge(keys_hi_ready, TB)
            for n in range(TB):
                for j in range(2):
                    rows = slice(j * DC, (j + 1) * DC)
                    to = (rows, slice(2 * n, 2 * n + 2), j)
                    last = nc.vector.tensor_tensor(keys_lo[to], bank[4 + n][rows].rearrange("p (b t) -> p b t", b=2),
                                                   keys_hi[to].bitcast(F32), ALU.subtract)
            last.then_inc(keys_lo_ready, 1)
            soft = OwnSteps(dve, dve_l, 2 * SEQS)
            cos = const("cosq").rearrange("p (c t) -> p c t", c=FCH)
            sin = const("sinq").rearrange("p (c t) -> p c t", c=FCH)

            def turn(p, v, first):
                n, f = v // FCH, v % FCH
                dve.wait_ge(lq_ready, 6 * p + v + 1)
                if f == 0 and not first:
                    dve.wait_ge(qr_done, TB * (p - 1) + n + 1)
                by_seq = lambda a: a.rearrange("p (b t) -> p b t", b=2)
                src = by_seq(bank[6 + v % 2])

                def times(dst, table, rows, to):
                    shape = [rows.stop - rows.start, 2, T]
                    return nc.vector.tensor_tensor(by_seq(dst[to]), src[rows], table[rows, f].unsqueeze(1).broadcast_to(shape),
                                                   ALU.mult)

                every, low, high = slice(0, P), slice(0, P // 2), slice(P // 2, P)
                times(own_cos[n][:, f], cos, every, every)
                if f < 2:
                    last = times(partner_sin[n][:, 1 - f], sin, every, every)
                else:
                    times(partner_sin[n][:, 2], sin, low, high)
                    last = times(partner_sin[n][:, 2], sin, high, low)
                last.then_inc(lq_turned, 1)

            def maxima(hp, u):
                dve.wait_ge(ls_ready, 2 * SEQS * hp + u + 1)
                nc.vector.tensor_reduce(lneg[u % 4][:], bank[u % 2].rearrange("p (i k) -> p i k", i=2), AX.X,
                                        ALU.max, negate=True).then_inc(lneg_ready, 1)

            def normalise(hp, u):
                dve.wait_ge(lexp_done, 2 * SEQS * hp + u + 1)
                soft(nc.vector.reciprocal(linv[u % 4][:], lsum[u % 4][:]))
                for i in range(2):
                    last = nc.vector.tensor_scalar(lprobs[u % 4][:, i, :], lprobs[u % 4][:, i, :],
                                                   linv[u % 4][:, i:i + 1], None, ALU.mult)
                last.then_inc(lprobs_ready, 1)

            def low_probs(hp, u):
                b, i = u // 2, u % 2
                dve.wait_ge(pT_hi_ready, 2 * SEQS * hp + u + 1)
                nc.vector.tensor_tensor(pT_lo[b % 2][:, :, i, :], bank[2 + u % 2].rearrange("p (k t) -> p k t", k=2),
                                        pT_hi[b % 2][:, :, i, :].bitcast(F32), ALU.subtract).then_inc(pT_lo_ready, 1)

            def low_queries(p, n):
                dve.wait_ge(q_hi_ready, TB * p + n + 1)
                cols = slice(n * BLK, (n + 1) * BLK)
                nc.vector.tensor_tensor(q_lo[:, cols], bank[5], q_hi[:, cols].bitcast(F32),
                                        ALU.subtract).then_inc(q_lo_ready, 1)

            def pair(hp, last):
                soft.round(hp)
                n = 2 * SEQS
                for u in range(n):
                    maxima(hp, u)
                    if u >= 1:
                        normalise(hp, u - 1)
                    if not last:
                        for v in QUERY_UNITS[u]:
                            turn(hp + 1, v, False)
                    if u >= 2:
                        low_probs(hp, u - 2)
                    if u == 7 and not last:
                        low_queries(hp + 1, 0)
                normalise(hp, 7)
                low_probs(hp, 6)
                low_probs(hp, 7)
                if not last:
                    low_queries(hp + 1, 1)

            for v in range(2 * FCH):
                if v == 5:
                    low_queries(0, 0)
                turn(0, v, True)
            low_queries(0, 1)
            pair(0, False)
            with dve.Fori(1, HP - 1) as hp:
                pair(hp, False)
            pair(HP - 1, True)
            own_d = OwnSteps(dve, dve_d, 2)
            for i in range(TILES):
                dve.wait_ge(x3_ready, i + 1)
                nc.vector.scalar_tensor_tensor(out=x_sb[:, i, :], in0=bank[i % 4][:, 0:D], scalar=tg[:, 1:2],
                                               in1=x_sb[:, i, :], op0=ALU.mult, op1=ALU.add).then_inc(x3_done, 1)
                dve.wait_ge(x3_done, i + 1)
                nc.vector.bn_stats(stats[:, i, :], x_sb[:, i, :]).then_inc(c_stats, 1)
                if i == EARLY - 1 or i == TILES - 1:
                    part = i // EARLY
                    dve.wait_ge(c_stats, i + 1)
                    variances(own_d, part, d_var)
                    normalised(own_d, part, d_root, xd_ready)

        @block.vector
        def _(dve):
            attention_a_dve(dve)
            mlp_dve(dve)
            latent_dve(dve)
            experts_dve(dve)


def laid_out(i):
    f = {k: np.ascontiguousarray(v) for k, v in i.items()}
    c = np.ascontiguousarray

    def rows(*vs):
        return c(np.broadcast_to(np.concatenate([v.reshape(-1) for v in vs])[None], (P, sum(v.size for v in vs))))

    wqr = f["L1_xattn_W_qr"]
    both = np.zeros((HP, 2, LQ, P), wqr.dtype)
    for j in range(2):
        both[:, j, :, j * LR:(j + 1) * LR] = wqr[j::2]
    wqrT = np.stack([pair_order(w) for w in both]).transpose(0, 3, 1, 2)
    wkrT = np.zeros((HP, 2, LR, 2, DC), wqr.dtype)
    for j in range(2):
        wkrT[:, j, :, j] = f["L1_xattn_W_kr"][j::2].transpose(0, 2, 1)
    gu = f["L1_ffn_gate_up_proj"].reshape(EP, 2, 2, EI, D)
    shared = np.zeros((1, 2, 2, EI, D), gu.dtype)
    shared[0, 0, 0], shared[0, 0, 1] = f["L1_ffn_shared_gate_w"], f["L1_ffn_shared_up_w"]
    gu = np.concatenate([shared, gu], 0).transpose(0, 4, 2, 1, 3).reshape(EP + 1, KD, P, 2, P)
    gu = gu.transpose(0, 2, 1, 3, 4)
    dn = f["L1_ffn_down_proj"].reshape(EP, 2, D, EI)
    sdn = np.zeros((1, 2, D, EI), dn.dtype)
    sdn[0, 0] = f["L1_ffn_shared_down_w"]
    dn = np.concatenate([sdn, dn], 0).transpose(0, 1, 3, 2).reshape(EP + 1, P, D)
    kmaj = lambda w: c(w.T.reshape(-1, P, w.shape[0]).transpose(1, 0, 2))
    return {
        "x": f["x"].reshape(TOK, D), "ctx": f["ctx_512"].reshape(TOK, DC),
        "consts": shape_constants(),
        "params": rows(f["g_xattn"], f["g_ffn"], f["L0_xattn_q_norm_w"], f["L0_xattn_k_norm_w"],
                       f["L0_ffn_b1"], f["L0_ffn_b2"]),
        "woutT": kmaj(f["L0_xattn_w_out"]), "w1T": kmaj(f["L0_ffn_w1"]), "w2T": kmaj(f["L0_ffn_w2"]),
        "wq": c(f["L1_xattn_Wq"].reshape(HP, 2, LK, D).transpose(0, 2, 1, 3).reshape(HP, LK, -1)),
        "wkcq": c(f["L1_xattn_w_kc_q"].reshape(HP, 2, LK, LQ).transpose(0, 2, 1, 3).reshape(HP, LK, -1)),
        "wqr": c(wqrT.reshape(HP, P, FCH * P)), "wkr": c(wkrT.reshape(HP, P, P)),
        "wkckv": c(f["L1_xattn_w_kc_kv"].reshape(HP, 2, LK, DC).transpose(0, 2, 1, 3).reshape(HP, LK, -1)),
        "woT": c(f["L1_xattn_Wo"].T.reshape(HP, 2, LK, D).transpose(0, 2, 1, 3).reshape(HP, LK, -1)),
        "routerT": kmaj(f["L1_ffn_router_w"]),
        "wsg": c(np.broadcast_to(f["L1_ffn_shared_expert_gate_w"].reshape(KD, P).T[:, :, None], (P, KD, P))),
        "experts": c(np.concatenate([gu.reshape(EP + 1, P, EW - D), dn], 2)),
    }


def kernel(**inputs):
    import concourse.bacc as bacc
    from concourse.bass_utils import run_bass_kernel_spmd

    nc = bacc.Bacc("TRN2", target_bir_lowering=False, num_devices=1)
    arrays = laid_out({k: np.asarray(v) for k, v in inputs.items()})
    args = [nc.dram_tensor(k, a.shape, mybir.dt.from_np(a.dtype), kind="ExternalInput").ap()
            for k, a in arrays.items()]
    out = nc.dram_tensor("y", (TOK, D), F32, kind="ExternalOutput").ap()
    flamingo_program(nc, *args, out)
    r = run_bass_kernel_spmd(nc, [arrays], core_ids=[0])
    return r.results[0]["y"].reshape(SEQS, T, D)
```
